# Optimizing a Trainium2 kernel written in Bass

```python
import numpy as np
import jax
import jax.numpy as jnp

def _softmax(x, axis=-1):
    return jax.nn.softmax(x, axis=axis)

def _gelu(x):
    return jax.nn.gelu(x, approximate=True)

def _silu(x):
    return jax.nn.silu(x)

def _sigmoid(x):
    return jax.nn.sigmoid(x)

def _layernorm(x, axis=-1, eps=1e-05):
    m = jnp.mean(x, axis=axis, keepdims=True)
    v = jnp.var(x, axis=axis, keepdims=True)
    return (x - m) / jnp.sqrt(v + eps)

def _scatter_add(tgt, idx, src, axis=0):
    return tgt.at[idx].add(src)

def _segment_sum(src, seg, n):
    return jax.ops.segment_sum(src, seg, n)
kernel_name = 'mk_vit_tower_d2_tok_img1024_r4_0cda95'

def setup_inputs(seed: int=0):
    np.random.seed(seed)
    _w = jnp.asarray

    def _rec_inputs():
        import jax
        import jax.numpy as jnp
        _rk = jax.random.key(seed)
        x = -0.00016672 + 0.999947 * jax.random.normal(jax.random.fold_in(_rk, 1), (64, 3, 96, 96), jnp.float32)
        return x
    x = _rec_inputs()

    def _L0_tok_setup():
        import jax, jax.numpy as jnp
        import numpy as np
        B, C, H, Wd = (64, 3, 96, 96)
        PH, PW, D = (16, 16, 256)
        PATCH_DIM = C * PH * PW
        N_TOK = H // PH * (Wd // PW)
        key = jax.random.key(seed)
        k1, k2, k3, k4, k5 = jax.random.split(key, 5)
        x = jax.random.normal(k1, (B, C, H, Wd), dtype=jnp.float32)
        W = jax.random.normal(k2, (D, PATCH_DIM), dtype=jnp.float32) * PATCH_DIM ** (-0.5)
        b = jax.random.normal(k3, (D,), dtype=jnp.float32) * 0.02
        cls_token = jax.random.normal(k4, (1, 1, D), dtype=jnp.float32)
        pos_embedding = jax.random.normal(k5, (1, N_TOK + 1, D), dtype=jnp.float32) * 0.02
        return {'x': x, 'W': W, 'b': b, 'cls_token': cls_token, 'pos_embedding': pos_embedding}
    _L0_tok_all = _L0_tok_setup()
    _L0_tok_in = {k: v for k, v in _L0_tok_all.items() if k in ('W', 'b', 'cls_token', 'pos_embedding')}
    del _L0_tok_all

    def _L0_attn_setup():
        import jax, jax.numpy as jnp
        import numpy as np
        DIM = 256
        HEADS = 16
        HEAD_DIM = 64
        key = jax.random.key(seed)
        ks = jax.random.split(key, 6)
        inner = HEADS * HEAD_DIM
        s = 0.02
        return {'x': jax.random.normal(ks[0], (2, 512, DIM), dtype=jnp.float32), 'Wq': jax.random.normal(ks[1], (DIM, inner), dtype=jnp.float32) * s, 'Wk': jax.random.normal(ks[2], (DIM, inner), dtype=jnp.float32) * s, 'Wv': jax.random.normal(ks[3], (DIM, inner), dtype=jnp.float32) * s, 'Wo': jax.random.normal(ks[4], (inner, DIM), dtype=jnp.float32) * s, 'bo': jax.random.normal(ks[5], (DIM,), dtype=jnp.float32) * s}
    _L0_attn_all = _L0_attn_setup()
    _L0_attn_in = {k: v for k, v in _L0_attn_all.items() if k in ('Wq', 'Wk', 'Wv', 'Wo', 'bo')}
    del _L0_attn_all

    def _L0_ffn_setup():
        import jax, jax.numpy as jnp
        import numpy as np
        B, T, D, F, E = (2, 256, 256, 1024, 8)
        EPS = 1e-06
        key = jax.random.key(seed)
        k = jax.random.split(key, 5)
        scale = 0.02
        return {'x': jax.random.normal(k[0], (B, T, D), dtype=jnp.float32), 'rms_w': jnp.ones((D,), dtype=jnp.float32), 'gate_w': jax.random.normal(k[1], (E, D), dtype=jnp.float32) * scale, 'W1': jax.random.normal(k[2], (E, D, F), dtype=jnp.float32) * scale, 'b1': jnp.zeros((E, F), dtype=jnp.float32), 'W2': jax.random.normal(k[3], (E, F, D), dtype=jnp.float32) * scale, 'b2': jnp.zeros((E, D), dtype=jnp.float32)}
    _L0_ffn_all = _L0_ffn_setup()
    _L0_ffn_in = {k: v for k, v in _L0_ffn_all.items() if k in ('rms_w', 'gate_w', 'W1', 'b1', 'W2', 'b2')}
    del _L0_ffn_all

    def _L1_attn_setup():
        import jax, jax.numpy as jnp
        import numpy as np
        D_MODEL = 256
        EXPAND = 2
        D_INNER = EXPAND * D_MODEL
        HEADDIM = 64
        NHEADS = D_INNER // HEADDIM
        D_STATE = 128
        D_CONV = 4
        NGROUPS = 1
        D_IN_PROJ = 2 * D_INNER + 2 * NGROUPS * D_STATE + NHEADS
        CONV_DIM = D_INNER + 2 * NGROUPS * D_STATE
        BATCH, SEQLEN = (4, 512)
        EPS = 1e-05

        def _mamba2(x, W_in, conv_w, conv_b, dt_bias, A_log, D_skip, rms_w, W_out):
            b, l, _ = x.shape
            zxbcdt = x @ W_in
            z = zxbcdt[..., :D_INNER]
            xBC = zxbcdt[..., D_INNER:D_INNER + CONV_DIM]
            dt = zxbcdt[..., D_INNER + CONV_DIM:]
            dt = jax.nn.softplus(dt + dt_bias)
            xBC_cl = jnp.transpose(xBC, (0, 2, 1))
            conv = jax.lax.conv_general_dilated(xBC_cl, conv_w[:, None, :], window_strides=(1,), padding=[(D_CONV - 1, 0)], feature_group_count=CONV_DIM, dimension_numbers=('NCL', 'OIL', 'NCL'))
            xBC = jax.nn.silu(jnp.transpose(conv, (0, 2, 1)) + conv_b)
            xs = xBC[..., :D_INNER]
            Bm = xBC[..., D_INNER:D_INNER + D_STATE]
            Cm = xBC[..., D_INNER + D_STATE:]
            A = -jnp.exp(A_log)
            xh = xs.reshape(b, l, NHEADS, HEADDIM)
            dt_t = jnp.transpose(dt, (1, 0, 2))
            x_t = jnp.transpose(xh, (1, 0, 2, 3))
            B_t = jnp.transpose(Bm, (1, 0, 2))
            C_t = jnp.transpose(Cm, (1, 0, 2))

            def step(h, inp):
                dti, xi, Bi, Ci = inp
                dA = jnp.exp(dti * A)
                h = h * dA[:, :, None, None] + dti[:, :, None, None] * xi[..., None] * Bi[:, None, None, :]
                y = jnp.einsum('bhpn,bn->bhp', h, Ci)
                return (h, y)
            h0 = jnp.zeros((b, NHEADS, HEADDIM, D_STATE), x.dtype)
            _, ys = jax.lax.scan(step, h0, (dt_t, x_t, B_t, C_t))
            y = jnp.transpose(ys, (1, 0, 2, 3)) + D_skip[None, None, :, None] * xh
            y = y.reshape(b, l, D_INNER)
            y = y * jax.nn.silu(z)
            y = y * jax.lax.rsqrt(jnp.mean(y * y, axis=-1, keepdims=True) + EPS) * rms_w
            return y @ W_out
        key = jax.random.key(seed)
        ks = jax.random.split(key, 8)
        sc = lambda k, shape, s=0.02: jax.random.normal(k, shape, jnp.float32) * s
        x = jax.random.normal(ks[0], (BATCH, SEQLEN, D_MODEL), jnp.float32)
        W_in = sc(ks[1], (D_MODEL, D_IN_PROJ))
        conv_w = sc(ks[2], (CONV_DIM, D_CONV), 0.1)
        conv_b = jnp.zeros((CONV_DIM,), jnp.float32)
        dt = jax.random.uniform(ks[3], (NHEADS,), jnp.float32, 0.001, 0.1)
        dt_bias = jnp.log(jnp.expm1(dt))
        A_log = jnp.log(jax.random.uniform(ks[4], (NHEADS,), jnp.float32, 1.0, 16.0))
        D_skip = jnp.ones((NHEADS,), jnp.float32)
        rms_w = jnp.ones((D_INNER,), jnp.float32)
        W_out = sc(ks[5], (D_INNER, D_MODEL))
        glu_w = sc(ks[6], (D_MODEL, 2 * D_MODEL))
        glu_b = jnp.zeros((2 * D_MODEL,), jnp.float32)
        ln_w = jnp.ones((D_MODEL,), jnp.float32)
        ln_b = jnp.zeros((D_MODEL,), jnp.float32)
        return dict(x=x, W_in=W_in, conv_w=conv_w, conv_b=conv_b, dt_bias=dt_bias, A_log=A_log, D_skip=D_skip, rms_w=rms_w, W_out=W_out, glu_w=glu_w, glu_b=glu_b, ln_w=ln_w, ln_b=ln_b)
    _L1_attn_all = _L1_attn_setup()
    _L1_attn_in = {k: v for k, v in _L1_attn_all.items() if k in ('W_in', 'conv_w', 'conv_b', 'dt_bias', 'A_log', 'D_skip', 'rms_w', 'W_out', 'glu_w', 'glu_b', 'ln_w', 'ln_b')}
    del _L1_attn_all

    def _L1_ffn_setup():
        import jax, jax.numpy as jnp
        import numpy as np
        B, T, D, E, H, K = (2, 512, 256, 8, 1024, 2)
        key = jax.random.key(seed)
        ks = jax.random.split(key, 8)
        s = 0.02
        return {'x': jax.random.normal(ks[0], (B, T, D), jnp.float32), 'rw1': jax.random.normal(ks[1], (D, D), jnp.float32) * s, 'rb1': jnp.zeros((D,), jnp.float32), 'rw2': jax.random.normal(ks[2], (D, E), jnp.float32) * s, 'rb2': jnp.zeros((E,), jnp.float32), 'we1': jax.random.normal(ks[3], (E, D, H), jnp.float32) * s, 'be1': jnp.zeros((E, H), jnp.float32), 'we2': jax.random.normal(ks[4], (E, H, D), jnp.float32) * s, 'be2': jnp.zeros((E, D), jnp.float32)}
    _L1_ffn_all = _L1_ffn_setup()
    _L1_ffn_in = {k: v for k, v in _L1_ffn_all.items() if k in ('rw1', 'rb1', 'rw2', 'rb2', 'we1', 'be1', 'we2', 'be2')}
    del _L1_ffn_all
    return {'x': x, 'L0_tok_W': _L0_tok_in['W'], 'L0_tok_b': _L0_tok_in['b'], 'L0_tok_cls_token': _L0_tok_in['cls_token'], 'L0_tok_pos_embedding': _L0_tok_in['pos_embedding'], 'L0_attn_Wq': _L0_attn_in['Wq'], 'L0_attn_Wk': _L0_attn_in['Wk'], 'L0_attn_Wv': _L0_attn_in['Wv'], 'L0_attn_Wo': _L0_attn_in['Wo'], 'L0_attn_bo': _L0_attn_in['bo'], 'L0_ffn_rms_w': _L0_ffn_in['rms_w'], 'L0_ffn_gate_w': _L0_ffn_in['gate_w'], 'L0_ffn_W1': _L0_ffn_in['W1'], 'L0_ffn_b1': _L0_ffn_in['b1'], 'L0_ffn_W2': _L0_ffn_in['W2'], 'L0_ffn_b2': _L0_ffn_in['b2'], 'L1_attn_W_in': _L1_attn_in['W_in'], 'L1_attn_conv_w': _L1_attn_in['conv_w'], 'L1_attn_conv_b': _L1_attn_in['conv_b'], 'L1_attn_dt_bias': _L1_attn_in['dt_bias'], 'L1_attn_A_log': _L1_attn_in['A_log'], 'L1_attn_D_skip': _L1_attn_in['D_skip'], 'L1_attn_rms_w': _L1_attn_in['rms_w'], 'L1_attn_W_out': _L1_attn_in['W_out'], 'L1_attn_glu_w': _L1_attn_in['glu_w'], 'L1_attn_glu_b': _L1_attn_in['glu_b'], 'L1_attn_ln_w': _L1_attn_in['ln_w'], 'L1_attn_ln_b': _L1_attn_in['ln_b'], 'L1_ffn_rw1': _L1_ffn_in['rw1'], 'L1_ffn_rb1': _L1_ffn_in['rb1'], 'L1_ffn_rw2': _L1_ffn_in['rw2'], 'L1_ffn_rb2': _L1_ffn_in['rb2'], 'L1_ffn_we1': _L1_ffn_in['we1'], 'L1_ffn_be1': _L1_ffn_in['be1'], 'L1_ffn_we2': _L1_ffn_in['we2'], 'L1_ffn_be2': _L1_ffn_in['be2']}

def reference(x, L0_tok_W, L0_tok_b, L0_tok_cls_token, L0_tok_pos_embedding, L0_attn_Wq, L0_attn_Wk, L0_attn_Wv, L0_attn_Wo, L0_attn_bo, L0_ffn_rms_w, L0_ffn_gate_w, L0_ffn_W1, L0_ffn_b1, L0_ffn_W2, L0_ffn_b2, L1_attn_W_in, L1_attn_conv_w, L1_attn_conv_b, L1_attn_dt_bias, L1_attn_A_log, L1_attn_D_skip, L1_attn_rms_w, L1_attn_W_out, L1_attn_glu_w, L1_attn_glu_b, L1_attn_ln_w, L1_attn_ln_b, L1_ffn_rw1, L1_ffn_rb1, L1_ffn_rw2, L1_ffn_rb2, L1_ffn_we1, L1_ffn_be1, L1_ffn_we2, L1_ffn_be2):
    import jax
    import jax.numpy as jnp

    def _L0_tok_ref(x, W, b, cls_token, pos_embedding):
        import jax, jax.numpy as jnp
        import numpy as np
        B, C, H, Wd = (64, 3, 96, 96)
        PH, PW, D = (16, 16, 256)
        PATCH_DIM = C * PH * PW
        N_TOK = H // PH * (Wd // PW)
        Bc = x.shape[0]
        nh, nw = (H // PH, Wd // PW)
        patches = x.reshape(Bc, C, nh, PH, nw, PW)
        patches = patches.transpose(0, 2, 4, 1, 3, 5).reshape(Bc, nh * nw, PATCH_DIM)
        tokens = jnp.einsum('bnp,dp->bnd', patches, W) + b
        cls = jnp.broadcast_to(cls_token, (Bc, 1, D))
        tokens = jnp.concatenate([cls, tokens], axis=1)
        return tokens + pos_embedding

    def _L0_attn_ref(x, Wq, Wk, Wv, Wo, bo):
        import jax, jax.numpy as jnp
        import numpy as np
        DIM = 256
        HEADS = 16
        HEAD_DIM = 64
        N, S, _ = x.shape
        scale = 1.0 / np.sqrt(HEAD_DIM).astype(np.float32)
        q = (x @ Wq).reshape(N, S, HEADS, HEAD_DIM).transpose(0, 2, 1, 3)
        k = (x @ Wk).reshape(N, S, HEADS, HEAD_DIM).transpose(0, 2, 1, 3)
        v = (x @ Wv).reshape(N, S, HEADS, HEAD_DIM).transpose(0, 2, 1, 3)
        logits = jnp.einsum('nhid,nhjd->nhij', q, k) * scale
        causal = 1000000000.0 * (jnp.tril(jnp.ones((S, S), dtype=logits.dtype)) - 1.0)
        logits = logits + causal[None, None, :, :]
        attn = jax.nn.softmax(logits, axis=-1)
        out = jnp.einsum('nhij,nhjd->nhid', attn, v)
        out = out.transpose(0, 2, 1, 3).reshape(N, S, HEADS * HEAD_DIM)
        return out @ Wo + bo

    def _L0_ffn_ref(x, rms_w, gate_w, W1, b1, W2, b2):
        import jax, jax.numpy as jnp
        import numpy as np
        B, T, D, F, E = (2, 256, 256, 1024, 8)
        EPS = 1e-06
        ms = jnp.mean(x * x, axis=-1, keepdims=True)
        xn = x * jax.lax.rsqrt(ms + EPS) * rms_w
        logits = jnp.einsum('btd,ed->bte', xn, gate_w)
        scores = jax.nn.softmax(logits, axis=-1)
        top1_idx = jnp.argmax(scores, axis=-1)
        top1_score = jnp.max(scores, axis=-1)
        out = jnp.zeros_like(xn)
        for e in range(E):
            h = jax.nn.silu(jnp.einsum('btd,df->btf', xn, W1[e]) + b1[e])
            ye = jnp.einsum('btf,fd->btd', h, W2[e]) + b2[e]
            out = jnp.where((top1_idx == e)[..., None], ye, out)
        return out * top1_score[..., None]

    def _L1_attn_ref(x, W_in, conv_w, conv_b, dt_bias, A_log, D_skip, rms_w, W_out, glu_w, glu_b, ln_w, ln_b):
        import jax, jax.numpy as jnp
        import numpy as np
        D_MODEL = 256
        EXPAND = 2
        D_INNER = EXPAND * D_MODEL
        HEADDIM = 64
        NHEADS = D_INNER // HEADDIM
        D_STATE = 128
        D_CONV = 4
        NGROUPS = 1
        D_IN_PROJ = 2 * D_INNER + 2 * NGROUPS * D_STATE + NHEADS
        CONV_DIM = D_INNER + 2 * NGROUPS * D_STATE
        BATCH, SEQLEN = (4, 512)
        EPS = 1e-05

        def _mamba2(x, W_in, conv_w, conv_b, dt_bias, A_log, D_skip, rms_w, W_out):
            b, l, _ = x.shape
            zxbcdt = x @ W_in
            z = zxbcdt[..., :D_INNER]
            xBC = zxbcdt[..., D_INNER:D_INNER + CONV_DIM]
            dt = zxbcdt[..., D_INNER + CONV_DIM:]
            dt = jax.nn.softplus(dt + dt_bias)
            xBC_cl = jnp.transpose(xBC, (0, 2, 1))
            conv = jax.lax.conv_general_dilated(xBC_cl, conv_w[:, None, :], window_strides=(1,), padding=[(D_CONV - 1, 0)], feature_group_count=CONV_DIM, dimension_numbers=('NCL', 'OIL', 'NCL'))
            xBC = jax.nn.silu(jnp.transpose(conv, (0, 2, 1)) + conv_b)
            xs = xBC[..., :D_INNER]
            Bm = xBC[..., D_INNER:D_INNER + D_STATE]
            Cm = xBC[..., D_INNER + D_STATE:]
            A = -jnp.exp(A_log)
            xh = xs.reshape(b, l, NHEADS, HEADDIM)
            dt_t = jnp.transpose(dt, (1, 0, 2))
            x_t = jnp.transpose(xh, (1, 0, 2, 3))
            B_t = jnp.transpose(Bm, (1, 0, 2))
            C_t = jnp.transpose(Cm, (1, 0, 2))

            def step(h, inp):
                dti, xi, Bi, Ci = inp
                dA = jnp.exp(dti * A)
                h = h * dA[:, :, None, None] + dti[:, :, None, None] * xi[..., None] * Bi[:, None, None, :]
                y = jnp.einsum('bhpn,bn->bhp', h, Ci)
                return (h, y)
            h0 = jnp.zeros((b, NHEADS, HEADDIM, D_STATE), x.dtype)
            _, ys = jax.lax.scan(step, h0, (dt_t, x_t, B_t, C_t))
            y = jnp.transpose(ys, (1, 0, 2, 3)) + D_skip[None, None, :, None] * xh
            y = y.reshape(b, l, D_INNER)
            y = y * jax.nn.silu(z)
            y = y * jax.lax.rsqrt(jnp.mean(y * y, axis=-1, keepdims=True) + EPS) * rms_w
            return y @ W_out
        y = _mamba2(x, W_in, conv_w, conv_b, dt_bias, A_log, D_skip, rms_w, W_out)
        y = y + x
        g = y @ glu_w + glu_b
        a, gate = (g[..., :D_MODEL], g[..., D_MODEL:])
        y = y + a * jax.nn.sigmoid(gate)
        mu = jnp.mean(y, axis=-1, keepdims=True)
        var = jnp.mean((y - mu) ** 2, axis=-1, keepdims=True)
        y = (y - mu) * jax.lax.rsqrt(var + EPS) * ln_w + ln_b
        return y

    def _L1_ffn_ref(x, rw1, rb1, rw2, rb2, we1, be1, we2, be2):
        import jax, jax.numpy as jnp
        import numpy as np
        B, T, D, E, H, K = (2, 512, 256, 8, 1024, 2)
        b, t, d = x.shape
        xt = x.reshape(b * t, d)
        n = xt.shape[0]
        logits = jax.nn.silu(xt @ rw1 + rb1) @ rw2 + rb2
        _, idx = jax.lax.top_k(logits, K)
        mask = jnp.zeros((n, E), bool).at[jnp.arange(n)[:, None], idx].set(True)
        w = jax.nn.softmax(jnp.where(mask, logits, -jnp.inf), axis=1)
        h = jax.nn.silu(jnp.einsum('nd,edh->enh', xt, we1) + be1[:, None, :])
        eo = jnp.einsum('enh,ehd->end', h, we2) + be2[:, None, :]
        y = xt + jnp.einsum('ne,end->nd', w, eo)
        return y.reshape(b, t, d)
    h = _L0_tok_ref(x, L0_tok_W, L0_tok_b, L0_tok_cls_token, L0_tok_pos_embedding)
    h = h + _L0_attn_ref(_layernorm(h, axis=-1), L0_attn_Wq, L0_attn_Wk, L0_attn_Wv, L0_attn_Wo, L0_attn_bo)
    h = h + _L0_ffn_ref(_layernorm(h, axis=-1), L0_ffn_rms_w, L0_ffn_gate_w, L0_ffn_W1, L0_ffn_b1, L0_ffn_W2, L0_ffn_b2)
    h = h + _L1_attn_ref(_layernorm(h, axis=-1), L1_attn_W_in, L1_attn_conv_w, L1_attn_conv_b, L1_attn_dt_bias, L1_attn_A_log, L1_attn_D_skip, L1_attn_rms_w, L1_attn_W_out, L1_attn_glu_w, L1_attn_glu_b, L1_attn_ln_w, L1_attn_ln_b)
    h = h + _L1_ffn_ref(_layernorm(h, axis=-1), L1_ffn_rw1, L1_ffn_rb1, L1_ffn_rw2, L1_ffn_rb2, L1_ffn_we1, L1_ffn_be1, L1_ffn_we2, L1_ffn_be2)
    return h

_drawn_inputs = setup_inputs


def setup_inputs(seed=0):
    import zlib

    import numpy as np

    out = dict(_drawn_inputs(seed))
    spreads = {'L0_ffn_rms_w': (1.0, 0.6),
     'L0_ffn_b1': (0.0, 0.8),
     'L0_ffn_b2': (0.0, 0.383),
     'L1_attn_conv_b': (0.0, 0.1),
     'L1_attn_D_skip': (1.0, 0.2),
     'L1_attn_rms_w': (1.0, 0.2),
     'L1_attn_glu_b': (0.0, 0.332),
     'L1_attn_ln_w': (1.0, 0.2),
     'L1_attn_ln_b': (0.0, 0.1),
     'L1_ffn_rb1': (0.0, 0.8),
     'L1_ffn_rb2': (0.0, 0.1),
     'L1_ffn_be1': (0.0, 0.8),
     'L1_ffn_be2': (0.0, 0.357)}
    factors = {'L0_tok_b': 2.689,
     'L0_tok_pos_embedding': 2.712,
     'L0_attn_Wq': 8.0,
     'L0_attn_Wk': 8.0,
     'L1_attn_dt_bias': 8.0,
     'L1_attn_A_log': 8.0,
     'L1_ffn_rw1': 7.627,
     'L1_ffn_rw2': 7.003}
    for name, (base, spread) in spreads.items():
        noise = np.random.default_rng([zlib.crc32(name.encode()), seed]).standard_normal(out[name].shape)
        drawn = base * np.exp(spread * noise) if base else spread * noise
        out[name] = jnp.asarray(drawn.astype(out[name].dtype))
    for name, factor in factors.items():
        out[name] = (out[name] * factor).astype(out[name].dtype)
    return out
```

```python
from contextlib import ExitStack

import numpy as np
import concourse.bass as bass
from concourse import mybir

ALU = mybir.AluOpType
ACT = mybir.ActivationFunctionType
AX = mybir.AxisListType
F32 = mybir.dt.float32
BF16 = mybir.dt.bfloat16

IMAGES, TOK, D = 64, 37, 256
PER = 3
TT = PER * TOK
NT = -(-IMAGES // PER)
NTOK = NT * TT
KD = D // 128
PATCH = 3 * 16 * 16
KP = PATCH // 128
HEADS, HD = 16, 64
INNER = HEADS * HD
KI = INNER // 128
E = 8
F = 1024
KF = F // 128
DI, DS, MH = 512, 128, 8
CONV = DI + 2 * DS
KC = CONV // 128
MASKED = -8.0e9


def run(eng, n, unroll, stages):
    longest = max(lag for lag, _ in stages)
    head = longest + unroll
    while head < n and (n - head) % unroll:
        head += 1

    def step(t, phase):
        for lag, fn in stages:
            if not isinstance(t, int) or 0 <= t - lag < n:
                fn(t - lag, (phase - lag) % unroll)

    for t in range(min(head, n)):
        step(t, t)
    if head < n:
        with eng.Fori(head, n - unroll + 1, unroll) as t0:
            for k in range(unroll):
                step(t0 + k, head + k)
    for t in range(n, n + longest):
        step(t, t)


def reused(eng, sem, i, depth, per=1, extra=0):
    if isinstance(i, int) and i < depth:
        return
    eng.wait_ge(sem, (i - depth + 1) * per + extra)


def through(eng, i, passed):
    if not isinstance(i, int):
        eng.sem_inc(passed, 1)


def build(nc, a, out):
    with ExitStack() as ctx:
        def sb(name, shape, dt=F32, c=ctx):
            return c.enter_context(nc.sbuf_tensor(name, shape, dt))

        def pb(name, shape, dt=F32, c=ctx):
            return c.enter_context(nc.psum_tensor(name, shape, dt))

        def sem(name, c=ctx):
            return c.enter_context(nc.semaphore(name))

        h = sb("h", [128, NT, D])
        xT = sb("xT", [128, KD, NTOK])
        ident = sb("ident", [128, 128])
        identb = sb("identb", [128, 128], BF16)
        mhalf = sb("mhalf", [128, 1])
        epsilon = sb("epsilon", [128, 2])
        loaded = sem("loaded")
        passed = sem("passed")
        g = dict(nc=nc, a=a, sb=sb, pb=pb, sem=sem, h=h, xT=xT, ident=ident, identb=identb, mhalf=mhalf, epsilon=epsilon,
                 passed=passed, loaded=loaded)
        embed(g)
        attention(g)
        with ExitStack() as c:
            weight = sb("weight0", [128, NT, E], c=c)
            route_top1(g, weight)
            experts(g, weight, "ffn0", ("W1_0", "b1_0", "W2_0", "b2_0"))
        mamba(g)
        with ExitStack() as c:
            weight = sb("weight1", [128, NT, E], c=c)
            route_top2(g, weight)
            experts(g, weight, "ffn1", ("W1_1", "b1_1", "W2_1", "b2_1"))
        store(g, out)


class LayerNorm:

    def __init__(self, g, c, name, slots=False):
        self.g = g
        self.eps = 0
        sb, pb, sem = g["sb"], g["pb"], g["sem"]
        self.stats = sb(name + "_stats", [128, 2, 6], c=c)
        self.mv = sb(name + "_mv", [128, 4, 2], c=c)
        self.rstd = sb(name + "_rstd", [128, 4, 2], c=c)
        self.xn = sb(name + "_xn", [128, 2, D], c=c)
        self.psT = pb(name + "_psT", [128, 2, 512], c=c)
        self.stats_done = sem(name + "_stats_done", c)
        self.mv_done = sem(name + "_mv_done", c)
        self.rstd_done = sem(name + "_rstd_done", c)
        self.xn_done = sem(name + "_xn_done", c)
        self.turned = sem(name + "_turned", c)
        self.kept = sem(name + "_kept", c)
        if slots:
            self.xs = sb(name + "_xs", [128, 2, KD, TT], c=c)
            self.xs_kept = sem(name + "_xs_kept", c)

    def statistics(self, dve, i, k, h_ready=None):
        nc, h = self.g["nc"], self.g["h"]
        if h_ready is not None:
            dve.wait_ge(h_ready, i + 1)
        through(dve, i, self.g["passed"])
        nc.vector.bn_stats(self.stats[0:TT, k % 2, :], h[0:TT, i, :]).then_inc(self.stats_done, 1)
        dve.wait_ge(self.stats_done, i + 1)
        reused(dve, self.xn_done, i, 2)
        through(dve, i, self.g["passed"])
        nc.vector.bn_aggr(self.mv[0:TT, k % 2, :], self.stats[0:TT, k % 2, :]).then_inc(self.mv_done, 1)

    def inverse(self, pool, i, k):
        nc = self.g["nc"]
        pool.wait_ge(self.mv_done, i + 1)
        reused(pool, self.xn_done, i, 2)
        nc.gpsimd.tensor_tensor(self.rstd[0:TT, k % 2, 0:1], self.mv[0:TT, k % 2, 1:2],
                                self.g["epsilon"][0:TT, self.eps:self.eps + 1], ALU.add).then_inc(self.rstd_done, 1)
        pool.wait_ge(self.rstd_done, i * 2 + 1)
        nc.gpsimd.tensor_tensor(self.rstd[0:TT, k % 2, 1:2], self.rstd[0:TT, k % 2, 0:1],
                                self.g["mhalf"][0:TT, :], ALU.pow).then_inc(self.rstd_done, 1)

    def normalise(self, dve, i, k, dst=None):
        nc, h = self.g["nc"], self.g["h"]
        dve.wait_ge(self.rstd_done, i * 2 + 2)
        dve.wait_ge(self.mv_done, i + 1)
        reused(dve, self.turned, i, 2)
        o = self.xn[0:TT, k % 2, :] if dst is None else dst
        nc.vector.tensor_scalar(o, h[0:TT, i, :], self.mv[0:TT, k % 2, 0:1], self.rstd[0:TT, k % 2, 1:2],
                                ALU.subtract, ALU.mult).then_inc(self.xn_done, 1)

    def turn(self, pe, i, k, ready=None, src=None):
        nc = self.g["nc"]
        pe.wait_ge(ready or self.xn_done, i + 1)
        reused(pe, self.kept, i, 2)
        src = self.xn[0:TT, k % 2, :] if src is None else src
        for c in range(KD):
            mm = nc.tensor.transpose(self.psT[:, k % 2, c * TT:(c + 1) * TT], src[:, c * 128:(c + 1) * 128],
                                     self.g["ident"][0:TT, 0:TT])
        mm.then_inc(self.turned, 1)

    def keep(self, act, i, k):
        nc, xT = self.g["nc"], self.g["xT"]
        act.wait_ge(self.turned, i + 1)
        through(act, i, self.g["passed"])
        nc.scalar.activation(xT[:, :, cols(i)], self.psT[:, k % 2, 0:KD * TT].rearrange("p (c t) -> p c t", c=KD),
                             ACT.Copy).then_inc(self.kept, 1)


    def keep_stationary(self, act, i, k, used):
        act.wait_ge(self.turned, i + 1)
        reused(act, used, i, 2)
        self.g["nc"].scalar.activation(self.xs[:, k % 2, :, :],
                                       self.psT[:, k % 2, 0:KD * TT].rearrange("p (c t) -> p c t", c=KD),
                                       ACT.Copy).then_inc(self.xs_kept, 1)


def cols(i, n=1):
    return slice(i * TT, i * TT + n * TT) if isinstance(i, int) else bass.ds(i * TT, n * TT)


def embed(g):
    nc, a, sb, pb, sem, h, ident = (g[k] for k in ("nc", "a", "sb", "pb", "sem", "h", "ident"))
    loaded = g["loaded"]
    with ExitStack() as c:
        NP = 4
        wT = sb("tok_wT", [128, KP, D], c=c)
        patches = sb("patches", [128, NP, KP, TT], c=c)
        base = sb("base", [128, D], c=c)
        pos = sb("pos", [128, D], c=c)
        psE = pb("psE", [128, 2, 512], c=c)
        patches_in = [sem(f"patches_in{s}", c) for s in range(NP)]
        mhalf_set = sem("mhalf_set", c)
        base_done = sem("base_done", c)
        embedded = sem("embedded", c)
        h_done = sem("h_done", c)
        ln = LayerNorm(g, c, "ln0")
        block = c.enter_context(nc.Block())

        @block.sync
        def _(sp):
            sp.dma_start(wT[:, :, :], a["tok_WT"].rearrange("(c p) d -> p c d", p=128)).then_inc(loaded, 16)
            sp.dma_start(base[0:TT, :], a["cls_or_b"]).then_inc(loaded, 16)
            sp.dma_start(pos[0:TT, :], a["pos"]).then_inc(loaded, 16)
            sp.dma_start(ident[:, :], a["ident"]).then_inc(loaded, 16)

            def load(i, k):
                reused(sp, embedded, i, NP)
                sp.dma_start(patches[:, k, :, :], a["patchesT"][:, i, :, :]).then_inc(patches_in[k], 16)
            run(sp, NT, NP, [(0, load)])

        @block.tensor
        def _(pe):
            pe.wait_ge(loaded, 64)

            def project(i, k):
                pe.wait_ge(patches_in[k], (i - k) * (16 // NP) + 16)
                reused(pe, h_done, i, 2)
                for kc in range(KP):
                    mm = nc.tensor.matmul(psE[0:TT, k % 2, 0:D], patches[:, k, kc, :], wT[:, kc, :],
                                          start=kc == 0, stop=kc == KP - 1)
                mm.then_inc(embedded, 1)
            run(pe, NT, NP, [(0, project), (2, lambda i, k: ln.turn(pe, i, k))])

        @block.vector
        def _(dve):
            nc.vector.memset(g["mhalf"][:, :], -0.5).then_inc(mhalf_set, 1)
            nc.vector.memset(g["epsilon"][:, 0:1], 1e-5).then_inc(mhalf_set, 1)
            nc.vector.memset(g["epsilon"][:, 1:2], 1e-6).then_inc(mhalf_set, 1)
            dve.wait_ge(loaded, 64)
            nc.vector.tensor_tensor(base[0:TT, :], base[0:TT, :], pos[0:TT, :], ALU.add).then_inc(base_done, 1)
            dve.wait_ge(base_done, 1)
            nc.vector.tensor_copy(g["identb"][:, :], ident[:, :]).then_inc(base_done, 1)

            def add(i, k):
                dve.wait_ge(embedded, i + 1)
                nc.vector.tensor_tensor(h[0:TT, i, :], psE[0:TT, k % 2, 0:D], base[0:TT, :],
                                        ALU.add).then_inc(h_done, 1)
            run(dve, NT, NP, [(0, add), (0, lambda i, k: ln.statistics(dve, i, k, h_done)),
                              (1, lambda i, k: ln.normalise(dve, i, k))])

        @block.gpsimd
        def _(pool):
            pool.wait_ge(mhalf_set, 3)
            run(pool, NT, NP, [(0, lambda i, k: ln.inverse(pool, i, k))])

        @block.scalar
        def _(act):
            run(act, NT, NP, [(2, lambda i, k: ln.keep(act, i, k))])


def attention(g):
    nc, a, sb, pb, sem, h, xT, ident = (g[k] for k in ("nc", "a", "sb", "pb", "sem", "h", "xT", "ident"))
    identb = g["identb"]
    U = 4
    with ExitStack() as c:
        wqk = sb("wqk", [128, 2, KD, INNER], c=c)
        wv = sb("wv", [128, KD, INNER], c=c)
        wo = sb("wo", [128, KI, D], c=c)
        bo = sb("bo", [128, D], c=c)
        mask = sb("mask", [128, 4 * TT], BF16, c=c)
        mask_f32 = sb("mask_f32", [128, 4 * TT], c=c)
        xs = sb("xs", [128, 2, KD, TT], c=c)
        qk = sb("qk", [128, 2, 2 * KI, 2 * TT], c=c)
        v = sb("v", [128, U, INNER], c=c)
        s = sb("s", [128, 2, HEADS, TT], c=c)
        pT = sb("pT", [128, HEADS, TT], c=c)
        oT = sb("oT", [128, 2, KI, TT], c=c)
        top = sb("top", [128, 2, HEADS], c=c)
        total = sb("total", [128, 2, HEADS], c=c)
        inv = sb("inv", [128, 2, HEADS], c=c)
        psS = pb("psS", [128, 2, 2, 512], c=c)
        psP = pb("psP", [128, 2, 512], c=c)
        psT = pb("psT", [128, 512], c=c)
        psO = pb("psO", [128, 512], c=c)
        weights_in = sem("attn_weights_in", c)
        xs_done = sem("xs_done", c)
        mask_done = sem("mask_done", c)
        proj_filled = sem("proj_filled", c)
        proj_freed = sem("proj_freed", c)
        scores_done = sem("scores_done", c)
        top_done = sem("top_done", c)
        shifted = sem("shifted", c)
        exp_done = sem("exp_done", c)
        total_done = sem("total_done", c)
        inv_done = sem("inv_done", c)
        prob_done = sem("prob_done", c)
        pT_filled = sem("pT_filled", c)
        pT_kept = sem("pT_kept", c)
        oT_filled = sem("oT_filled", c)
        oT_kept = sem("oT_kept", c)
        wo_done = sem("wo_done", c)
        h_done = sem("attn_h_done", c)
        h_bias = sem("attn_h_bias", c)
        block = c.enter_context(nc.Block())
        NLOAD = 6 * 16

        def unit(t, k, n):
            return t * 6 + n if k % 2 == 0 else (t - 1) * 6 + 10 + n

        @block.sync
        def _(sp):
            for j, w in enumerate(("Wq", "Wk")):
                sp.dma_start(wqk[:, j, :, :], a[w].rearrange("(c p) n -> p c n", p=128)).then_inc(weights_in, 16)
            sp.dma_start(wv[:, :, :], a["Wv"].rearrange("(c p) n -> p c n", p=128)).then_inc(weights_in, 16)
            sp.dma_start(wo[:, :, :], a["Wo"].rearrange("(c p) n -> p c n", p=128)).then_inc(weights_in, 16)
            sp.dma_start(bo[0:TT, :], a["bo"]).then_inc(weights_in, 16)
            sp.dma_start(mask_f32[0:TT, :], a["mask4"]).then_inc(weights_in, 16)

        @block.gpsimd
        def _(pool):
            def stationary(i, k):
                if not (isinstance(i, int) and i < 2):
                    pool.wait_ge(proj_filled, unit(i - 2, k, 1) + 1)
                through(pool, i, g["passed"])
                nc.gpsimd.tensor_copy(xs[:, k % 2, :, :], xT[:, :, cols(i)]).then_inc(xs_done, 1)
            run(pool, NT, U, [(0, stationary)])

        @block.tensor
        def _(pe):
            pe.wait_ge(weights_in, NLOAD)
            pe.wait_ge(mask_done, 1)

            def free_unit(t, k, n):
                if not (isinstance(t, int) and unit(t, k, n) < 2):
                    pe.wait_ge(proj_freed, unit(t, k, n) - 1)

            def values(n):
                def fn(t, k):
                    if n == 0:
                        pe.wait_ge(xs_done, t + 1)
                    free_unit(t, k, n)
                    for kc in range(KD):
                        mm = nc.tensor.matmul(psP[0:TT, n % 2, :], xs[:, k % 2, kc, :],
                                              wv[:, kc, n * 512:(n + 1) * 512], start=kc == 0, stop=kc == KD - 1)
                    mm.then_inc(proj_filled, 1)
                return fn

            def queries_keys(t, k):
                if k % 2:
                    return
                for n in range(8):
                    free_unit(t, k, n + 2)
                    for half in range(2):
                        ch = 2 * n + half
                        for kc in range(KD):
                            mm = nc.tensor.matmul(psP[:, n % 2, half * 2 * TT:(half + 1) * 2 * TT],
                                                  wqk[:, ch // KI, kc, (ch % KI) * 128:(ch % KI + 1) * 128],
                                                  xT[:, kc, cols(t, 2)], start=kc == 0, stop=kc == KD - 1)
                    mm.then_inc(proj_filled, 1)

            def scores(hf):
                def fn(i, k):
                    base = i if k % 2 == 0 else i - 1
                    pe.wait_ge(proj_freed, base * 6 + 10)
                    reused(pe, shifted, i, 1, 2, hf - 1)
                    for p in range(2):
                        nc.tensor.matmul(psS[0:TT, hf, p, 0:4 * TT], identb[0:TT, 0:TT], mask[0:TT, :],
                                         start=True, stop=False)
                        for j in range(4):
                            ch = hf * 4 + j
                            q = qk[64 * p:64 * p + 64, (k // 2) % 2, ch, (k % 2) * TT:(k % 2 + 1) * TT]
                            kk = qk[64 * p:64 * p + 64, (k // 2) % 2, KI + ch, (k % 2) * TT:(k % 2 + 1) * TT]
                            mm = nc.tensor.matmul(psS[0:TT, hf, p, j * TT:(j + 1) * TT], q, kk,
                                                  start=False, stop=j == 3)
                    mm.then_inc(scores_done, 1)
                return fn

            def turn(q):
                def fn(i, k):
                    pe.wait_ge(prob_done, i * 2 + q // 2 + 1)
                    if q or not isinstance(i, int) or i:
                        pe.wait_ge(pT_kept, i * 4 + q)
                    for j in range(4):
                        mm = nc.tensor.transpose(psT[0:TT, j * TT:(j + 1) * TT], s[0:TT, k % 2, 4 * q + j, :],
                                                 ident[0:TT, 0:TT])
                    mm.then_inc(pT_filled, 1)
                return fn

            def mix(hf):
                def fn(i, k):
                    pe.wait_ge(pT_kept, i * 4 + 2 * hf + 2)
                    if hf == 0:
                        pe.wait_ge(proj_freed, unit(i, k, 1) + 1)
                        reused(pe, h_done, i, 1)
                    else:
                        pe.wait_ge(oT_kept, i * 2 + 1)
                    for j in range(4):
                        for p in range(2):
                            head = 2 * (4 * hf + j) + p
                            mm = nc.tensor.matmul(psO[64 * p:64 * p + 64, j * TT:(j + 1) * TT],
                                                  v[0:TT, k, head * HD:(head + 1) * HD],
                                                  pT[0:TT, 8 * hf + 4 * p + j, :], start=True, stop=True)
                    mm.then_inc(oT_filled, 1)
                return fn

            def output(i, k):
                pe.wait_ge(oT_kept, i * 2 + 2)
                for ch in range(KI):
                    mm = nc.tensor.matmul(psO[0:TT, 0:D], oT[:, k % 2, ch, :], wo[:, ch, :],
                                          start=ch == 0, stop=ch == KI - 1)
                mm.then_inc(wo_done, 1)

            run(pe, NT, U, [(0, values(0)), (3, turn(0)), (0, values(1)), (3, turn(1)), (2, scores(0)),
                            (3, turn(2)), (3, mix(0)), (2, scores(1)), (3, turn(3)), (3, mix(1)),
                            (0, queries_keys), (3, output)])

        @block.scalar
        def _(act):
            def values(n):
                def fn(t, k):
                    act.wait_ge(proj_filled, unit(t, k, n) + 1)
                    reused(act, oT_filled, t, U, 2)
                    nc.scalar.activation(v[0:TT, k, n * 512:(n + 1) * 512], psP[0:TT, n % 2, :],
                                         ACT.Copy).then_inc(proj_freed, 1)
                return fn

            def queries_keys(lo, hi):
                def fn(t, k):
                    if k % 2:
                        return
                    for n in range(lo, hi):
                        act.wait_ge(proj_filled, unit(t, k, n + 2) + 1)
                        if n == 0 and not (isinstance(t, int) and t < 4):
                            act.wait_ge(scores_done, (t - 2) * 2)
                        nc.scalar.activation(
                            qk[:, (k // 2) % 2, 2 * n:2 * n + 2, :],
                            psP[:, n % 2, 0:4 * TT].rearrange("p (c t) -> p c t", c=2),
                            ACT.Copy).then_inc(proj_freed, 1)
                return fn

            def keep_pT(q):
                def fn(i, k):
                    act.wait_ge(pT_filled, i * 4 + q + 1)
                    if not (isinstance(i, int) and i < 1):
                        act.wait_ge(oT_filled, (i - 1) * 2 + q // 2 + 1)
                    nc.scalar.activation(pT[0:TT, 4 * q:4 * q + 4, :],
                                         psT[0:TT, 0:4 * TT].rearrange("p (j t) -> p j t", j=4),
                                         ACT.Copy).then_inc(pT_kept, 1)
                return fn

            def keep_oT(hf):
                def fn(i, k):
                    act.wait_ge(oT_filled, i * 2 + hf + 1)
                    reused(act, wo_done, i, 2)
                    nc.scalar.activation(oT[:, k % 2, 4 * hf:4 * hf + 4, :],
                                         psO[:, 0:4 * TT].rearrange("p (j t) -> p j t", j=4),
                                         ACT.Copy).then_inc(oT_kept, 1)
                return fn

            def exps(hf):
                def fn(i, k):
                    act.wait_ge(shifted, i * 2 + hf + 1)
                    sv = s[0:TT, k % 2, 8 * hf:8 * hf + 8, :]
                    nc.scalar.activation(sv, sv, ACT.Exp, scale=HD ** -0.5).then_inc(exp_done, 1)
                return fn

            run(act, NT, U, [(0, values(0)), (3, keep_pT(0)), (0, values(1)), (3, keep_pT(1)),
                             (3, keep_pT(2)), (3, keep_oT(0)), (3, keep_pT(3)), (3, keep_oT(1)),
                             (2, exps(0)), (0, queries_keys(0, 4)), (2, exps(1)), (0, queries_keys(4, 8))])

        @block.vector
        def _(dve):
            dve.wait_ge(weights_in, NLOAD)
            nc.vector.tensor_copy(mask[0:TT, :], mask_f32[0:TT, :]).then_inc(mask_done, 1)

            def shift(hf):
                def fn(i, k):
                    dve.wait_ge(scores_done, i * 2 + hf + 1)
                    reused(dve, shifted, i, 1, 2, hf - 1)
                    src = psS[0:TT, hf, :, 0:4 * TT].rearrange("q p (j t) -> q p j t", j=4)
                    tv = top[0:TT, hf, 0:8]
                    nc.vector.tensor_reduce(tv.rearrange("q (p j) -> q p j", p=2), src, AX.X, ALU.max)\
                        .then_inc(top_done, 1)
                    dve.wait_ge(top_done, i * 2 + hf + 1)
                    reused(dve, pT_filled, i, 2, 4, 0)
                    nc.vector.tensor_tensor(
                        s[0:TT, k % 2, 8 * hf:8 * hf + 8, :].rearrange("q (p j) t -> q p j t", p=2), src,
                        tv.rearrange("q (p j) -> q p j", p=2).unsqueeze(3).broadcast_to([TT, 2, 4, TT]),
                        ALU.subtract).then_inc(shifted, 1)
                return fn

            def scale(hf):
                def fn(i, k):
                    dve.wait_ge(exp_done, i * 2 + hf + 1)
                    sv = s[0:TT, k % 2, 8 * hf:8 * hf + 8, :]
                    nc.vector.tensor_reduce(total[0:TT, hf, 0:8], sv, AX.X, ALU.add).then_inc(total_done, 1)
                    dve.wait_ge(total_done, i * 2 + hf + 1)
                    nc.vector.reciprocal(inv[0:TT, hf, 0:8], total[0:TT, hf, 0:8]).then_inc(inv_done, 1)
                    dve.wait_ge(inv_done, i * 2 + hf + 1)
                    nc.vector.tensor_tensor(sv, sv, inv[0:TT, hf, 0:8].unsqueeze(2).broadcast_to([TT, 8, TT]),
                                            ALU.mult).then_inc(prob_done, 1)
                return fn

            def add(i, k):
                nc.vector.tensor_tensor(h[0:TT, i, :], h[0:TT, i, :], bo[0:TT, :], ALU.add).then_inc(h_bias, 1)
                dve.wait_ge(h_bias, i + 1)
                dve.wait_ge(wo_done, i + 1)
                nc.vector.tensor_tensor(h[0:TT, i, :], h[0:TT, i, :], psO[0:TT, 0:D], ALU.add)\
                    .then_inc(h_done, 1)

            run(dve, NT, U, [(2, shift(0)), (2, shift(1)), (2, scale(0)), (2, scale(1)), (3, add)])


def linker(eng, sem):
    count = [0]

    def link(ins):
        count[0] += 1
        ins.then_inc(sem, 1)
        eng.wait_ge(sem, count[0])
    return link


def one_hot_of_max(nc, link, x, top, hit, number, number_less_e, first):
    wide = [TT, NT, E]
    link(nc.vector.tensor_reduce(top, x, AX.X, ALU.max))
    link(nc.vector.tensor_tensor(hit, x, top.unsqueeze(2).broadcast_to(wide), ALU.is_equal))
    link(nc.vector.tensor_tensor(number, hit, number_less_e.unsqueeze(1).broadcast_to(wide), ALU.mult))
    link(nc.vector.tensor_reduce(first, number, AX.X, ALU.min))
    link(nc.vector.tensor_tensor(hit, number_less_e.unsqueeze(1).broadcast_to(wide),
                                 first.unsqueeze(2).broadcast_to(wide), ALU.is_equal))


def route_top1(g, weight):
    nc, a, sb, pb, sem, h, xT = (g[k] for k in ("nc", "a", "sb", "pb", "sem", "h", "xT"))
    U = 2
    with ExitStack() as c:
        ln = LayerNorm(g, c, "ln1", slots=True)
        rms_w = sb("rms_w", [128, D], c=c)
        gate = sb("gate", [128, KD, E], c=c)
        less_e = sb("less_e", [128, E], c=c)
        square = sb("square", [128, D], c=c)
        ms = sb("ms", [128, 2, 3], c=c)
        xr = sb("xr", [128, 2, D], c=c)
        logits = sb("logits", [128, NT, E], c=c)
        p = sb("p", [128, NT, E], c=c)
        top, first, total, best = (sb(n, [128, NT], c=c) for n in ("r_top", "r_first", "r_total", "r_best"))
        psG = pb("psG", [128, 2, 512], c=c)
        weights_in = sem("gate_weights_in", c)
        ms_done = sem("ms_done", c)
        ms_eps = sem("ms_eps", c)
        rms_done = sem("rms_done", c)
        xr_done = sem("xr_done", c)
        gated = sem("gated", c)
        logits_done = sem("logits_done", c)
        chain = sem("route_chain", c)
        shift_done = sem("route_shift_done", c)
        exp_done = sem("route_exp_done", c)
        block = c.enter_context(nc.Block())

        @block.sync
        def _(sp):
            sp.dma_start(rms_w[0:TT, :], a["ffn_rms_w"]).then_inc(weights_in, 16)
            sp.dma_start(gate[:, :, :], a["gate_wT"].rearrange("(c p) e -> p c e", p=128)).then_inc(weights_in, 16)
            sp.dma_start(less_e[0:TT, :], a["number_less_e"]).then_inc(weights_in, 16)

        @block.vector
        def _(dve):
            dve.wait_ge(weights_in, 48)

            def mean_square(i, k):
                dve.wait_ge(ln.xn_done, i + 1)
                reused(dve, xr_done, i, 2)
                nc.vector.scalar_tensor_tensor(out=square[0:TT, :], in0=ln.xn[0:TT, k % 2, :], scalar=1.0 / D,
                                               in1=ln.xn[0:TT, k % 2, :], op0=ALU.mult, op1=ALU.mult,
                                               accum_out=ms[0:TT, k % 2, 0:1]).then_inc(ms_done, 1)

            def rms(i, k):
                dve.wait_ge(rms_done, i + 1)
                reused(dve, ln.turned, i, 2)
                nc.vector.scalar_tensor_tensor(out=xr[0:TT, k % 2, :], in0=ln.xn[0:TT, k % 2, :],
                                               scalar=ms[0:TT, k % 2, 2:3], in1=rms_w[0:TT, :],
                                               op0=ALU.mult, op1=ALU.mult).then_inc(xr_done, 1)

            def normalise(i, k):
                reused(dve, xr_done, i, 2)
                ln.normalise(dve, i, k)

            def keep_logits(i, k):
                dve.wait_ge(gated, i + 1)
                nc.vector.tensor_scalar(logits[0:TT, i, :], psG[0:TT, k % 2, 0:E], 0.0, None, ALU.add)\
                    .then_inc(logits_done, 1)
            run(dve, NT, U, [(0, lambda i, k: ln.statistics(dve, i, k)), (1, normalise), (1, mean_square),
                             (2, rms), (4, keep_logits)])
            link = linker(dve, chain)
            dve.wait_ge(logits_done, NT)
            hit, number = p, weight
            one_hot_of_max(nc, link, logits[0:TT], top[0:TT], hit[0:TT], number[0:TT], less_e[0:TT], first[0:TT])
            nc.vector.tensor_tensor(logits[0:TT], logits[0:TT], top[0:TT].unsqueeze(2).broadcast_to([TT, NT, E]),
                                    ALU.subtract).then_inc(shift_done, 1)
            dve.wait_ge(exp_done, 1)
            link(nc.vector.tensor_reduce(total[0:TT], logits[0:TT], AX.X, ALU.add))
            link(nc.vector.tensor_reduce(best[0:TT], logits[0:TT], AX.X, ALU.max))
            link(nc.vector.reciprocal(total[0:TT], total[0:TT]))
            link(nc.vector.tensor_tensor(best[0:TT], best[0:TT], total[0:TT], ALU.mult))
            link(nc.vector.tensor_tensor(weight[0:TT], hit[0:TT], best[0:TT].unsqueeze(2).broadcast_to([TT, NT, E]),
                                         ALU.mult))

        @block.gpsimd
        def _(pool):
            def inverse_rms(i, k):
                pool.wait_ge(ms_done, i + 1)
                nc.gpsimd.tensor_tensor(ms[0:TT, k % 2, 1:2], ms[0:TT, k % 2, 0:1], g["epsilon"][0:TT, 1:2],
                                        ALU.add).then_inc(ms_eps, 1)
                pool.wait_ge(ms_eps, i + 1)
                nc.gpsimd.tensor_tensor(ms[0:TT, k % 2, 2:3], ms[0:TT, k % 2, 1:2], g["mhalf"][0:TT, :],
                                        ALU.pow).then_inc(rms_done, 1)
            run(pool, NT, U, [(0, lambda i, k: ln.inverse(pool, i, k)), (1, inverse_rms)])

        @block.tensor
        def _(pe):
            pe.wait_ge(weights_in, 48)

            def logit(i, k):
                pe.wait_ge(ln.xs_kept, i + 1)
                reused(pe, logits_done, i, 2)
                for kc in range(KD):
                    mm = nc.tensor.matmul(psG[0:TT, k % 2, 0:E], ln.xs[:, k % 2, kc, :], gate[:, kc, :],
                                          start=kc == 0, stop=kc == KD - 1)
                mm.then_inc(gated, 1)
            run(pe, NT, U, [(2, lambda i, k: ln.turn(pe, i, k, xr_done, xr[0:TT, k % 2, :])), (3, logit)])

        @block.scalar
        def _(act):
            run(act, NT, U, [(2, lambda i, k: ln.keep_stationary(act, i, k, gated)),
                             (2, lambda i, k: ln.keep(act, i, k))])
            act.wait_ge(shift_done, 1)
            nc.scalar.activation(logits[0:TT], logits[0:TT], ACT.Exp).then_inc(exp_done, 1)


def route_top2(g, weight):
    nc, a, sb, pb, sem, h, xT = (g[k] for k in ("nc", "a", "sb", "pb", "sem", "h", "xT"))
    U = 2
    with ExitStack() as c:
        ln = LayerNorm(g, c, "ln3", slots=True)
        rw1 = sb("rw1", [128, KD, D], c=c)
        rb1 = sb("rb1", [128, KD], c=c)
        rw2 = sb("rw2", [128, KD, E], c=c)
        rb2 = sb("rb2", [128, E], c=c)
        less_e = sb("less_e2", [128, E], c=c)
        hidden = sb("hidden", [128, 2, KD, TT], c=c)
        logits = sb("logits2", [128, NT, E], c=c)
        rest, hit1, hit2 = (sb(n, [128, NT, E], c=c) for n in ("r_rest", "r_hit1", "r_hit2"))
        top1, top2, first, total = (sb(n, [128, NT], c=c) for n in ("r_top1", "r_top2", "r2_first", "r2_total"))
        psH = pb("psRH", [128, 2, 512], c=c)
        psG = pb("psRG", [128, 2, 512], c=c)
        weights_in = sem("router_weights_in", c)
        hidden_filled = sem("hidden_filled", c)
        hidden_kept = sem("hidden_kept", c)
        gated = sem("gated2", c)
        logits_done = sem("logits2_done", c)
        h_done = sem("router_h_done", c)
        chain = sem("route2_chain", c)
        shift_done = sem("route2_shift_done", c)
        exp_done = sem("route2_exp_done", c)
        block = c.enter_context(nc.Block())

        @block.sync
        def _(sp):
            sp.dma_start(rw1[:, :, :], a["rw1"].rearrange("(c p) e -> p c e", p=128)).then_inc(weights_in, 16)
            sp.dma_start(rw2[:, :, :], a["rw2"].rearrange("(c p) e -> p c e", p=128)).then_inc(weights_in, 16)
            sp.dma_start(rb1[:, :], a["rb1"]).then_inc(weights_in, 16)
            sp.dma_start(rb2[0:TT, :], a["rb2"]).then_inc(weights_in, 16)
            sp.dma_start(less_e[0:TT, :], a["number_less_e"]).then_inc(weights_in, 16)

        @block.vector
        def _(dve):
            dve.wait_ge(weights_in, 80)

            def residual(i, k):
                dve.wait_ge(ln.xn_done, i + 1)
                nc.vector.tensor_tensor(h[0:TT, i, :], h[0:TT, i, :], ln.xn[0:TT, k % 2, :], ALU.add)\
                    .then_inc(h_done, 1)

            def normalise(i, k):
                reused(dve, h_done, i, 2)
                ln.normalise(dve, i, k)

            def keep_logits(i, k):
                dve.wait_ge(gated, i + 1)
                nc.vector.tensor_tensor(logits[0:TT, i, :], psG[0:TT, k % 2, 0:E], rb2[0:TT, :], ALU.add)\
                    .then_inc(logits_done, 1)
            run(dve, NT, U, [(0, lambda i, k: ln.statistics(dve, i, k)), (1, normalise), (1, residual),
                             (3, keep_logits)])
            link = linker(dve, chain)
            dve.wait_ge(logits_done, NT)
            wide = [TT, NT, E]
            number = weight
            one_hot_of_max(nc, link, logits[0:TT], top1[0:TT], hit1[0:TT], number[0:TT], less_e[0:TT], first[0:TT])
            link(nc.vector.scalar_tensor_tensor(out=rest[0:TT], in0=hit1[0:TT], scalar=-1.0e30, in1=logits[0:TT],
                                                op0=ALU.mult, op1=ALU.add))
            one_hot_of_max(nc, link, rest[0:TT], top2[0:TT], hit2[0:TT], number[0:TT], less_e[0:TT], first[0:TT])
            nc.vector.tensor_tensor(top2[0:TT], top2[0:TT], top1[0:TT], ALU.subtract).then_inc(shift_done, 1)
            dve.wait_ge(exp_done, 1)
            link(nc.vector.tensor_scalar(total[0:TT], top2[0:TT], 1.0, None, ALU.add))
            link(nc.vector.reciprocal(total[0:TT], total[0:TT]))
            link(nc.vector.tensor_tensor(top2[0:TT], top2[0:TT], total[0:TT], ALU.mult))
            link(nc.vector.tensor_tensor(hit1[0:TT], hit1[0:TT], total[0:TT].unsqueeze(2).broadcast_to(wide), ALU.mult))
            link(nc.vector.tensor_tensor(hit2[0:TT], hit2[0:TT], top2[0:TT].unsqueeze(2).broadcast_to(wide), ALU.mult))
            link(nc.vector.tensor_tensor(weight[0:TT], hit1[0:TT], hit2[0:TT], ALU.add))

        @block.gpsimd
        def _(pool):
            run(pool, NT, U, [(0, lambda i, k: ln.inverse(pool, i, k))])

        @block.tensor
        def _(pe):
            pe.wait_ge(weights_in, 80)

            def hide(i, k):
                pe.wait_ge(ln.xs_kept, i + 1)
                reused(pe, hidden_kept, i, 2)
                for m in range(KD):
                    for kc in range(KD):
                        mm = nc.tensor.matmul(psH[:, k % 2, m * TT:(m + 1) * TT], rw1[:, kc, m * 128:(m + 1) * 128],
                                              ln.xs[:, k % 2, kc, :], start=kc == 0, stop=kc == KD - 1)
                mm.then_inc(hidden_filled, 1)

            def logit(i, k):
                pe.wait_ge(hidden_kept, i + 1)
                reused(pe, logits_done, i, 2)
                for kc in range(KD):
                    mm = nc.tensor.matmul(psG[0:TT, k % 2, 0:E], hidden[:, k % 2, kc, :], rw2[:, kc, :],
                                          start=kc == 0, stop=kc == KD - 1)
                mm.then_inc(gated, 1)
            run(pe, NT, U, [(1, lambda i, k: ln.turn(pe, i, k)), (2, hide), (3, logit)])

        @block.scalar
        def _(act):
            act.wait_ge(weights_in, 80)

            def keep_hidden(i, k):
                act.wait_ge(hidden_filled, i + 1)
                reused(act, gated, i, 2)
                for m in range(KD):
                    ins = nc.scalar.activation(hidden[:, k % 2, m, :], psH[:, k % 2, m * TT:(m + 1) * TT], ACT.Silu,
                                               bias=rb1[:, m:m + 1])
                ins.then_inc(hidden_kept, 1)
            run(act, NT, U, [(1, lambda i, k: ln.keep_stationary(act, i, k, hidden_filled)),
                             (1, lambda i, k: ln.keep(act, i, k)), (2, keep_hidden)])
            act.wait_ge(shift_done, 1)
            nc.scalar.activation(top2[0:TT], top2[0:TT], ACT.Exp).then_inc(exp_done, 1)


def step_sizes(g, ln_out, dt, dA):
    nc, a, sb, pb, sem, h, xT = (g[k] for k in ("nc", "a", "sb", "pb", "sem", "h", "xT"))
    U = 2
    with ExitStack() as c:
        ln = LayerNorm(g, c, "ln2", slots=True)
        wdt = sb("wdt", [128, KD, MH], c=c)
        dt_bias = sb("dt_bias", [128, MH], c=c)
        A_log = sb("A_log", [128, MH], c=c)
        A_exp = sb("A_exp", [128, MH], c=c)
        raw, u, w, lnw, t0 = (sb("sp_" + n, [128, NT, MH], c=c) for n in ("raw", "u", "w", "lnw", "t0"))
        psD = pb("psD", [128, 2, 512], c=c)
        weights_in = sem("dt_weights_in", c)
        dt_filled = sem("dt_filled", c)
        raw_done = sem("dt_raw_done", c)
        xn_kept = sem("xn_kept", c)
        chain = sem("dt_chain", c)
        abs_done = sem("dt_abs_done", c)
        exp_done = sem("dt_exp_done", c)
        w_done = sem("dt_w_done", c)
        ln_done = sem("dt_ln_done", c)
        block = c.enter_context(nc.Block())

        @block.sync
        def _(sp):
            sp.dma_start(wdt[:, :, :], a["W_in"].rearrange("(c p) n -> p c n", p=128)[:, :, DI + CONV:])\
                .then_inc(weights_in, 16)
            sp.dma_start(dt_bias[0:TT, :], a["dt_bias"]).then_inc(weights_in, 16)
            sp.dma_start(A_log[0:TT, :], a["A_log"]).then_inc(weights_in, 16)

        @block.vector
        def _(dve):
            dve.wait_ge(weights_in, 48)

            def normalise(i, k):
                reused(dve, xn_kept, i, 2)
                ln.normalise(dve, i, k)

            def keep_raw(i, k):
                dve.wait_ge(dt_filled, i + 1)
                nc.vector.tensor_tensor(raw[0:TT, i, :], psD[0:TT, k % 2, 0:MH], dt_bias[0:TT, :], ALU.add)\
                    .then_inc(raw_done, 1)
            run(dve, NT, U, [(0, lambda i, k: ln.statistics(dve, i, k)), (1, normalise), (3, keep_raw)])
            link = linker(dve, chain)
            dve.wait_ge(raw_done, NT)
            nc.vector.scalar_tensor_tensor(out=u[0:TT], in0=raw[0:TT], scalar=-1.0, in1=raw[0:TT],
                                           op0=ALU.mult, op1=ALU.max).then_inc(abs_done, 1)
            dve.wait_ge(exp_done, 1)
            nc.vector.tensor_scalar(w[0:TT], u[0:TT], 1.0, None, ALU.add).then_inc(w_done, 1)
            dve.wait_ge(ln_done, 1)
            link(nc.vector.tensor_scalar(w[0:TT], w[0:TT], -1.0, None, ALU.add))
            link(nc.vector.tensor_scalar(t0[0:TT], w[0:TT], 0.0, None, ALU.is_equal))
            link(nc.vector.tensor_tensor(w[0:TT], w[0:TT], t0[0:TT], ALU.add))
            link(nc.vector.reciprocal(w[0:TT], w[0:TT]))
            link(nc.vector.tensor_tensor(lnw[0:TT], lnw[0:TT], w[0:TT], ALU.mult))
            link(nc.vector.tensor_tensor(lnw[0:TT], lnw[0:TT], t0[0:TT], ALU.add))
            link(nc.vector.tensor_tensor(u[0:TT], u[0:TT], lnw[0:TT], ALU.mult))
            link(nc.vector.scalar_tensor_tensor(out=dt[0:TT], in0=raw[0:TT], scalar=0.0, in1=u[0:TT],
                                                op0=ALU.max, op1=ALU.add))
            link(nc.vector.scalar_tensor_tensor(out=dA[0:TT], in0=dt[0:TT], scalar=-1.0,
                                                in1=A_exp[0:TT].unsqueeze(1).broadcast_to([TT, NT, MH]),
                                                op0=ALU.mult, op1=ALU.mult))

        @block.gpsimd
        def _(pool):
            def keep_xn(i, k):
                pool.wait_ge(ln.xn_done, i + 1)
                through(pool, i, g["passed"])
                nc.gpsimd.tensor_copy(ln_out[0:TT, i, :], ln.xn[0:TT, k % 2, :]).then_inc(xn_kept, 1)
            run(pool, NT, U, [(0, lambda i, k: ln.inverse(pool, i, k)), (1, keep_xn)])

        @block.tensor
        def _(pe):
            pe.wait_ge(weights_in, 48)

            def product(i, k):
                pe.wait_ge(ln.xs_kept, i + 1)
                reused(pe, raw_done, i, 2)
                for kc in range(KD):
                    mm = nc.tensor.matmul(psD[0:TT, k % 2, 0:MH], ln.xs[:, k % 2, kc, :], wdt[:, kc, :],
                                          start=kc == 0, stop=kc == KD - 1)
                mm.then_inc(dt_filled, 1)
            run(pe, NT, U, [(1, lambda i, k: ln.turn(pe, i, k)), (2, product)])

        @block.scalar
        def _(act):
            act.wait_ge(weights_in, 48)
            run(act, NT, U, [(1, lambda i, k: ln.keep_stationary(act, i, k, dt_filled)),
                             (1, lambda i, k: ln.keep(act, i, k))])
            nc.scalar.activation(A_exp[0:TT], A_log[0:TT], ACT.Exp)
            act.wait_ge(abs_done, 1)
            nc.scalar.activation(u[0:TT], u[0:TT], ACT.Exp, scale=-1.0).then_inc(exp_done, 1)
            act.wait_ge(w_done, 1)
            nc.scalar.activation(lnw[0:TT], w[0:TT], ACT.Ln).then_inc(ln_done, 1)


def mamba(g):
    nc, a, sb, pb, sem, h, xT, ident = (g[k] for k in ("nc", "a", "sb", "pb", "sem", "h", "xT", "ident"))
    U = 2
    PAD = 3
    UN = 2 * TT
    NU = KC // 2
    KY = DI // 128
    HH = MH // 2
    with ExitStack() as c:
        xn = sb("xn", [128, NT, D], c=c)
        dt = sb("dt", [128, NT, MH], c=c)
        dA = sb("dA", [128, NT, MH], c=c)
        step_sizes(g, xn, dt, dA)

        wz = sb("wz", [128, KD, DI], c=c)
        wx = sb("wx", [128, KD, CONV], c=c)
        wout = sb("wout", [128, KY, D], c=c)
        wglu = sb("wglu", [128, KD, 2 * D], c=c)
        glu_b = sb("glu_b", [128, 2 * D], c=c)
        conv_w = sb("conv_w", [128, KC, 4], c=c)
        conv_b = sb("conv_b", [128, KC], c=c)
        out_w = sb("out_w", [128, KY], c=c)
        skip = sb("skip", [128, MH], c=c)
        ln_w = sb("ln_w", [128, D], c=c)
        ln_b = sb("ln_b", [128, D], c=c)
        after = sb("after", [128, TT], c=c)
        upto = sb("upto", [128, TT], c=c)
        causal = sb("causal", [128, TT], c=c)
        xs = sb("m_xs", [128, 2, KD, TT], c=c)
        raw = sb("m_raw", [128, 2, KC, PER, PAD + TOK], c=c)
        acc = sb("m_acc", [128, 2, KC, TT], c=c)
        xbc = sb("m_xbc", [128, 2, KC, TT], c=c)
        zs = sb("m_zs", [128, 2, DI], c=c)
        R = sb("m_R", [128, 2, MH, TT], c=c)
        W = sb("m_W", [128, 2, MH, TT], c=c)
        G = sb("m_G", [128, 2, TT], c=c)
        xdt = sb("m_xdt", [128, 2, DI], c=c)
        xD = sb("m_xD", [128, 2, DI], c=c)
        y = sb("m_y", [128, 2, DI], c=c)
        junk = sb("m_junk", [128, DI], c=c)
        ms = sb("m_ms", [128, 2, 3], c=c)
        yT = sb("m_yT", [128, 2, KY, TT], c=c)
        y1 = sb("m_y1", [128, 2, D], c=c)
        y1T = sb("m_y1T", [128, 2, KD, TT], c=c)
        glu = sb("m_glu", [128, 2, 2 * D], c=c)
        th = sb("m_th", [128, 2, D], c=c)
        y2 = sb("m_y2", [128, 2, D], c=c)
        st = sb("m_st", [128, 2, 6], c=c)
        mv = sb("m_mv", [128, 2, 2], c=c)
        rs = sb("m_rs", [128, 2, 2], c=c)
        nrm = sb("m_nrm", [128, 2, D], c=c)
        psC = pb("psC", [128, 2, 512], c=c)
        psG = pb("psCB", [128, 512], c=c)
        psR = pb("psR", [128, 512], c=c)
        psX = pb("psX", [128, 512], c=c)
        psS = pb("psSeg", [128, 512], c=c)
        psY = pb("psY", [128, 512], c=c)
        psU = pb("psU", [128, 512], c=c)
        names = ("weights_in raw_zeroed wout_done xs_done xbc_filled raw_kept conv_tap xbc_done z_filled zs_done "
                 "R_done x_filled G_filled xdt_done xD_done G_done seg_filled seg_exp W_done y_filled y_summed "
                 "y_gated y_squared ms_eps ms_done yT_filled yT_kept out_filled y1_done y1T_filled y1T_kept "
                 "glu_filled glu_biased tanh_done gated y2_done st_done mv_done rs_eps rs_done nrm_done scaled "
                 "biased h_done").split()
        m = {n: sem("m_" + n, c) for n in names}
        (weights_in, raw_zeroed, wout_done, xs_done, xbc_filled, raw_kept, conv_tap, xbc_done, z_filled, zs_done,
         R_done, x_filled, G_filled, xdt_done, xD_done, G_done, seg_filled, seg_exp, W_done, y_filled, y_summed,
         y_gated, y_squared, ms_eps, ms_done, yT_filled, yT_kept, out_filled, y1_done, y1T_filled, y1T_kept,
         glu_filled, glu_biased, tanh_done, gated, y2_done, st_done, mv_done, rs_eps, rs_done, nrm_done, scaled,
         biased, h_done) = (m[n] for n in names)
        block = c.enter_context(nc.Block())
        loads = [(wz[:, :, :], a["W_in"].rearrange("(c p) n -> p c n", p=128)[:, :, 0:DI]),
                 (wx[:, :, :], a["W_in"].rearrange("(c p) n -> p c n", p=128)[:, :, DI:DI + CONV]),
                 (wout[:, :, :], a["W_out"].rearrange("(c p) n -> p c n", p=128)),
                 (wglu[:, :, :], a["glu_w"].rearrange("(c p) n -> p c n", p=128)),
                 (glu_b[0:TT, :], a["glu_b"]), (conv_w[:, :, :], a["conv_w"]), (conv_b[:, :], a["conv_b"]),
                 (out_w[:, :], a["m_rms_w"]), (skip[0:TT, :], a["D_skip"]), (ln_w[0:TT, :], a["ln_w"]),
                 (ln_b[0:TT, :], a["ln_b"]), (after[0:TT, :], a["after"]), (upto[0:TT, :], a["upto"]),
                 (causal[0:TT, :], a["causal"])]
        ALL = 16 * len(loads)

        @block.sync
        def _(sp):
            for dst, src in loads:
                sp.dma_start(dst, src).then_inc(weights_in, 16)

        @block.gpsimd
        def _(pool):
            passed = g["passed"]
            pool.wait_ge(weights_in, ALL)

            def stationary(i, k):
                reused(pool, z_filled, i, 2)
                through(pool, i, passed)
                nc.gpsimd.tensor_copy(xs[:, k % 2, :, :], xT[:, :, cols(i)]).then_inc(xs_done, 1)

            def spread(i, k):
                reused(pool, seg_filled, i, 2, 2, 0)
                through(pool, i, passed)
                nc.gpsimd.tensor_tensor(R[0:TT, k % 2, :, :], upto[0:TT, :].unsqueeze(1).broadcast_to([TT, MH, TT]),
                                        dA[0:TT, i, :].unsqueeze(2).broadcast_to([TT, MH, TT]), ALU.mult)\
                    .then_inc(R_done, 1)

            def inverse_rms(i, k):
                pool.wait_ge(y_squared, i + 1)
                nc.gpsimd.tensor_tensor(ms[0:TT, k % 2, 1:2], ms[0:TT, k % 2, 0:1], g["epsilon"][0:TT, 0:1],
                                        ALU.add).then_inc(ms_eps, 1)
                pool.wait_ge(ms_eps, i + 1)
                nc.gpsimd.tensor_tensor(ms[0:TT, k % 2, 2:3], ms[0:TT, k % 2, 1:2], g["mhalf"][0:TT, :],
                                        ALU.pow).then_inc(ms_done, 1)

            def inverse_deviation(i, k):
                pool.wait_ge(mv_done, i + 1)
                reused(pool, nrm_done, i, 2)
                nc.gpsimd.tensor_tensor(rs[0:TT, k % 2, 0:1], mv[0:TT, k % 2, 1:2], g["epsilon"][0:TT, 0:1],
                                        ALU.add).then_inc(rs_eps, 1)
                pool.wait_ge(rs_eps, i + 1)
                nc.gpsimd.tensor_tensor(rs[0:TT, k % 2, 1:2], rs[0:TT, k % 2, 0:1], g["mhalf"][0:TT, :],
                                        ALU.pow).then_inc(rs_done, 1)

            def affine(i, k):
                pool.wait_ge(nrm_done, i + 1)
                nc.gpsimd.tensor_tensor(nrm[0:TT, k % 2, :], nrm[0:TT, k % 2, :], ln_w[0:TT, :], ALU.mult)\
                    .then_inc(scaled, 1)
                pool.wait_ge(scaled, i + 1)
                nc.gpsimd.tensor_tensor(nrm[0:TT, k % 2, :], nrm[0:TT, k % 2, :], ln_b[0:TT, :], ALU.add)\
                    .then_inc(biased, 1)
                pool.wait_ge(biased, i + 1)
                through(pool, i, passed)
                nc.gpsimd.tensor_tensor(h[0:TT, i, :], h[0:TT, i, :], nrm[0:TT, k % 2, :], ALU.add)\
                    .then_inc(h_done, 1)
            run(pool, NT, U, [(0, stationary), (1, spread), (3, inverse_rms), (5, inverse_deviation), (6, affine)])

        @block.tensor
        def _(pe):
            pe.wait_ge(weights_in, ALL)
            pe.wait_ge(wout_done, 1)

            def heads(i, k):
                pe.wait_ge(W_done, i * 2 + 2)
                pe.wait_ge(xdt_done, i + 1)
                reused(pe, y_summed, i, 1)
                for hd in range(MH):
                    mm = nc.tensor.matmul(psY[0:TT, hd * 64:(hd + 1) * 64], W[0:TT, k % 2, hd, :],
                                          xdt[0:TT, k % 2, hd * 64:(hd + 1) * 64], start=True, stop=True)
                mm.then_inc(y_filled, 1)

            def project(i, k):
                pe.wait_ge(xs_done, i + 1)
                for u in range(NU):
                    if u == 0:
                        reused(pe, raw_kept, i, 1, NU, 0)
                    elif u == 1:
                        reused(pe, zs_done, i, 2)
                    else:
                        pe.wait_ge(raw_kept, i * NU + 1)
                    for half in range(2):
                        ch = 2 * u + half
                        for kc in range(KD):
                            mm = nc.tensor.matmul(psC[:, u % 2, half * TT:(half + 1) * TT],
                                                  wx[:, kc, ch * 128:(ch + 1) * 128], xs[:, k % 2, kc, :],
                                                  start=kc == 0, stop=kc == KD - 1)
                    mm.then_inc(xbc_filled, 1)

            def turn_y1(i, k):
                pe.wait_ge(y1_done, i + 1)
                for ch in range(KD):
                    mm = nc.tensor.transpose(psR[:, ch * TT:(ch + 1) * TT],
                                             y1[0:TT, k % 2, ch * 128:(ch + 1) * 128], ident[0:TT, 0:TT])
                mm.then_inc(y1T_filled, 1)

            def gates(i, k):
                pe.wait_ge(raw_kept, NT * NU if isinstance(i, int) and i == NT - 1 else (i + 1) * NU + 2)
                for kc in range(KD):
                    mm = nc.tensor.matmul(psC[0:TT, 1, :], xs[:, k % 2, kc, :], wz[:, kc, :],
                                          start=kc == 0, stop=kc == KD - 1)
                mm.then_inc(z_filled, 1)

            def turn_x(i, k):
                pe.wait_ge(xbc_done, i + 1)
                reused(pe, xD_done, i, 1)
                for ch in range(KY):
                    mm = nc.tensor.transpose(psX[0:TT, ch * 128:(ch + 1) * 128], xbc[:, k % 2, ch, :], ident[:, :])
                mm.then_inc(x_filled, 1)
                reused(pe, G_done, i, 1)
                nc.tensor.matmul(psG[0:TT, 0:TT], xbc[:, k % 2, KY, :], xbc[:, k % 2, KY + 1, :],
                                 start=True, stop=True).then_inc(G_filled, 1)

            def turn_y(i, k):
                pe.wait_ge(y_gated, i + 1)
                reused(pe, y1T_kept, i, 1)
                for ch in range(KY):
                    mm = nc.tensor.transpose(psR[:, ch * TT:(ch + 1) * TT],
                                             y[0:TT, k % 2, ch * 128:(ch + 1) * 128], ident[0:TT, 0:TT])
                mm.then_inc(yT_filled, 1)

            def sums(i, k):
                pe.wait_ge(R_done, i + 1)
                for hf in range(2):
                    if not (isinstance(i, int) and i * 2 + hf < 1):
                        pe.wait_ge(seg_exp, i * 2 + hf)
                    nc.tensor.matmul(psS[0:TT, 0:HH * TT], after[0:TT, :],
                                     R[0:TT, k % 2, hf * HH:(hf + 1) * HH, :], start=True, stop=True)\
                        .then_inc(seg_filled, 1)

            def linear_unit(i, k):
                pe.wait_ge(y1T_kept, i + 1)
                reused(pe, glu_biased, i, 1)
                for kc in range(KD):
                    mm = nc.tensor.matmul(psU[0:TT, :], y1T[:, k % 2, kc, :], wglu[:, kc, :],
                                          start=kc == 0, stop=kc == KD - 1)
                mm.then_inc(glu_filled, 1)

            def output(i, k):
                pe.wait_ge(yT_kept, i + 1)
                for ch in range(KY):
                    mm = nc.tensor.matmul(psR[0:TT, 0:D], yT[:, k % 2, ch, :], wout[:, ch, :],
                                          start=ch == 0, stop=ch == KY - 1)
                mm.then_inc(out_filled, 1)
            run(pe, NT, U, [(3, heads), (0, project), (5, turn_y1), (1, gates), (2, turn_x), (4, turn_y), (2, sums),
                            (5, linear_unit), (4, output)])

        @block.scalar
        def _(act):
            act.wait_ge(raw_zeroed, 1)

            def keep_raw(i, k):
                reused(act, conv_tap, i, 2, 4, 0)
                for u in range(NU):
                    act.wait_ge(xbc_filled, i * NU + u + 1)
                    for half in range(2):
                        ins = nc.scalar.activation(
                            raw[:, k % 2, 2 * u + half, :, PAD:],
                            psC[:, u % 2, half * TT:(half + 1) * TT].rearrange("p (b t) -> p b t", b=PER), ACT.Copy)
                    ins.then_inc(raw_kept, 1)

            def keep_y1T(i, k):
                act.wait_ge(y1T_filled, i + 1)
                reused(act, glu_filled, i, 2)
                nc.scalar.activation(y1T[:, k % 2, :, :], psR[:, 0:UN].rearrange("p (c t) -> p c t", c=KD),
                                     ACT.Copy).then_inc(y1T_kept, 1)

            def activate(i, k):
                act.wait_ge(conv_tap, i * 4 + 4)
                reused(act, G_filled, i, 2)
                nc.scalar.activation(xbc[:, k % 2, :, :], acc[:, k % 2, :, :], ACT.Silu).then_inc(xbc_done, 1)

            def gate(i, k):
                reused(act, y_gated, i, 2)
                act.wait_ge(z_filled, i + 1)
                nc.scalar.activation(zs[0:TT, k % 2, :], psC[0:TT, 1, :], ACT.Silu).then_inc(zs_done, 1)

            def keep_yT(i, k):
                act.wait_ge(yT_filled, i + 1)
                reused(act, out_filled, i, 2)
                nc.scalar.activation(yT[:, k % 2, :, :], psR[:, 0:KY * TT].rearrange("p (c t) -> p c t", c=KY),
                                     ACT.Copy).then_inc(yT_kept, 1)

            def decay(i, k):
                reused(act, y_filled, i, 2)
                for hf in range(2):
                    act.wait_ge(seg_filled, i * 2 + hf + 1)
                    nc.scalar.activation(W[0:TT, k % 2, hf * HH:(hf + 1) * HH, :],
                                         psS[0:TT, 0:HH * TT].rearrange("p (j t) -> p j t", j=HH), ACT.Exp)\
                        .then_inc(seg_exp, 1)

            def half_gate(i, k):
                act.wait_ge(glu_biased, i + 1)
                reused(act, gated, i, 2)
                nc.scalar.activation(th[0:TT, k % 2, :], glu[0:TT, k % 2, D:], ACT.Tanh, scale=0.5)\
                    .then_inc(tanh_done, 1)
            run(act, NT, U, [(0, keep_raw), (5, keep_y1T), (1, activate), (1, gate), (4, keep_yT), (2, decay),
                             (5, half_gate)])

        @block.vector
        def _(dve):
            nc.vector.memset(raw[:, :, :, :, :], 0.0).then_inc(raw_zeroed, 1)
            dve.wait_ge(weights_in, ALL)
            nc.vector.tensor_tensor(wout[:, :, :], wout[:, :, :], out_w[:, :].unsqueeze(2).broadcast_to([128, KY, D]),
                                    ALU.mult).then_inc(wout_done, 1)

            def heads(i, k):
                v = y[0:TT, k % 2, :]
                dve.wait_ge(y_filled, i + 1)
                dve.wait_ge(xD_done, i + 1)
                reused(dve, yT_filled, i, 2)
                nc.vector.tensor_tensor(v, psY[0:TT, :], xD[0:TT, k % 2, :], ALU.add).then_inc(y_summed, 1)
                dve.wait_ge(y_summed, i + 1)
                dve.wait_ge(zs_done, i + 1)
                nc.vector.tensor_tensor(v, v, zs[0:TT, k % 2, :], ALU.mult).then_inc(y_gated, 1)
                dve.wait_ge(y_gated, i + 1)
                reused(dve, y1_done, i, 2)
                nc.vector.scalar_tensor_tensor(out=junk[0:TT, :], in0=v, scalar=1.0 / DI, in1=v, op0=ALU.mult,
                                               op1=ALU.mult, accum_out=ms[0:TT, k % 2, 0:1]).then_inc(y_squared, 1)

            def convolve(i, k):
                dve.wait_ge(raw_kept, i * NU + NU)
                reused(dve, xbc_done, i, 2)
                for tap in range(4):
                    if tap:
                        dve.wait_ge(conv_tap, i * 4 + tap)
                    for ch in range(KC):
                        src = raw[:, k % 2, ch, :, tap:tap + TOK]
                        dst = acc[:, k % 2, ch, :].rearrange("p (b t) -> p b t", b=PER)
                        if tap == 0:
                            ins = nc.vector.tensor_scalar(dst, src, conv_w[:, ch, 0:1], conv_b[:, ch:ch + 1],
                                                          ALU.mult, ALU.add)
                        else:
                            ins = nc.vector.scalar_tensor_tensor(out=dst, in0=src, scalar=conv_w[:, ch, tap:tap + 1],
                                                                 in1=dst, op0=ALU.mult, op1=ALU.add)
                    ins.then_inc(conv_tap, 1)

            def inputs(i, k):
                xv = psX[0:TT, :].rearrange("s (j d) -> s j d", j=MH)
                wide = [TT, MH, 64]
                dve.wait_ge(x_filled, i + 1)
                reused(dve, y_filled, i, 2)
                nc.vector.tensor_tensor(xdt[0:TT, k % 2, :].rearrange("s (j d) -> s j d", j=MH), xv,
                                        dt[0:TT, i, :].unsqueeze(2).broadcast_to(wide), ALU.mult).then_inc(xdt_done, 1)
                reused(dve, y_summed, i, 2)
                nc.vector.tensor_tensor(xD[0:TT, k % 2, :].rearrange("s (j d) -> s j d", j=MH), xv,
                                        skip[0:TT, :].unsqueeze(2).broadcast_to(wide), ALU.mult).then_inc(xD_done, 1)
                dve.wait_ge(G_filled, i + 1)
                nc.vector.tensor_tensor(G[0:TT, k % 2, :], psG[0:TT, 0:TT], causal[0:TT, :], ALU.mult)\
                    .then_inc(G_done, 1)

            def decayed(i, k):
                dve.wait_ge(G_done, i + 1)
                for hf in range(2):
                    dve.wait_ge(seg_exp, i * 2 + hf + 1)
                    w = W[0:TT, k % 2, hf * HH:(hf + 1) * HH, :]
                    nc.vector.tensor_tensor(w, w, G[0:TT, k % 2, :].unsqueeze(1).broadcast_to([TT, HH, TT]), ALU.mult)\
                        .then_inc(W_done, 1)

            def residual(i, k):
                dve.wait_ge(out_filled, i + 1)
                dve.wait_ge(ms_done, i + 1)
                reused(dve, y2_done, i, 2)
                nc.vector.scalar_tensor_tensor(out=y1[0:TT, k % 2, :], in0=psR[0:TT, 0:D],
                                               scalar=ms[0:TT, k % 2, 2:3], in1=xn[0:TT, i, :],
                                               op0=ALU.mult, op1=ALU.add).then_inc(y1_done, 1)

            def linear_unit(i, k):
                dve.wait_ge(glu_filled, i + 1)
                reused(dve, gated, i, 2)
                nc.vector.tensor_tensor(glu[0:TT, k % 2, :], psU[0:TT, :], glu_b[0:TT, :], ALU.add)\
                    .then_inc(glu_biased, 1)
                dve.wait_ge(tanh_done, i + 1)
                nc.vector.scalar_tensor_tensor(out=th[0:TT, k % 2, :], in0=th[0:TT, k % 2, :], scalar=1.0,
                                               in1=glu[0:TT, k % 2, 0:D], op0=ALU.add, op1=ALU.mult).then_inc(gated, 1)
                dve.wait_ge(gated, i + 1)
                dve.wait_ge(y1_done, i + 1)
                reused(dve, nrm_done, i, 2)
                nc.vector.scalar_tensor_tensor(out=y2[0:TT, k % 2, :], in0=th[0:TT, k % 2, :], scalar=0.5,
                                               in1=y1[0:TT, k % 2, :], op0=ALU.mult, op1=ALU.add).then_inc(y2_done, 1)
                dve.wait_ge(y2_done, i + 1)
                nc.vector.bn_stats(st[0:TT, k % 2, :], y2[0:TT, k % 2, :]).then_inc(st_done, 1)
                dve.wait_ge(st_done, i + 1)
                through(dve, i, g["passed"])
                nc.vector.bn_aggr(mv[0:TT, k % 2, :], st[0:TT, k % 2, :]).then_inc(mv_done, 1)

            def normalise(i, k):
                dve.wait_ge(rs_done, i + 1)
                reused(dve, h_done, i, 2)
                nc.vector.tensor_scalar(nrm[0:TT, k % 2, :], y2[0:TT, k % 2, :], mv[0:TT, k % 2, 0:1],
                                        rs[0:TT, k % 2, 1:2], ALU.subtract, ALU.mult).then_inc(nrm_done, 1)
            run(dve, NT, U, [(3, heads), (0, convolve), (2, inputs), (2, decayed), (6, normalise), (5, linear_unit),
                             (4, residual)])


def experts(g, weight, name, keys):
    nc, a, sb, pb, sem, h, xT, ident = (g[k] for k in ("nc", "a", "sb", "pb", "sem", "h", "xT", "ident"))
    NP = NT // 2
    assert NP % 2 and E % 2 == 0
    W1, b1, W2, b2 = (a[k] for k in keys)
    with ExitStack() as c:
        w1 = sb(name + "_w1", [128, 2, KD, F], c=c)
        w2 = sb(name + "_w2", [128, 2, KF, D], c=c)
        bias1 = sb(name + "_bias1", [128, E, KF], c=c)
        bias2 = sb(name + "_bias2", [E, D], c=c)
        wT = sb(name + "_wT", [E, 2, TT], c=c)
        wslot = sb(name + "_wslot", [128, 2, E], c=c)
        act1 = sb(name + "_act1", [128, 2, KF, 2 * TT], c=c)
        ps1 = pb(name + "_ps1", [128, 4, 512], c=c)
        ps2 = pb(name + "_ps2", [128, 2, 512], c=c)
        psW = pb(name + "_psW", [128, 2, 512], c=c)
        bias_in = sem(name + "_bias_in", c)
        wslot_done = sem(name + "_wslot_done", c)
        w1_in = [sem(f"{name}_w1_in{s}", c) for s in range(2)]
        w2_in = [sem(f"{name}_w2_in{s}", c) for s in range(2)]
        wT_filled = sem(name + "_wT_filled", c)
        wT_kept = sem(name + "_wT_kept", c)
        b2_filled = sem(name + "_b2_filled", c)
        b2_added = sem(name + "_b2_added", c)
        filled1 = sem(name + "_filled1", c)
        kept1 = sem(name + "_kept1", c)
        filled2 = sem(name + "_filled2", c)
        added = sem(name + "_added", c)
        block = c.enter_context(nc.Block())

        def steps(eng, up, down):
            def expert(e, slot, first):
                def at(pair, k):
                    return e * NP + pair, (slot * NP + k) % 2
                s, par = at(0, 0)
                if up:
                    up(e, slot, 0, s, par)
                if down and not first:
                    down(e - 1, 1 - slot, NP - 1, s - 1, 1 - par)
                for pair in (1, 2) if first else ():
                    s, par = at(pair, pair)
                    if up:
                        up(e, slot, pair, s, par)
                    if down:
                        down(e, slot, pair - 1, s - 1, 1 - par)
                with eng.Fori(3 if first else 1, NP - 1, 2) as p0:
                    for k in range(2):
                        s, par = at(p0 + k, 1 + k)
                        if up:
                            up(e, slot, p0 + k, s, par)
                        if down:
                            down(e, slot, p0 + k - 1, s - 1, 1 - par)
            expert(0, 0, True)
            expert(1, 1, False)
            with eng.Fori(2, E - 1, 2) as e0:
                expert(e0, 0, False)
                expert(e0 + 1, 1, False)
            if down:
                down(E - 1, (E - 1) % 2, NP - 1, E * NP - 1, (E * NP - 1) % 2)

        @block.sync
        def _(sp):
            sp.dma_start(bias1[:, :, :], b1).then_inc(bias_in, 16)
            sp.dma_start(bias2[:, :], b2).then_inc(bias_in, 16)

            def load(e, slot):
                if not isinstance(e, int):
                    sp.wait_ge(filled2, (e - 1) * (2 * NP))
                sp.dma_start(w1[:, slot, :, :], W1[e].rearrange("(c p) f -> p c f", p=128)).then_inc(w1_in[slot], 16)
                sp.dma_start(w2[:, slot, :, :], W2[e].rearrange("(c p) d -> p c d", p=128)).then_inc(w2_in[slot], 16)
            load(0, 0)
            load(1, 1)
            with sp.Fori(2, E - 1, 2) as e0:
                load(e0, 0)
                load(e0 + 1, 1)

        @block.tensor
        def _(pe):
            pe.wait_ge(bias_in, 32)

            def turn(i, k):
                pe.wait_ge(wslot_done, i + 1)
                reused(pe, wT_kept, i, 2)
                nc.tensor.matmul(psW[0:E, k % 2, 0:TT], wslot[0:TT, k % 2, :], ident[0:TT, 0:TT], start=True, stop=True)\
                    .then_inc(wT_filled, 1)

            def bias(i, k):
                pe.wait_ge(wT_kept, i + 1)
                reused(pe, b2_added, i, 2)
                nc.tensor.matmul(ps2[0:TT, k % 2, 0:D], wT[:, k % 2, :], bias2[:, :], start=True, stop=True)\
                    .then_inc(b2_filled, 1)

            run(pe, NT, 2, [(0, turn), (1, bias)])
            pe.wait_ge(b2_added, NT)

            def up(e, slot, pair, s, par):
                if isinstance(e, int):
                    pe.wait_ge(w1_in[slot], 16)
                else:
                    pe.wait_ge(w1_in[slot], (e - slot) * 8 + 16)
                for u in range(4):
                    reused(pe, kept1, s, 1, 4, u - 3)
                    for half in range(2):
                        f = 2 * u + half
                        for kc in range(KD):
                            mm = nc.tensor.matmul(ps1[:, u, half * 2 * TT:(half + 1) * 2 * TT],
                                                  w1[:, slot, kc, f * 128:(f + 1) * 128],
                                                  xT[:, kc, cols(pair * 2, 2)], start=kc == 0, stop=kc == KD - 1)
                    mm.then_inc(filled1, 1)

            def down(e, slot, pair, s, par):
                if isinstance(e, int):
                    pe.wait_ge(w2_in[slot], 16)
                else:
                    pe.wait_ge(w2_in[slot], (e - slot) * 8 + 16)
                pe.wait_ge(kept1, s * 4 + 4)
                for j in range(2):
                    reused(pe, added, s, 1, 2, j - 1)
                    for f in range(KF):
                        mm = nc.tensor.matmul(ps2[0:TT, j, 0:D], act1[:, par, f, j * TT:(j + 1) * TT],
                                              w2[:, slot, f, :], start=f == 0, stop=f == KF - 1)
                    mm.then_inc(filled2, 1)
            steps(pe, up, down)

        @block.scalar
        def _(act):
            act.wait_ge(bias_in, 32)

            def keep_wT(i, k):
                act.wait_ge(wT_filled, i + 1)
                reused(act, b2_filled, i, 2)
                nc.scalar.activation(wT[:, k % 2, :], psW[0:E, k % 2, 0:TT], ACT.Copy).then_inc(wT_kept, 1)
            run(act, NT, 2, [(0, keep_wT)])

            def up(e, slot, pair, s, par):
                if not (isinstance(s, int) and s < 2):
                    act.wait_ge(filled2, s * 2 - 2)
                for u in range(4):
                    act.wait_ge(filled1, s * 4 + u + 1)
                    for half in range(2):
                        f = 2 * u + half
                        through(act, e, g["passed"])
                        ins = nc.scalar.activation(act1[:, par, f, :], ps1[:, u, half * 2 * TT:(half + 1) * 2 * TT],
                                                   ACT.Silu, bias=bias1[:, e, f:f + 1])
                    ins.then_inc(kept1, 1)
            steps(act, up, None)

        @block.vector
        def _(dve):
            def place(i, k):
                reused(dve, wT_filled, i, 2)
                nc.vector.tensor_scalar(wslot[0:TT, k % 2, :], weight[0:TT, i, :], 0.0, None, ALU.add)\
                    .then_inc(wslot_done, 1)

            def add_bias(i, k):
                dve.wait_ge(b2_filled, i + 1)
                nc.vector.tensor_tensor(h[0:TT, i, :], h[0:TT, i, :], ps2[0:TT, k % 2, 0:D], ALU.add)\
                    .then_inc(b2_added, 1)
            run(dve, NT, 2, [(0, place), (1, add_bias)])

            def down(e, slot, pair, s, par):
                for j in range(2):
                    dve.wait_ge(filled2, s * 2 + j + 1)
                    nc.vector.scalar_tensor_tensor(
                        out=h[0:TT, pair * 2 + j, :], in0=ps2[0:TT, j, 0:D],
                        scalar=weight[0:TT, pair * 2 + j, e:e + 1] if isinstance(e, int)
                        else weight[0:TT, pair * 2 + j, bass.ds(e, 1)],
                        in1=h[0:TT, pair * 2 + j, :], op0=ALU.mult, op1=ALU.add).then_inc(added, 1)
            steps(dve, None, down)


def store(g, out):
    nc, h, sem = g["nc"], g["h"], g["sem"]
    with ExitStack() as c:
        stored = sem("stored", c)
        block = c.enter_context(nc.Block())
        flat = out.rearrange("b t d -> (b t) d")
        whole = IMAGES * TOK // TT
        rest = IMAGES * TOK - whole * TT

        @block.sync
        def _(sp):
            sp.dma_start(flat[0:whole * TT, :].rearrange("(n p) d -> p n d", p=TT), h[0:TT, 0:whole, :])\
                .then_inc(stored, 16)
            sp.dma_start(flat[whole * TT:, :], h[0:rest, whole, :]).then_inc(stored, 16)
            sp.wait_ge(stored, 32)


def host_arrays(v):
    x = np.asarray(v["x"])
    side = 6
    p = x.reshape(IMAGES, 3, side, 16, side, 16).transpose(1, 3, 5, 0, 2, 4).reshape(PATCH, IMAGES, side * side)
    pt = np.zeros((PATCH, NT * PER, TOK), x.dtype)
    pt[:, :IMAGES, 1:] = p
    pt = pt.reshape(KP, 128, NT, TT).transpose(1, 2, 0, 3)
    rows = np.asarray(v["L0_tok_b"])[None].repeat(TOK, 0)
    rows[0] = np.asarray(v["L0_tok_cls_token"])[0, 0]

    def bc(name):
        return np.asarray(v[name]).reshape(1, -1).repeat(TT, 0)

    tok = np.arange(TT)
    same = tok[:, None] // TOK == tok[None] // TOK
    mask = np.where(same & (tok[None] <= tok[:, None]), 0.0, MASKED).astype(np.float32)
    a = {
        "patchesT": pt,
        "tok_WT": np.asarray(v["L0_tok_W"]).T,
        "cls_or_b": np.tile(rows, (PER, 1)),
        "pos": np.tile(np.asarray(v["L0_tok_pos_embedding"])[0], (PER, 1)),
        "ident": np.eye(128, dtype=np.float32),
        "mask4": np.tile(mask, (1, 4)),
        "bo": bc("L0_attn_bo"),
        "ffn_rms_w": bc("L0_ffn_rms_w"),
        "gate_wT": np.asarray(v["L0_ffn_gate_w"]).T,
        "number_less_e": np.tile(np.arange(E, dtype=np.float32) - E, (TT, 1)),
        "W1_0": np.asarray(v["L0_ffn_W1"]), "W2_0": np.asarray(v["L0_ffn_W2"]), "b2_0": np.asarray(v["L0_ffn_b2"]),
        "b1_0": np.asarray(v["L0_ffn_b1"]).reshape(E, KF, 128).transpose(2, 0, 1),
        "W1_1": np.asarray(v["L1_ffn_we1"]), "W2_1": np.asarray(v["L1_ffn_we2"]), "b2_1": np.asarray(v["L1_ffn_be2"]),
        "b1_1": np.asarray(v["L1_ffn_be1"]).reshape(E, KF, 128).transpose(2, 0, 1),
        "W_in": np.asarray(v["L1_attn_W_in"]), "W_out": np.asarray(v["L1_attn_W_out"]),
        "glu_w": np.asarray(v["L1_attn_glu_w"]), "glu_b": bc("L1_attn_glu_b"),
        "conv_w": np.asarray(v["L1_attn_conv_w"]).reshape(KC, 128, 4).transpose(1, 0, 2),
        "conv_b": np.asarray(v["L1_attn_conv_b"]).reshape(KC, 128).T,
        "m_rms_w": np.asarray(v["L1_attn_rms_w"]).reshape(DI // 128, 128).T,
        "D_skip": bc("L1_attn_D_skip"), "dt_bias": bc("L1_attn_dt_bias"), "A_log": bc("L1_attn_A_log"),
        "ln_w": bc("L1_attn_ln_w"), "ln_b": bc("L1_attn_ln_b"),
        "after": (tok[:, None] > tok[None]).astype(np.float32),
        "upto": (tok[:, None] <= tok[None]).astype(np.float32),
        "causal": (same & (tok[:, None] <= tok[None])).astype(np.float32),
        "rw1": np.asarray(v["L1_ffn_rw1"]), "rw2": np.asarray(v["L1_ffn_rw2"]), "rb2": bc("L1_ffn_rb2"),
        "rb1": np.asarray(v["L1_ffn_rb1"]).reshape(KD, 128).T,
    }
    for w in ("Wq", "Wk", "Wv", "Wo"):
        a[w] = np.asarray(v["L0_attn_" + w])
    return a



def kernel(**inputs):
    import concourse.bacc as _bacc
    from concourse.bass_utils import run_bass_kernel_spmd as _run

    nc = _bacc.Bacc("TRN2", target_bir_lowering=False, num_devices=1)
    arrays, args = {}, {}
    for name, arr in host_arrays(inputs).items():
        arr = np.ascontiguousarray(arr)
        arrays[f"in_{name}"] = arr
        args[name] = nc.dram_tensor(f"in_{name}", arr.shape, mybir.dt.from_np(arr.dtype), kind="ExternalInput").ap()
    out = nc.dram_tensor("out_0", (IMAGES, TOK, D), F32, kind="ExternalOutput").ap()
    build(nc, args, out)
    r = _run(nc, [arrays], core_ids=[0])
    return r.results[0]["out_0"]
```

```python
from contextlib import ExitStack

import numpy as np
import concourse.bass as bass
from concourse import mybir

ALU = mybir.AluOpType
ACT = mybir.ActivationFunctionType
AX = mybir.AxisListType
F32 = mybir.dt.float32
BF16 = mybir.dt.bfloat16

IMAGES, TOK, D = 64, 37, 256
PER = 3
TT = PER * TOK
NT = -(-IMAGES // PER)
NTOK = NT * TT
KD = D // 128
PATCH = 3 * 16 * 16
KP = PATCH // 128
HEADS, HD = 16, 64
INNER = HEADS * HD
KI = INNER // 128
E = 8
F = 1024
KF = F // 128
DI, DS, MH = 512, 128, 8
CONV = DI + 2 * DS
KC = CONV // 128
BLOCK = 128
SUB = BLOCK // 128
MASKED = -8.0e9


def run(eng, n, unroll, stages):
    longest = max(lag for lag, _ in stages)
    head = longest + unroll
    while head < n and (n - head) % unroll:
        head += 1

    def step(t, phase):
        for lag, fn in stages:
            if not isinstance(t, int) or 0 <= t - lag < n:
                fn(t - lag, (phase - lag) % unroll)

    for t in range(min(head, n)):
        step(t, t)
    if head < n:
        with eng.Fori(head, n - unroll + 1, unroll) as t0:
            for k in range(unroll):
                step(t0 + k, head + k)
    for t in range(n, n + longest):
        step(t, t)


def reused(eng, sem, i, depth, per=1, extra=0):
    if isinstance(i, int) and i < depth:
        return
    eng.wait_ge(sem, (i - depth + 1) * per + extra)


def through(eng, i, passed):
    if not isinstance(i, int):
        eng.sem_inc(passed, 1)


def build(nc, a, out):
    with ExitStack() as ctx:
        def sb(name, shape, dt=F32, c=ctx):
            return c.enter_context(nc.sbuf_tensor(name, shape, dt))

        def pb(name, shape, dt=F32, c=ctx):
            return c.enter_context(nc.psum_tensor(name, shape, dt))

        phases = {}

        def clear(sems):
            nc.clear_and_free_semaphores(sems)
            nc.all_engine_barrier()

        def sem(name, c=None):
            if c is None:
                return ctx.enter_context(nc.semaphore(name))
            if id(c) not in phases:
                phases[id(c)] = []
                c.callback(lambda: clear(phases.pop(id(c))))
            phases[id(c)].append(nc.alloc_semaphore(name))
            return phases[id(c)][-1]

        h = sb("h", [128, NT, D])
        xT = sb("xT", [128, KD, NTOK])
        ident = sb("ident", [128, 128])
        identb = sb("identb", [128, 128], BF16)
        mhalf = sb("mhalf", [128, 1])
        epsilon = sb("epsilon", [128, 2])
        loaded = sem("loaded")
        slots_zeroed = sem("slots_zeroed")
        passed = sem("passed")
        g = dict(nc=nc, a=a, sb=sb, pb=pb, sem=sem, h=h, xT=xT, ident=ident, identb=identb, mhalf=mhalf, epsilon=epsilon,
                 passed=passed, loaded=loaded, slots_zeroed=slots_zeroed)
        sparse = [Sparse(g, "ffn0", 1, "0"), Sparse(g, "ffn1", 2, "1")]
        embed(g, sparse)
        attention(g)
        with ExitStack() as c:
            ffn = sparse[0]
            ffn.allocate(c)
            route_top1(g, ffn)
            ffn.place(g)
            ffn.experts(g)
        mamba(g)
        with ExitStack() as c:
            ffn = sparse[1]
            ffn.allocate(c)
            route_top2(g, ffn)
            ffn.place(g)
            ffn.experts(g)
        store(g, out)


class LayerNorm:

    def __init__(self, g, c, name, slots=False):
        self.g = g
        self.eps = 0
        sb, pb, sem = g["sb"], g["pb"], g["sem"]
        self.stats = sb(name + "_stats", [128, 2, 6], c=c)
        self.mv = sb(name + "_mv", [128, 4, 2], c=c)
        self.rstd = sb(name + "_rstd", [128, 4, 2], c=c)
        self.xn = sb(name + "_xn", [128, 2, D], c=c)
        self.psT = pb(name + "_psT", [128, 2, 512], c=c)
        self.stats_done = sem(name + "_stats_done", c)
        self.mv_done = sem(name + "_mv_done", c)
        self.rstd_done = sem(name + "_rstd_done", c)
        self.xn_done = sem(name + "_xn_done", c)
        self.turned = sem(name + "_turned", c)
        self.kept = sem(name + "_kept", c)
        if slots:
            self.xs = sb(name + "_xs", [128, 2, KD, TT], c=c)
            self.xs_kept = sem(name + "_xs_kept", c)

    def statistics(self, dve, i, k, h_ready=None):
        nc, h = self.g["nc"], self.g["h"]
        if h_ready is not None:
            dve.wait_ge(h_ready, i + 1)
        through(dve, i, self.g["passed"])
        nc.vector.bn_stats(self.stats[0:TT, k % 2, :], h[0:TT, i, :]).then_inc(self.stats_done, 1)
        dve.wait_ge(self.stats_done, i + 1)
        reused(dve, self.xn_done, i, 2)
        through(dve, i, self.g["passed"])
        nc.vector.bn_aggr(self.mv[0:TT, k % 2, :], self.stats[0:TT, k % 2, :]).then_inc(self.mv_done, 1)

    def inverse(self, pool, i, k):
        nc = self.g["nc"]
        pool.wait_ge(self.mv_done, i + 1)
        reused(pool, self.xn_done, i, 2)
        nc.gpsimd.tensor_tensor(self.rstd[0:TT, k % 2, 0:1], self.mv[0:TT, k % 2, 1:2],
                                self.g["epsilon"][0:TT, self.eps:self.eps + 1], ALU.add).then_inc(self.rstd_done, 1)
        pool.wait_ge(self.rstd_done, i * 2 + 1)
        nc.gpsimd.tensor_tensor(self.rstd[0:TT, k % 2, 1:2], self.rstd[0:TT, k % 2, 0:1],
                                self.g["mhalf"][0:TT, :], ALU.pow).then_inc(self.rstd_done, 1)

    def normalise(self, dve, i, k, dst=None):
        nc, h = self.g["nc"], self.g["h"]
        dve.wait_ge(self.rstd_done, i * 2 + 2)
        dve.wait_ge(self.mv_done, i + 1)
        reused(dve, self.turned, i, 2)
        o = self.xn[0:TT, k % 2, :] if dst is None else dst
        nc.vector.tensor_scalar(o, h[0:TT, i, :], self.mv[0:TT, k % 2, 0:1], self.rstd[0:TT, k % 2, 1:2],
                                ALU.subtract, ALU.mult).then_inc(self.xn_done, 1)

    def turn(self, pe, i, k, ready=None, src=None):
        nc = self.g["nc"]
        pe.wait_ge(ready or self.xn_done, i + 1)
        reused(pe, self.kept, i, 2)
        src = self.xn[0:TT, k % 2, :] if src is None else src
        for c in range(KD):
            mm = nc.tensor.transpose(self.psT[:, k % 2, c * TT:(c + 1) * TT], src[:, c * 128:(c + 1) * 128],
                                     self.g["ident"][0:TT, 0:TT])
        mm.then_inc(self.turned, 1)

    def keep(self, act, i, k):
        nc, xT = self.g["nc"], self.g["xT"]
        act.wait_ge(self.turned, i + 1)
        through(act, i, self.g["passed"])
        nc.scalar.activation(xT[:, :, cols(i)], self.psT[:, k % 2, 0:KD * TT].rearrange("p (c t) -> p c t", c=KD),
                             ACT.Copy).then_inc(self.kept, 1)


    def keep_stationary(self, act, i, k, used, last=False):
        act.wait_ge(self.turned, i + 1)
        reused(act, used, i, 2)
        self.g["nc"].scalar.activation(self.xs[:, k % 2, :, :],
                                       self.psT[:, k % 2, 0:KD * TT].rearrange("p (c t) -> p c t", c=KD),
                                       ACT.Copy).then_inc(self.kept if last else self.xs_kept, 1)


def cols(i, n=1):
    return slice(i * TT, i * TT + n * TT) if isinstance(i, int) else bass.ds(i * TT, n * TT)


def embed(g, sparse):
    nc, a, sb, pb, sem, h, ident = (g[k] for k in ("nc", "a", "sb", "pb", "sem", "h", "ident"))
    loaded = g["loaded"]
    with ExitStack() as c:
        NP = 4
        wT = sb("tok_wT", [128, KP, D], c=c)
        patches = sb("patches", [128, NP, KP, TT], c=c)
        base = sb("base", [128, D], c=c)
        pos = sb("pos", [128, D], c=c)
        psE = pb("psE", [128, 2, 512], c=c)
        patches_in = [sem(f"patches_in{s}", c) for s in range(NP)]
        mhalf_set = sem("mhalf_set", c)
        base_done = sem("base_done", c)
        zero = sb("zero", [128, SUB, D], c=c)
        embedded = sem("embedded", c)
        h_done = sem("h_done", c)
        ln = LayerNorm(g, c, "ln0")
        block = c.enter_context(nc.Block())

        @block.sync
        def _(sp):
            sp.dma_start(wT[:, :, :], a["tok_WT"].rearrange("(c p) d -> p c d", p=128)).then_inc(loaded, 16)
            sp.dma_start(base[0:TT, :], a["cls_or_b"]).then_inc(loaded, 16)
            sp.dma_start(pos[0:TT, :], a["pos"]).then_inc(loaded, 16)
            sp.dma_start(ident[:, :], a["ident"]).then_inc(loaded, 16)

            def load(i, k):
                reused(sp, embedded, i, NP)
                sp.dma_start(patches[:, k, :, :], a["patchesT"][:, i, :, :]).then_inc(patches_in[k], 16)
            run(sp, NT, NP, [(0, load)])
            sp.wait_ge(mhalf_set, 4)
            for ffn in sparse:
                for b in range(ffn.blocks):
                    sp.dma_start(ffn.x_slots[b * BLOCK:(b + 1) * BLOCK, :].rearrange("(j p) d -> p j d", p=128),
                                 zero[:, :, :]).then_inc(g["slots_zeroed"], 16)

        @block.tensor
        def _(pe):
            pe.wait_ge(loaded, 64)

            def project(i, k):
                pe.wait_ge(patches_in[k], (i - k) * (16 // NP) + 16)
                reused(pe, h_done, i, 2)
                for kc in range(KP):
                    mm = nc.tensor.matmul(psE[0:TT, k % 2, 0:D], patches[:, k, kc, :], wT[:, kc, :],
                                          start=kc == 0, stop=kc == KP - 1)
                mm.then_inc(embedded, 1)
            run(pe, NT, NP, [(0, project), (2, lambda i, k: ln.turn(pe, i, k))])

        @block.vector
        def _(dve):
            nc.vector.memset(g["mhalf"][:, :], -0.5).then_inc(mhalf_set, 1)
            nc.vector.memset(g["epsilon"][:, 0:1], 1e-5).then_inc(mhalf_set, 1)
            nc.vector.memset(g["epsilon"][:, 1:2], 1e-6).then_inc(mhalf_set, 1)
            nc.vector.memset(zero[:, :, :], 0.0).then_inc(mhalf_set, 1)
            dve.wait_ge(loaded, 64)
            nc.vector.tensor_tensor(base[0:TT, :], base[0:TT, :], pos[0:TT, :], ALU.add).then_inc(base_done, 1)
            dve.wait_ge(base_done, 1)
            nc.vector.tensor_copy(g["identb"][:, :], ident[:, :]).then_inc(base_done, 1)

            def add(i, k):
                dve.wait_ge(embedded, i + 1)
                nc.vector.tensor_tensor(h[0:TT, i, :], psE[0:TT, k % 2, 0:D], base[0:TT, :],
                                        ALU.add).then_inc(h_done, 1)
            run(dve, NT, NP, [(0, add), (0, lambda i, k: ln.statistics(dve, i, k, h_done)),
                              (1, lambda i, k: ln.normalise(dve, i, k))])

        @block.gpsimd
        def _(pool):
            pool.wait_ge(mhalf_set, 3)
            run(pool, NT, NP, [(0, lambda i, k: ln.inverse(pool, i, k))])

        @block.scalar
        def _(act):
            run(act, NT, NP, [(2, lambda i, k: ln.keep(act, i, k))])


def attention(g):
    nc, a, sb, pb, sem, h, xT, ident = (g[k] for k in ("nc", "a", "sb", "pb", "sem", "h", "xT", "ident"))
    identb = g["identb"]
    U = 4
    with ExitStack() as c:
        wqk = sb("wqk", [128, 2, KD, INNER], c=c)
        wv = sb("wv", [128, KD, INNER], c=c)
        wo = sb("wo", [128, KI, D], c=c)
        bo = sb("bo", [128, D], c=c)
        mask = sb("mask", [128, 4 * TT], BF16, c=c)
        mask_f32 = sb("mask_f32", [128, 4 * TT], c=c)
        xs = sb("xs", [128, 2, KD, TT], c=c)
        qk = sb("qk", [128, 2, 2 * KI, 2 * TT], c=c)
        v = sb("v", [128, U, INNER], c=c)
        s = sb("s", [128, 2, HEADS, TT], c=c)
        pT = sb("pT", [128, HEADS, TT], c=c)
        oT = sb("oT", [128, 2, KI, TT], c=c)
        top = sb("top", [128, 2, HEADS], c=c)
        total = sb("total", [128, 2, HEADS], c=c)
        inv = sb("inv", [128, 2, HEADS], c=c)
        psS = pb("psS", [128, 2, 2, 512], c=c)
        psP = pb("psP", [128, 2, 512], c=c)
        psT = pb("psT", [128, 512], c=c)
        psO = pb("psO", [128, 512], c=c)
        weights_in = sem("attn_weights_in", c)
        xs_done = sem("xs_done", c)
        mask_done = sem("mask_done", c)
        proj_filled = sem("proj_filled", c)
        proj_freed = sem("proj_freed", c)
        scores_done = sem("scores_done", c)
        top_done = sem("top_done", c)
        shifted = sem("shifted", c)
        exp_done = sem("exp_done", c)
        total_done = sem("total_done", c)
        inv_done = sem("inv_done", c)
        prob_done = sem("prob_done", c)
        pT_filled = sem("pT_filled", c)
        pT_kept = sem("pT_kept", c)
        oT_filled = sem("oT_filled", c)
        oT_kept = sem("oT_kept", c)
        wo_done = sem("wo_done", c)
        h_done = sem("attn_h_done", c)
        h_bias = sem("attn_h_bias", c)
        block = c.enter_context(nc.Block())
        NLOAD = 6 * 16

        def unit(t, k, n):
            return t * 6 + n if k % 2 == 0 else (t - 1) * 6 + 10 + n

        @block.sync
        def _(sp):
            for j, w in enumerate(("Wq", "Wk")):
                sp.dma_start(wqk[:, j, :, :], a[w].rearrange("(c p) n -> p c n", p=128)).then_inc(weights_in, 16)
            sp.dma_start(wv[:, :, :], a["Wv"].rearrange("(c p) n -> p c n", p=128)).then_inc(weights_in, 16)
            sp.dma_start(wo[:, :, :], a["Wo"].rearrange("(c p) n -> p c n", p=128)).then_inc(weights_in, 16)
            sp.dma_start(bo[0:TT, :], a["bo"]).then_inc(weights_in, 16)
            sp.dma_start(mask_f32[0:TT, :], a["mask4"]).then_inc(weights_in, 16)

        @block.gpsimd
        def _(pool):
            def stationary(i, k):
                if not (isinstance(i, int) and i < 2):
                    pool.wait_ge(proj_filled, unit(i - 2, k, 1) + 1)
                through(pool, i, g["passed"])
                nc.gpsimd.tensor_copy(xs[:, k % 2, :, :], xT[:, :, cols(i)]).then_inc(xs_done, 1)
            run(pool, NT, U, [(0, stationary)])

        @block.tensor
        def _(pe):
            pe.wait_ge(weights_in, NLOAD)
            pe.wait_ge(mask_done, 1)

            def free_unit(t, k, n):
                if not (isinstance(t, int) and unit(t, k, n) < 2):
                    pe.wait_ge(proj_freed, unit(t, k, n) - 1)

            def values(n):
                def fn(t, k):
                    if n == 0:
                        pe.wait_ge(xs_done, t + 1)
                    free_unit(t, k, n)
                    for kc in range(KD):
                        mm = nc.tensor.matmul(psP[0:TT, n % 2, :], xs[:, k % 2, kc, :],
                                              wv[:, kc, n * 512:(n + 1) * 512], start=kc == 0, stop=kc == KD - 1)
                    mm.then_inc(proj_filled, 1)
                return fn

            def queries_keys(t, k):
                if k % 2:
                    return
                for n in range(8):
                    free_unit(t, k, n + 2)
                    for half in range(2):
                        ch = 2 * n + half
                        for kc in range(KD):
                            mm = nc.tensor.matmul(psP[:, n % 2, half * 2 * TT:(half + 1) * 2 * TT],
                                                  wqk[:, ch // KI, kc, (ch % KI) * 128:(ch % KI + 1) * 128],
                                                  xT[:, kc, cols(t, 2)], start=kc == 0, stop=kc == KD - 1)
                    mm.then_inc(proj_filled, 1)

            def scores(hf):
                def fn(i, k):
                    base = i if k % 2 == 0 else i - 1
                    pe.wait_ge(proj_freed, base * 6 + 10)
                    reused(pe, shifted, i, 1, 2, hf - 1)
                    for p in range(2):
                        nc.tensor.matmul(psS[0:TT, hf, p, 0:4 * TT], identb[0:TT, 0:TT], mask[0:TT, :],
                                         start=True, stop=False)
                        for j in range(4):
                            ch = hf * 4 + j
                            q = qk[64 * p:64 * p + 64, (k // 2) % 2, ch, (k % 2) * TT:(k % 2 + 1) * TT]
                            kk = qk[64 * p:64 * p + 64, (k // 2) % 2, KI + ch, (k % 2) * TT:(k % 2 + 1) * TT]
                            mm = nc.tensor.matmul(psS[0:TT, hf, p, j * TT:(j + 1) * TT], q, kk,
                                                  start=False, stop=j == 3)
                    mm.then_inc(scores_done, 1)
                return fn

            def turn(q):
                def fn(i, k):
                    pe.wait_ge(prob_done, i * 2 + q // 2 + 1)
                    if q or not isinstance(i, int) or i:
                        pe.wait_ge(pT_kept, i * 4 + q)
                    for j in range(4):
                        mm = nc.tensor.transpose(psT[0:TT, j * TT:(j + 1) * TT], s[0:TT, k % 2, 4 * q + j, :],
                                                 ident[0:TT, 0:TT])
                    mm.then_inc(pT_filled, 1)
                return fn

            def mix(hf):
                def fn(i, k):
                    pe.wait_ge(pT_kept, i * 4 + 2 * hf + 2)
                    if hf == 0:
                        pe.wait_ge(proj_freed, unit(i, k, 1) + 1)
                        reused(pe, h_done, i, 1)
                    else:
                        pe.wait_ge(oT_kept, i * 2 + 1)
                    for j in range(4):
                        for p in range(2):
                            head = 2 * (4 * hf + j) + p
                            mm = nc.tensor.matmul(psO[64 * p:64 * p + 64, j * TT:(j + 1) * TT],
                                                  v[0:TT, k, head * HD:(head + 1) * HD],
                                                  pT[0:TT, 8 * hf + 4 * p + j, :], start=True, stop=True)
                    mm.then_inc(oT_filled, 1)
                return fn

            def output(i, k):
                pe.wait_ge(oT_kept, i * 2 + 2)
                for ch in range(KI):
                    mm = nc.tensor.matmul(psO[0:TT, 0:D], oT[:, k % 2, ch, :], wo[:, ch, :],
                                          start=ch == 0, stop=ch == KI - 1)
                mm.then_inc(wo_done, 1)

            run(pe, NT, U, [(0, values(0)), (3, turn(0)), (0, values(1)), (3, turn(1)), (2, scores(0)),
                            (3, turn(2)), (3, mix(0)), (2, scores(1)), (3, turn(3)), (3, mix(1)),
                            (0, queries_keys), (3, output)])

        @block.scalar
        def _(act):
            def values(n):
                def fn(t, k):
                    act.wait_ge(proj_filled, unit(t, k, n) + 1)
                    reused(act, oT_filled, t, U, 2)
                    nc.scalar.activation(v[0:TT, k, n * 512:(n + 1) * 512], psP[0:TT, n % 2, :],
                                         ACT.Copy).then_inc(proj_freed, 1)
                return fn

            def queries_keys(lo, hi):
                def fn(t, k):
                    if k % 2:
                        return
                    for n in range(lo, hi):
                        act.wait_ge(proj_filled, unit(t, k, n + 2) + 1)
                        if n == 0 and not (isinstance(t, int) and t < 4):
                            act.wait_ge(scores_done, (t - 2) * 2)
                        nc.scalar.activation(
                            qk[:, (k // 2) % 2, 2 * n:2 * n + 2, :],
                            psP[:, n % 2, 0:4 * TT].rearrange("p (c t) -> p c t", c=2),
                            ACT.Copy).then_inc(proj_freed, 1)
                return fn

            def keep_pT(q):
                def fn(i, k):
                    act.wait_ge(pT_filled, i * 4 + q + 1)
                    if not (isinstance(i, int) and i < 1):
                        act.wait_ge(oT_filled, (i - 1) * 2 + q // 2 + 1)
                    nc.scalar.activation(pT[0:TT, 4 * q:4 * q + 4, :],
                                         psT[0:TT, 0:4 * TT].rearrange("p (j t) -> p j t", j=4),
                                         ACT.Copy).then_inc(pT_kept, 1)
                return fn

            def keep_oT(hf):
                def fn(i, k):
                    act.wait_ge(oT_filled, i * 2 + hf + 1)
                    reused(act, wo_done, i, 2)
                    nc.scalar.activation(oT[:, k % 2, 4 * hf:4 * hf + 4, :],
                                         psO[:, 0:4 * TT].rearrange("p (j t) -> p j t", j=4),
                                         ACT.Copy).then_inc(oT_kept, 1)
                return fn

            def exps(hf):
                def fn(i, k):
                    act.wait_ge(shifted, i * 2 + hf + 1)
                    sv = s[0:TT, k % 2, 8 * hf:8 * hf + 8, :]
                    nc.scalar.activation(sv, sv, ACT.Exp, scale=HD ** -0.5).then_inc(exp_done, 1)
                return fn

            run(act, NT, U, [(0, values(0)), (3, keep_pT(0)), (0, values(1)), (3, keep_pT(1)),
                             (3, keep_pT(2)), (3, keep_oT(0)), (3, keep_pT(3)), (3, keep_oT(1)),
                             (2, exps(0)), (0, queries_keys(0, 4)), (2, exps(1)), (0, queries_keys(4, 8))])

        @block.vector
        def _(dve):
            dve.wait_ge(weights_in, NLOAD)
            nc.vector.tensor_copy(mask[0:TT, :], mask_f32[0:TT, :]).then_inc(mask_done, 1)

            def shift(hf):
                def fn(i, k):
                    dve.wait_ge(scores_done, i * 2 + hf + 1)
                    reused(dve, shifted, i, 1, 2, hf - 1)
                    src = psS[0:TT, hf, :, 0:4 * TT].rearrange("q p (j t) -> q p j t", j=4)
                    tv = top[0:TT, hf, 0:8]
                    nc.vector.tensor_reduce(tv.rearrange("q (p j) -> q p j", p=2), src, AX.X, ALU.max)\
                        .then_inc(top_done, 1)
                    dve.wait_ge(top_done, i * 2 + hf + 1)
                    reused(dve, pT_filled, i, 2, 4, 0)
                    nc.vector.tensor_tensor(
                        s[0:TT, k % 2, 8 * hf:8 * hf + 8, :].rearrange("q (p j) t -> q p j t", p=2), src,
                        tv.rearrange("q (p j) -> q p j", p=2).unsqueeze(3).broadcast_to([TT, 2, 4, TT]),
                        ALU.subtract).then_inc(shifted, 1)
                return fn

            def scale(hf):
                def fn(i, k):
                    dve.wait_ge(exp_done, i * 2 + hf + 1)
                    sv = s[0:TT, k % 2, 8 * hf:8 * hf + 8, :]
                    nc.vector.tensor_reduce(total[0:TT, hf, 0:8], sv, AX.X, ALU.add).then_inc(total_done, 1)
                    dve.wait_ge(total_done, i * 2 + hf + 1)
                    nc.vector.reciprocal(inv[0:TT, hf, 0:8], total[0:TT, hf, 0:8]).then_inc(inv_done, 1)
                    dve.wait_ge(inv_done, i * 2 + hf + 1)
                    nc.vector.tensor_tensor(sv, sv, inv[0:TT, hf, 0:8].unsqueeze(2).broadcast_to([TT, 8, TT]),
                                            ALU.mult).then_inc(prob_done, 1)
                return fn

            def add(i, k):
                nc.vector.tensor_tensor(h[0:TT, i, :], h[0:TT, i, :], bo[0:TT, :], ALU.add).then_inc(h_bias, 1)
                dve.wait_ge(h_bias, i + 1)
                dve.wait_ge(wo_done, i + 1)
                nc.vector.tensor_tensor(h[0:TT, i, :], h[0:TT, i, :], psO[0:TT, 0:D], ALU.add)\
                    .then_inc(h_done, 1)

            run(dve, NT, U, [(2, shift(0)), (2, shift(1)), (2, scale(0)), (2, scale(1)), (3, add)])


def linker(eng, sem):
    count = [0]

    def link(ins):
        count[0] += 1
        ins.then_inc(sem, 1)
        eng.wait_ge(sem, count[0])
    return link


def one_hot_of_max(nc, link, x, top, hit, number, number_less_e, first):
    wide = [TT, NT, E]
    link(nc.vector.tensor_reduce(top, x, AX.X, ALU.max))
    link(nc.vector.tensor_tensor(hit, x, top.unsqueeze(2).broadcast_to(wide), ALU.is_equal))
    link(nc.vector.tensor_tensor(number, hit, number_less_e.unsqueeze(1).broadcast_to(wide), ALU.mult))
    link(nc.vector.tensor_reduce(first, number, AX.X, ALU.min))
    link(nc.vector.tensor_tensor(hit, number_less_e.unsqueeze(1).broadcast_to(wide),
                                 first.unsqueeze(2).broadcast_to(wide), ALU.is_equal))


def route_top1(g, ffn):
    nc, a, sb, pb, sem, h, xT = (g[k] for k in ("nc", "a", "sb", "pb", "sem", "h", "xT"))
    U = 2
    with ExitStack() as c:
        ln = LayerNorm(g, c, "ln1", slots=True)
        rms_w = sb("rms_w", [128, D], c=c)
        gate = sb("gate", [128, KD, E], c=c)
        less_e = sb("less_e", [128, E], c=c)
        square = sb("square", [128, D], c=c)
        ms = sb("ms", [128, 2, 3], c=c)
        xr = sb("xr", [128, 2, D], c=c)
        logits = sb("logits", [128, NT, E], c=c)
        p = sb("p", [128, NT, E], c=c)
        top, first, total, best = (sb(n, [128, NT], c=c) for n in ("r_top", "r_first", "r_total", "r_best"))
        psG = pb("psG", [128, 2, 512], c=c)
        weights_in = sem("gate_weights_in", c)
        ms_done = sem("ms_done", c)
        ms_eps = sem("ms_eps", c)
        rms_done = sem("rms_done", c)
        xr_done = sem("xr_done", c)
        x_kept = sem("route_x_kept", c)
        gated = sem("gated", c)
        logits_done = sem("logits_done", c)
        chain = sem("route_chain", c)
        shift_done = sem("route_shift_done", c)
        exp_done = sem("route_exp_done", c)
        block = c.enter_context(nc.Block())

        @block.sync
        def _(sp):
            sp.dma_start(rms_w[0:TT, :], a["ffn_rms_w"]).then_inc(weights_in, 16)
            sp.dma_start(gate[:, :, :], a["gate_wT"].rearrange("(c p) e -> p c e", p=128)).then_inc(weights_in, 16)
            sp.dma_start(less_e[0:TT, :], a["number_less_e"]).then_inc(weights_in, 16)

        @block.vector
        def _(dve):
            dve.wait_ge(weights_in, 48)

            def mean_square(i, k):
                dve.wait_ge(ln.xn_done, i + 1)
                reused(dve, xr_done, i, 2)
                nc.vector.scalar_tensor_tensor(out=square[0:TT, :], in0=ln.xn[0:TT, k % 2, :], scalar=1.0 / D,
                                               in1=ln.xn[0:TT, k % 2, :], op0=ALU.mult, op1=ALU.mult,
                                               accum_out=ms[0:TT, k % 2, 0:1]).then_inc(ms_done, 1)

            def rms(i, k):
                dve.wait_ge(rms_done, i + 1)
                reused(dve, ln.turned, i, 2)
                reused(dve, x_kept, i, 2)
                nc.vector.scalar_tensor_tensor(out=xr[0:TT, k % 2, :], in0=ln.xn[0:TT, k % 2, :],
                                               scalar=ms[0:TT, k % 2, 2:3], in1=rms_w[0:TT, :],
                                               op0=ALU.mult, op1=ALU.mult).then_inc(xr_done, 1)

            def normalise(i, k):
                reused(dve, xr_done, i, 2)
                ln.normalise(dve, i, k)

            def keep_logits(i, k):
                dve.wait_ge(gated, i + 1)
                nc.vector.tensor_scalar(logits[0:TT, i, :], psG[0:TT, k % 2, 0:E], 0.0, None, ALU.add)\
                    .then_inc(logits_done, 1)
            run(dve, NT, U, [(0, lambda i, k: ln.statistics(dve, i, k)), (1, normalise), (1, mean_square),
                             (2, rms), (4, keep_logits)])
            link = linker(dve, chain)
            dve.wait_ge(logits_done, NT)
            hit, number = ffn.hits[0], p
            one_hot_of_max(nc, link, logits[0:TT], top[0:TT], hit[0:TT], number[0:TT], less_e[0:TT], first[0:TT])
            nc.vector.tensor_tensor(logits[0:TT], logits[0:TT], top[0:TT].unsqueeze(2).broadcast_to([TT, NT, E]),
                                    ALU.subtract).then_inc(shift_done, 1)
            dve.wait_ge(exp_done, 1)
            link(nc.vector.tensor_reduce(total[0:TT], logits[0:TT], AX.X, ALU.add))
            link(nc.vector.tensor_reduce(best[0:TT], logits[0:TT], AX.X, ALU.max))
            link(nc.vector.reciprocal(total[0:TT], total[0:TT]))
            link(nc.vector.tensor_tensor(ffn.scores[0][0:TT], best[0:TT], total[0:TT], ALU.mult))

        @block.gpsimd
        def _(pool):
            def inverse_rms(i, k):
                pool.wait_ge(ms_done, i + 1)
                nc.gpsimd.tensor_tensor(ms[0:TT, k % 2, 1:2], ms[0:TT, k % 2, 0:1], g["epsilon"][0:TT, 1:2],
                                        ALU.add).then_inc(ms_eps, 1)
                pool.wait_ge(ms_eps, i + 1)
                nc.gpsimd.tensor_tensor(ms[0:TT, k % 2, 2:3], ms[0:TT, k % 2, 1:2], g["mhalf"][0:TT, :],
                                        ALU.pow).then_inc(rms_done, 1)

            def keep_x(i, k):
                pool.wait_ge(xr_done, i + 1)
                through(pool, i, g["passed"])
                nc.gpsimd.tensor_copy(ffn.x[0:TT, i, :], xr[0:TT, k % 2, :]).then_inc(x_kept, 1)
            run(pool, NT, U, [(0, lambda i, k: ln.inverse(pool, i, k)), (1, inverse_rms), (2, keep_x)])

        @block.tensor
        def _(pe):
            pe.wait_ge(weights_in, 48)

            def logit(i, k):
                pe.wait_ge(ln.kept, i + 1)
                reused(pe, logits_done, i, 2)
                for kc in range(KD):
                    mm = nc.tensor.matmul(psG[0:TT, k % 2, 0:E], ln.xs[:, k % 2, kc, :], gate[:, kc, :],
                                          start=kc == 0, stop=kc == KD - 1)
                mm.then_inc(gated, 1)
            run(pe, NT, U, [(2, lambda i, k: ln.turn(pe, i, k, xr_done, xr[0:TT, k % 2, :])), (3, logit)])

        @block.scalar
        def _(act):
            run(act, NT, U, [(2, lambda i, k: ln.keep_stationary(act, i, k, gated, last=True))])
            act.wait_ge(shift_done, 1)
            nc.scalar.activation(logits[0:TT], logits[0:TT], ACT.Exp).then_inc(exp_done, 1)


def route_top2(g, ffn):
    nc, a, sb, pb, sem, h, xT = (g[k] for k in ("nc", "a", "sb", "pb", "sem", "h", "xT"))
    U = 2
    with ExitStack() as c:
        ln = LayerNorm(g, c, "ln3", slots=True)
        rw1 = sb("rw1", [128, KD, D], c=c)
        rb1 = sb("rb1", [128, KD], c=c)
        rw2 = sb("rw2", [128, KD, E], c=c)
        rb2 = sb("rb2", [128, E], c=c)
        less_e = sb("less_e2", [128, E], c=c)
        hidden = sb("hidden", [128, 2, KD, TT], c=c)
        logits = sb("logits2", [128, NT, E], c=c)
        rest, number = (sb(n, [128, NT, E], c=c) for n in ("r_rest", "r_number"))
        hit1, hit2 = ffn.hits
        top1, top2, first, total = (sb(n, [128, NT], c=c) for n in ("r_top1", "r_top2", "r2_first", "r2_total"))
        psH = pb("psRH", [128, 2, 512], c=c)
        psG = pb("psRG", [128, 2, 512], c=c)
        weights_in = sem("router_weights_in", c)
        hidden_filled = sem("hidden_filled", c)
        hidden_kept = sem("hidden_kept", c)
        gated = sem("gated2", c)
        logits_done = sem("logits2_done", c)
        h_done = sem("router_h_done", c)
        x_kept = sem("route2_x_kept", c)
        chain = sem("route2_chain", c)
        shift_done = sem("route2_shift_done", c)
        exp_done = sem("route2_exp_done", c)
        block = c.enter_context(nc.Block())

        @block.sync
        def _(sp):
            sp.dma_start(rw1[:, :, :], a["rw1"].rearrange("(c p) e -> p c e", p=128)).then_inc(weights_in, 16)
            sp.dma_start(rw2[:, :, :], a["rw2"].rearrange("(c p) e -> p c e", p=128)).then_inc(weights_in, 16)
            sp.dma_start(rb1[:, :], a["rb1"]).then_inc(weights_in, 16)
            sp.dma_start(rb2[0:TT, :], a["rb2"]).then_inc(weights_in, 16)
            sp.dma_start(less_e[0:TT, :], a["number_less_e"]).then_inc(weights_in, 16)

        @block.vector
        def _(dve):
            dve.wait_ge(weights_in, 80)

            def residual(i, k):
                dve.wait_ge(ln.xn_done, i + 1)
                nc.vector.tensor_tensor(h[0:TT, i, :], h[0:TT, i, :], ln.xn[0:TT, k % 2, :], ALU.add)\
                    .then_inc(h_done, 1)

            def normalise(i, k):
                reused(dve, h_done, i, 2)
                reused(dve, x_kept, i, 2)
                ln.normalise(dve, i, k)

            def keep_logits(i, k):
                dve.wait_ge(gated, i + 1)
                nc.vector.tensor_tensor(logits[0:TT, i, :], psG[0:TT, k % 2, 0:E], rb2[0:TT, :], ALU.add)\
                    .then_inc(logits_done, 1)
            run(dve, NT, U, [(0, lambda i, k: ln.statistics(dve, i, k)), (1, normalise), (1, residual),
                             (3, keep_logits)])
            link = linker(dve, chain)
            dve.wait_ge(logits_done, NT)
            one_hot_of_max(nc, link, logits[0:TT], top1[0:TT], hit1[0:TT], number[0:TT], less_e[0:TT], first[0:TT])
            link(nc.vector.scalar_tensor_tensor(out=rest[0:TT], in0=hit1[0:TT], scalar=-1.0e30, in1=logits[0:TT],
                                                op0=ALU.mult, op1=ALU.add))
            one_hot_of_max(nc, link, rest[0:TT], top2[0:TT], hit2[0:TT], number[0:TT], less_e[0:TT], first[0:TT])
            nc.vector.tensor_tensor(top2[0:TT], top2[0:TT], top1[0:TT], ALU.subtract).then_inc(shift_done, 1)
            dve.wait_ge(exp_done, 1)
            link(nc.vector.tensor_scalar(total[0:TT], top2[0:TT], 1.0, None, ALU.add))
            link(nc.vector.reciprocal(ffn.scores[0][0:TT], total[0:TT]))
            link(nc.vector.tensor_tensor(ffn.scores[1][0:TT], top2[0:TT], ffn.scores[0][0:TT], ALU.mult))

        @block.gpsimd
        def _(pool):
            def keep_x(i, k):
                pool.wait_ge(ln.xn_done, i + 1)
                through(pool, i, g["passed"])
                nc.gpsimd.tensor_copy(ffn.x[0:TT, i, :], ln.xn[0:TT, k % 2, :]).then_inc(x_kept, 1)
            run(pool, NT, U, [(0, lambda i, k: ln.inverse(pool, i, k)), (1, keep_x)])

        @block.tensor
        def _(pe):
            pe.wait_ge(weights_in, 80)

            def hide(i, k):
                pe.wait_ge(ln.kept, i + 1)
                reused(pe, hidden_kept, i, 2)
                for m in range(KD):
                    for kc in range(KD):
                        mm = nc.tensor.matmul(psH[:, k % 2, m * TT:(m + 1) * TT], rw1[:, kc, m * 128:(m + 1) * 128],
                                              ln.xs[:, k % 2, kc, :], start=kc == 0, stop=kc == KD - 1)
                mm.then_inc(hidden_filled, 1)

            def logit(i, k):
                pe.wait_ge(hidden_kept, i + 1)
                reused(pe, logits_done, i, 2)
                for kc in range(KD):
                    mm = nc.tensor.matmul(psG[0:TT, k % 2, 0:E], hidden[:, k % 2, kc, :], rw2[:, kc, :],
                                          start=kc == 0, stop=kc == KD - 1)
                mm.then_inc(gated, 1)
            run(pe, NT, U, [(1, lambda i, k: ln.turn(pe, i, k)), (2, hide), (3, logit)])

        @block.scalar
        def _(act):
            act.wait_ge(weights_in, 80)

            def keep_hidden(i, k):
                act.wait_ge(hidden_filled, i + 1)
                reused(act, gated, i, 2)
                for m in range(KD):
                    ins = nc.scalar.activation(hidden[:, k % 2, m, :], psH[:, k % 2, m * TT:(m + 1) * TT], ACT.Silu,
                                               bias=rb1[:, m:m + 1])
                ins.then_inc(hidden_kept, 1)
            run(act, NT, U, [(1, lambda i, k: ln.keep_stationary(act, i, k, hidden_filled, last=True)),
                             (2, keep_hidden)])
            act.wait_ge(shift_done, 1)
            nc.scalar.activation(top2[0:TT], top2[0:TT], ACT.Exp).then_inc(exp_done, 1)


def step_sizes(g, ln_out, dt, dA):
    nc, a, sb, pb, sem, h, xT = (g[k] for k in ("nc", "a", "sb", "pb", "sem", "h", "xT"))
    U = 2
    with ExitStack() as c:
        ln = LayerNorm(g, c, "ln2", slots=True)
        wdt = sb("wdt", [128, KD, MH], c=c)
        dt_bias = sb("dt_bias", [128, MH], c=c)
        A_log = sb("A_log", [128, MH], c=c)
        A_exp = sb("A_exp", [128, MH], c=c)
        raw, u, w, lnw, t0 = (sb("sp_" + n, [128, NT, MH], c=c) for n in ("raw", "u", "w", "lnw", "t0"))
        psD = pb("psD", [128, 2, 512], c=c)
        weights_in = sem("dt_weights_in", c)
        dt_filled = sem("dt_filled", c)
        raw_done = sem("dt_raw_done", c)
        xn_kept = sem("xn_kept", c)
        chain = sem("dt_chain", c)
        abs_done = sem("dt_abs_done", c)
        exp_done = sem("dt_exp_done", c)
        w_done = sem("dt_w_done", c)
        ln_done = sem("dt_ln_done", c)
        block = c.enter_context(nc.Block())

        @block.sync
        def _(sp):
            sp.dma_start(wdt[:, :, :], a["W_in"].rearrange("(c p) n -> p c n", p=128)[:, :, DI + CONV:])\
                .then_inc(weights_in, 16)
            sp.dma_start(dt_bias[0:TT, :], a["dt_bias"]).then_inc(weights_in, 16)
            sp.dma_start(A_log[0:TT, :], a["A_log"]).then_inc(weights_in, 16)

        @block.vector
        def _(dve):
            dve.wait_ge(weights_in, 48)

            def normalise(i, k):
                reused(dve, xn_kept, i, 2)
                ln.normalise(dve, i, k)

            def keep_raw(i, k):
                dve.wait_ge(dt_filled, i + 1)
                nc.vector.tensor_tensor(raw[0:TT, i, :], psD[0:TT, k % 2, 0:MH], dt_bias[0:TT, :], ALU.add)\
                    .then_inc(raw_done, 1)
            run(dve, NT, U, [(0, lambda i, k: ln.statistics(dve, i, k)), (1, normalise), (3, keep_raw)])
            link = linker(dve, chain)
            dve.wait_ge(raw_done, NT)
            nc.vector.scalar_tensor_tensor(out=u[0:TT], in0=raw[0:TT], scalar=-1.0, in1=raw[0:TT],
                                           op0=ALU.mult, op1=ALU.max).then_inc(abs_done, 1)
            dve.wait_ge(exp_done, 1)
            nc.vector.tensor_scalar(w[0:TT], u[0:TT], 1.0, None, ALU.add).then_inc(w_done, 1)
            dve.wait_ge(ln_done, 1)
            link(nc.vector.tensor_scalar(w[0:TT], w[0:TT], -1.0, None, ALU.add))
            link(nc.vector.tensor_scalar(t0[0:TT], w[0:TT], 0.0, None, ALU.is_equal))
            link(nc.vector.tensor_tensor(w[0:TT], w[0:TT], t0[0:TT], ALU.add))
            link(nc.vector.reciprocal(w[0:TT], w[0:TT]))
            link(nc.vector.tensor_tensor(lnw[0:TT], lnw[0:TT], w[0:TT], ALU.mult))
            link(nc.vector.tensor_tensor(lnw[0:TT], lnw[0:TT], t0[0:TT], ALU.add))
            link(nc.vector.tensor_tensor(u[0:TT], u[0:TT], lnw[0:TT], ALU.mult))
            link(nc.vector.scalar_tensor_tensor(out=dt[0:TT], in0=raw[0:TT], scalar=0.0, in1=u[0:TT],
                                                op0=ALU.max, op1=ALU.add))
            link(nc.vector.scalar_tensor_tensor(out=dA[0:TT], in0=dt[0:TT], scalar=-1.0,
                                                in1=A_exp[0:TT].unsqueeze(1).broadcast_to([TT, NT, MH]),
                                                op0=ALU.mult, op1=ALU.mult))

        @block.gpsimd
        def _(pool):
            def keep_xn(i, k):
                pool.wait_ge(ln.xn_done, i + 1)
                through(pool, i, g["passed"])
                nc.gpsimd.tensor_copy(ln_out[0:TT, i, :], ln.xn[0:TT, k % 2, :]).then_inc(xn_kept, 1)
            run(pool, NT, U, [(0, lambda i, k: ln.inverse(pool, i, k)), (1, keep_xn)])

        @block.tensor
        def _(pe):
            pe.wait_ge(weights_in, 48)

            def product(i, k):
                pe.wait_ge(ln.xs_kept, i + 1)
                reused(pe, raw_done, i, 2)
                for kc in range(KD):
                    mm = nc.tensor.matmul(psD[0:TT, k % 2, 0:MH], ln.xs[:, k % 2, kc, :], wdt[:, kc, :],
                                          start=kc == 0, stop=kc == KD - 1)
                mm.then_inc(dt_filled, 1)
            run(pe, NT, U, [(1, lambda i, k: ln.turn(pe, i, k)), (2, product)])

        @block.scalar
        def _(act):
            act.wait_ge(weights_in, 48)
            run(act, NT, U, [(1, lambda i, k: ln.keep_stationary(act, i, k, dt_filled)),
                             (1, lambda i, k: ln.keep(act, i, k))])
            nc.scalar.activation(A_exp[0:TT], A_log[0:TT], ACT.Exp)
            act.wait_ge(abs_done, 1)
            nc.scalar.activation(u[0:TT], u[0:TT], ACT.Exp, scale=-1.0).then_inc(exp_done, 1)
            act.wait_ge(w_done, 1)
            nc.scalar.activation(lnw[0:TT], w[0:TT], ACT.Ln).then_inc(ln_done, 1)


def mamba(g):
    nc, a, sb, pb, sem, h, xT, ident = (g[k] for k in ("nc", "a", "sb", "pb", "sem", "h", "xT", "ident"))
    U = 2
    PAD = 3
    UN = 2 * TT
    NU = KC // 2
    KY = DI // 128
    HH = MH // 2
    with ExitStack() as c:
        xn = sb("xn", [128, NT, D], c=c)
        dt = sb("dt", [128, NT, MH], c=c)
        dA = sb("dA", [128, NT, MH], c=c)
        step_sizes(g, xn, dt, dA)

        wz = sb("wz", [128, KD, DI], c=c)
        wx = sb("wx", [128, KD, CONV], c=c)
        wout = sb("wout", [128, KY, D], c=c)
        wglu = sb("wglu", [128, KD, 2 * D], c=c)
        glu_b = sb("glu_b", [128, 2 * D], c=c)
        conv_w = sb("conv_w", [128, KC, 4], c=c)
        conv_b = sb("conv_b", [128, KC], c=c)
        out_w = sb("out_w", [128, KY], c=c)
        skip = sb("skip", [128, MH], c=c)
        ln_w = sb("ln_w", [128, D], c=c)
        ln_b = sb("ln_b", [128, D], c=c)
        after = sb("after", [128, TT], c=c)
        upto = sb("upto", [128, TT], c=c)
        causal = sb("causal", [128, TT], c=c)
        xs = sb("m_xs", [128, 2, KD, TT], c=c)
        raw = sb("m_raw", [128, 2, KC, PER, PAD + TOK], c=c)
        acc = sb("m_acc", [128, 2, KC, TT], c=c)
        xbc = sb("m_xbc", [128, 2, KC, TT], c=c)
        zs = sb("m_zs", [128, 2, DI], c=c)
        R = sb("m_R", [128, 2, MH, TT], c=c)
        W = sb("m_W", [128, 2, MH, TT], c=c)
        G = sb("m_G", [128, 2, TT], c=c)
        xdt = sb("m_xdt", [128, 2, DI], c=c)
        xD = sb("m_xD", [128, 2, DI], c=c)
        y = sb("m_y", [128, 2, DI], c=c)
        junk = sb("m_junk", [128, DI], c=c)
        ms = sb("m_ms", [128, 2, 3], c=c)
        yT = sb("m_yT", [128, 2, KY, TT], c=c)
        y1 = sb("m_y1", [128, 2, D], c=c)
        y1T = sb("m_y1T", [128, 2, KD, TT], c=c)
        glu = sb("m_glu", [128, 2, 2 * D], c=c)
        th = sb("m_th", [128, 2, D], c=c)
        y2 = sb("m_y2", [128, 2, D], c=c)
        st = sb("m_st", [128, 2, 6], c=c)
        mv = sb("m_mv", [128, 2, 2], c=c)
        rs = sb("m_rs", [128, 2, 2], c=c)
        nrm = sb("m_nrm", [128, 2, D], c=c)
        psC = pb("psC", [128, 2, 512], c=c)
        psG = pb("psCB", [128, 512], c=c)
        psR = pb("psR", [128, 512], c=c)
        psX = pb("psX", [128, 512], c=c)
        psS = pb("psSeg", [128, 512], c=c)
        psY = pb("psY", [128, 512], c=c)
        psU = pb("psU", [128, 512], c=c)
        names = ("weights_in raw_zeroed wout_done xs_done xbc_filled raw_kept conv_tap xbc_done z_filled zs_done "
                 "R_done x_filled G_filled xdt_done xD_done G_done seg_filled seg_exp W_done y_filled y_summed "
                 "y_gated y_squared ms_eps ms_done yT_filled yT_kept out_filled y1_done y1T_filled y1T_kept "
                 "glu_filled glu_biased tanh_done gated y2_done st_done mv_done rs_eps rs_done nrm_done scaled "
                 "biased h_done").split()
        m = {n: sem("m_" + n, c) for n in names}
        (weights_in, raw_zeroed, wout_done, xs_done, xbc_filled, raw_kept, conv_tap, xbc_done, z_filled, zs_done,
         R_done, x_filled, G_filled, xdt_done, xD_done, G_done, seg_filled, seg_exp, W_done, y_filled, y_summed,
         y_gated, y_squared, ms_eps, ms_done, yT_filled, yT_kept, out_filled, y1_done, y1T_filled, y1T_kept,
         glu_filled, glu_biased, tanh_done, gated, y2_done, st_done, mv_done, rs_eps, rs_done, nrm_done, scaled,
         biased, h_done) = (m[n] for n in names)
        block = c.enter_context(nc.Block())
        loads = [(wz[:, :, :], a["W_in"].rearrange("(c p) n -> p c n", p=128)[:, :, 0:DI]),
                 (wx[:, :, :], a["W_in"].rearrange("(c p) n -> p c n", p=128)[:, :, DI:DI + CONV]),
                 (wout[:, :, :], a["W_out"].rearrange("(c p) n -> p c n", p=128)),
                 (wglu[:, :, :], a["glu_w"].rearrange("(c p) n -> p c n", p=128)),
                 (glu_b[0:TT, :], a["glu_b"]), (conv_w[:, :, :], a["conv_w"]), (conv_b[:, :], a["conv_b"]),
                 (out_w[:, :], a["m_rms_w"]), (skip[0:TT, :], a["D_skip"]), (ln_w[0:TT, :], a["ln_w"]),
                 (ln_b[0:TT, :], a["ln_b"]), (after[0:TT, :], a["after"]), (upto[0:TT, :], a["upto"]),
                 (causal[0:TT, :], a["causal"])]
        ALL = 16 * len(loads)

        @block.sync
        def _(sp):
            for dst, src in loads:
                sp.dma_start(dst, src).then_inc(weights_in, 16)

        @block.gpsimd
        def _(pool):
            passed = g["passed"]
            pool.wait_ge(weights_in, ALL)

            def stationary(i, k):
                reused(pool, z_filled, i, 2)
                through(pool, i, passed)
                nc.gpsimd.tensor_copy(xs[:, k % 2, :, :], xT[:, :, cols(i)]).then_inc(xs_done, 1)

            def spread(i, k):
                reused(pool, seg_filled, i, 2, 2, 0)
                through(pool, i, passed)
                nc.gpsimd.tensor_tensor(R[0:TT, k % 2, :, :], upto[0:TT, :].unsqueeze(1).broadcast_to([TT, MH, TT]),
                                        dA[0:TT, i, :].unsqueeze(2).broadcast_to([TT, MH, TT]), ALU.mult)\
                    .then_inc(R_done, 1)

            def inverse_rms(i, k):
                pool.wait_ge(y_squared, i + 1)
                nc.gpsimd.tensor_tensor(ms[0:TT, k % 2, 1:2], ms[0:TT, k % 2, 0:1], g["epsilon"][0:TT, 0:1],
                                        ALU.add).then_inc(ms_eps, 1)
                pool.wait_ge(ms_eps, i + 1)
                nc.gpsimd.tensor_tensor(ms[0:TT, k % 2, 2:3], ms[0:TT, k % 2, 1:2], g["mhalf"][0:TT, :],
                                        ALU.pow).then_inc(ms_done, 1)

            def inverse_deviation(i, k):
                pool.wait_ge(mv_done, i + 1)
                reused(pool, nrm_done, i, 2)
                nc.gpsimd.tensor_tensor(rs[0:TT, k % 2, 0:1], mv[0:TT, k % 2, 1:2], g["epsilon"][0:TT, 0:1],
                                        ALU.add).then_inc(rs_eps, 1)
                pool.wait_ge(rs_eps, i + 1)
                nc.gpsimd.tensor_tensor(rs[0:TT, k % 2, 1:2], rs[0:TT, k % 2, 0:1], g["mhalf"][0:TT, :],
                                        ALU.pow).then_inc(rs_done, 1)

            def affine(i, k):
                pool.wait_ge(nrm_done, i + 1)
                nc.gpsimd.tensor_tensor(nrm[0:TT, k % 2, :], nrm[0:TT, k % 2, :], ln_w[0:TT, :], ALU.mult)\
                    .then_inc(scaled, 1)
                pool.wait_ge(scaled, i + 1)
                nc.gpsimd.tensor_tensor(nrm[0:TT, k % 2, :], nrm[0:TT, k % 2, :], ln_b[0:TT, :], ALU.add)\
                    .then_inc(biased, 1)
                pool.wait_ge(biased, i + 1)
                through(pool, i, passed)
                nc.gpsimd.tensor_tensor(h[0:TT, i, :], h[0:TT, i, :], nrm[0:TT, k % 2, :], ALU.add)\
                    .then_inc(h_done, 1)
            run(pool, NT, U, [(0, stationary), (1, spread), (3, inverse_rms), (5, inverse_deviation), (6, affine)])

        @block.tensor
        def _(pe):
            pe.wait_ge(weights_in, ALL)
            pe.wait_ge(wout_done, 1)

            def heads(i, k):
                pe.wait_ge(W_done, i * 2 + 2)
                pe.wait_ge(xdt_done, i + 1)
                reused(pe, y_summed, i, 1)
                for hd in range(MH):
                    mm = nc.tensor.matmul(psY[0:TT, hd * 64:(hd + 1) * 64], W[0:TT, k % 2, hd, :],
                                          xdt[0:TT, k % 2, hd * 64:(hd + 1) * 64], start=True, stop=True)
                mm.then_inc(y_filled, 1)

            def project(i, k):
                pe.wait_ge(xs_done, i + 1)
                for u in range(NU):
                    if u == 0:
                        reused(pe, raw_kept, i, 1, NU, 0)
                    elif u == 1:
                        reused(pe, zs_done, i, 2)
                    else:
                        pe.wait_ge(raw_kept, i * NU + 1)
                    for half in range(2):
                        ch = 2 * u + half
                        for kc in range(KD):
                            mm = nc.tensor.matmul(psC[:, u % 2, half * TT:(half + 1) * TT],
                                                  wx[:, kc, ch * 128:(ch + 1) * 128], xs[:, k % 2, kc, :],
                                                  start=kc == 0, stop=kc == KD - 1)
                    mm.then_inc(xbc_filled, 1)

            def turn_y1(i, k):
                pe.wait_ge(y1_done, i + 1)
                for ch in range(KD):
                    mm = nc.tensor.transpose(psR[:, ch * TT:(ch + 1) * TT],
                                             y1[0:TT, k % 2, ch * 128:(ch + 1) * 128], ident[0:TT, 0:TT])
                mm.then_inc(y1T_filled, 1)

            def gates(i, k):
                pe.wait_ge(raw_kept, NT * NU if isinstance(i, int) and i == NT - 1 else (i + 1) * NU + 2)
                for kc in range(KD):
                    mm = nc.tensor.matmul(psC[0:TT, 1, :], xs[:, k % 2, kc, :], wz[:, kc, :],
                                          start=kc == 0, stop=kc == KD - 1)
                mm.then_inc(z_filled, 1)

            def turn_x(i, k):
                pe.wait_ge(xbc_done, i + 1)
                reused(pe, xD_done, i, 1)
                for ch in range(KY):
                    mm = nc.tensor.transpose(psX[0:TT, ch * 128:(ch + 1) * 128], xbc[:, k % 2, ch, :], ident[:, :])
                mm.then_inc(x_filled, 1)
                reused(pe, G_done, i, 1)
                nc.tensor.matmul(psG[0:TT, 0:TT], xbc[:, k % 2, KY, :], xbc[:, k % 2, KY + 1, :],
                                 start=True, stop=True).then_inc(G_filled, 1)

            def turn_y(i, k):
                pe.wait_ge(y_gated, i + 1)
                reused(pe, y1T_kept, i, 1)
                for ch in range(KY):
                    mm = nc.tensor.transpose(psR[:, ch * TT:(ch + 1) * TT],
                                             y[0:TT, k % 2, ch * 128:(ch + 1) * 128], ident[0:TT, 0:TT])
                mm.then_inc(yT_filled, 1)

            def sums(i, k):
                pe.wait_ge(R_done, i + 1)
                for hf in range(2):
                    if not (isinstance(i, int) and i * 2 + hf < 1):
                        pe.wait_ge(seg_exp, i * 2 + hf)
                    nc.tensor.matmul(psS[0:TT, 0:HH * TT], after[0:TT, :],
                                     R[0:TT, k % 2, hf * HH:(hf + 1) * HH, :], start=True, stop=True)\
                        .then_inc(seg_filled, 1)

            def linear_unit(i, k):
                pe.wait_ge(y1T_kept, i + 1)
                reused(pe, glu_biased, i, 1)
                for kc in range(KD):
                    mm = nc.tensor.matmul(psU[0:TT, :], y1T[:, k % 2, kc, :], wglu[:, kc, :],
                                          start=kc == 0, stop=kc == KD - 1)
                mm.then_inc(glu_filled, 1)

            def output(i, k):
                pe.wait_ge(yT_kept, i + 1)
                for ch in range(KY):
                    mm = nc.tensor.matmul(psR[0:TT, 0:D], yT[:, k % 2, ch, :], wout[:, ch, :],
                                          start=ch == 0, stop=ch == KY - 1)
                mm.then_inc(out_filled, 1)
            run(pe, NT, U, [(3, heads), (0, project), (5, turn_y1), (1, gates), (2, turn_x), (4, turn_y), (2, sums),
                            (5, linear_unit), (4, output)])

        @block.scalar
        def _(act):
            act.wait_ge(raw_zeroed, 1)

            def keep_raw(i, k):
                reused(act, conv_tap, i, 2, 4, 0)
                for u in range(NU):
                    act.wait_ge(xbc_filled, i * NU + u + 1)
                    for half in range(2):
                        ins = nc.scalar.activation(
                            raw[:, k % 2, 2 * u + half, :, PAD:],
                            psC[:, u % 2, half * TT:(half + 1) * TT].rearrange("p (b t) -> p b t", b=PER), ACT.Copy)
                    ins.then_inc(raw_kept, 1)

            def keep_y1T(i, k):
                act.wait_ge(y1T_filled, i + 1)
                reused(act, glu_filled, i, 2)
                nc.scalar.activation(y1T[:, k % 2, :, :], psR[:, 0:UN].rearrange("p (c t) -> p c t", c=KD),
                                     ACT.Copy).then_inc(y1T_kept, 1)

            def activate(i, k):
                act.wait_ge(conv_tap, i * 4 + 4)
                reused(act, G_filled, i, 2)
                nc.scalar.activation(xbc[:, k % 2, :, :], acc[:, k % 2, :, :], ACT.Silu).then_inc(xbc_done, 1)

            def gate(i, k):
                reused(act, y_gated, i, 2)
                act.wait_ge(z_filled, i + 1)
                nc.scalar.activation(zs[0:TT, k % 2, :], psC[0:TT, 1, :], ACT.Silu).then_inc(zs_done, 1)

            def keep_yT(i, k):
                act.wait_ge(yT_filled, i + 1)
                reused(act, out_filled, i, 2)
                nc.scalar.activation(yT[:, k % 2, :, :], psR[:, 0:KY * TT].rearrange("p (c t) -> p c t", c=KY),
                                     ACT.Copy).then_inc(yT_kept, 1)

            def decay(i, k):
                reused(act, y_filled, i, 2)
                for hf in range(2):
                    act.wait_ge(seg_filled, i * 2 + hf + 1)
                    nc.scalar.activation(W[0:TT, k % 2, hf * HH:(hf + 1) * HH, :],
                                         psS[0:TT, 0:HH * TT].rearrange("p (j t) -> p j t", j=HH), ACT.Exp)\
                        .then_inc(seg_exp, 1)

            def half_gate(i, k):
                act.wait_ge(glu_biased, i + 1)
                reused(act, gated, i, 2)
                nc.scalar.activation(th[0:TT, k % 2, :], glu[0:TT, k % 2, D:], ACT.Tanh, scale=0.5)\
                    .then_inc(tanh_done, 1)
            run(act, NT, U, [(0, keep_raw), (5, keep_y1T), (1, activate), (1, gate), (4, keep_yT), (2, decay),
                             (5, half_gate)])

        @block.vector
        def _(dve):
            nc.vector.memset(raw[:, :, :, :, :], 0.0).then_inc(raw_zeroed, 1)
            dve.wait_ge(weights_in, ALL)
            nc.vector.tensor_tensor(wout[:, :, :], wout[:, :, :], out_w[:, :].unsqueeze(2).broadcast_to([128, KY, D]),
                                    ALU.mult).then_inc(wout_done, 1)

            def heads(i, k):
                v = y[0:TT, k % 2, :]
                dve.wait_ge(y_filled, i + 1)
                dve.wait_ge(xD_done, i + 1)
                reused(dve, yT_filled, i, 2)
                nc.vector.tensor_tensor(v, psY[0:TT, :], xD[0:TT, k % 2, :], ALU.add).then_inc(y_summed, 1)
                dve.wait_ge(y_summed, i + 1)
                dve.wait_ge(zs_done, i + 1)
                nc.vector.tensor_tensor(v, v, zs[0:TT, k % 2, :], ALU.mult).then_inc(y_gated, 1)
                dve.wait_ge(y_gated, i + 1)
                reused(dve, y1_done, i, 2)
                nc.vector.scalar_tensor_tensor(out=junk[0:TT, :], in0=v, scalar=1.0 / DI, in1=v, op0=ALU.mult,
                                               op1=ALU.mult, accum_out=ms[0:TT, k % 2, 0:1]).then_inc(y_squared, 1)

            def convolve(i, k):
                dve.wait_ge(raw_kept, i * NU + NU)
                reused(dve, xbc_done, i, 2)
                for tap in range(4):
                    if tap:
                        dve.wait_ge(conv_tap, i * 4 + tap)
                    for ch in range(KC):
                        src = raw[:, k % 2, ch, :, tap:tap + TOK]
                        dst = acc[:, k % 2, ch, :].rearrange("p (b t) -> p b t", b=PER)
                        if tap == 0:
                            ins = nc.vector.tensor_scalar(dst, src, conv_w[:, ch, 0:1], conv_b[:, ch:ch + 1],
                                                          ALU.mult, ALU.add)
                        else:
                            ins = nc.vector.scalar_tensor_tensor(out=dst, in0=src, scalar=conv_w[:, ch, tap:tap + 1],
                                                                 in1=dst, op0=ALU.mult, op1=ALU.add)
                    ins.then_inc(conv_tap, 1)

            def inputs(i, k):
                xv = psX[0:TT, :].rearrange("s (j d) -> s j d", j=MH)
                wide = [TT, MH, 64]
                dve.wait_ge(x_filled, i + 1)
                reused(dve, y_filled, i, 2)
                nc.vector.tensor_tensor(xdt[0:TT, k % 2, :].rearrange("s (j d) -> s j d", j=MH), xv,
                                        dt[0:TT, i, :].unsqueeze(2).broadcast_to(wide), ALU.mult).then_inc(xdt_done, 1)
                reused(dve, y_summed, i, 2)
                nc.vector.tensor_tensor(xD[0:TT, k % 2, :].rearrange("s (j d) -> s j d", j=MH), xv,
                                        skip[0:TT, :].unsqueeze(2).broadcast_to(wide), ALU.mult).then_inc(xD_done, 1)
                dve.wait_ge(G_filled, i + 1)
                nc.vector.tensor_tensor(G[0:TT, k % 2, :], psG[0:TT, 0:TT], causal[0:TT, :], ALU.mult)\
                    .then_inc(G_done, 1)

            def decayed(i, k):
                dve.wait_ge(G_done, i + 1)
                for hf in range(2):
                    dve.wait_ge(seg_exp, i * 2 + hf + 1)
                    w = W[0:TT, k % 2, hf * HH:(hf + 1) * HH, :]
                    nc.vector.tensor_tensor(w, w, G[0:TT, k % 2, :].unsqueeze(1).broadcast_to([TT, HH, TT]), ALU.mult)\
                        .then_inc(W_done, 1)

            def residual(i, k):
                dve.wait_ge(out_filled, i + 1)
                dve.wait_ge(ms_done, i + 1)
                reused(dve, y2_done, i, 2)
                nc.vector.scalar_tensor_tensor(out=y1[0:TT, k % 2, :], in0=psR[0:TT, 0:D],
                                               scalar=ms[0:TT, k % 2, 2:3], in1=xn[0:TT, i, :],
                                               op0=ALU.mult, op1=ALU.add).then_inc(y1_done, 1)

            def linear_unit(i, k):
                dve.wait_ge(glu_filled, i + 1)
                reused(dve, gated, i, 2)
                nc.vector.tensor_tensor(glu[0:TT, k % 2, :], psU[0:TT, :], glu_b[0:TT, :], ALU.add)\
                    .then_inc(glu_biased, 1)
                dve.wait_ge(tanh_done, i + 1)
                nc.vector.scalar_tensor_tensor(out=th[0:TT, k % 2, :], in0=th[0:TT, k % 2, :], scalar=1.0,
                                               in1=glu[0:TT, k % 2, 0:D], op0=ALU.add, op1=ALU.mult).then_inc(gated, 1)
                dve.wait_ge(gated, i + 1)
                dve.wait_ge(y1_done, i + 1)
                reused(dve, nrm_done, i, 2)
                nc.vector.scalar_tensor_tensor(out=y2[0:TT, k % 2, :], in0=th[0:TT, k % 2, :], scalar=0.5,
                                               in1=y1[0:TT, k % 2, :], op0=ALU.mult, op1=ALU.add).then_inc(y2_done, 1)
                dve.wait_ge(y2_done, i + 1)
                nc.vector.bn_stats(st[0:TT, k % 2, :], y2[0:TT, k % 2, :]).then_inc(st_done, 1)
                dve.wait_ge(st_done, i + 1)
                through(dve, i, g["passed"])
                nc.vector.bn_aggr(mv[0:TT, k % 2, :], st[0:TT, k % 2, :]).then_inc(mv_done, 1)

            def normalise(i, k):
                dve.wait_ge(rs_done, i + 1)
                reused(dve, h_done, i, 2)
                nc.vector.tensor_scalar(nrm[0:TT, k % 2, :], y2[0:TT, k % 2, :], mv[0:TT, k % 2, 0:1],
                                        rs[0:TT, k % 2, 1:2], ALU.subtract, ALU.mult).then_inc(nrm_done, 1)
            run(dve, NT, U, [(3, heads), (0, convolve), (2, inputs), (2, decayed), (6, normalise), (5, linear_unit),
                             (4, residual)])


class Sparse:

    def __init__(self, g, name, choices, suffix):
        nc = g["nc"]
        self.name, self.choices, self.suffix = name, choices, suffix
        self.most = -(-IMAGES * TOK // BLOCK)
        self.blocks = (choices * IMAGES * TOK - E) // BLOCK + E
        self.slots = self.blocks * BLOCK
        self.x_slots = nc.dram_tensor(name + "_x_slots", (self.slots + choices * 128, D), F32, kind="Internal").ap()
        self.y_slots = nc.dram_tensor(name + "_y_slots", (self.slots, D), F32, kind="Internal").ap()
        self.g = g
        g["zeroed"] = self.zeroed = g.get("zeroed", 0) + self.blocks

    def allocate(self, c):
        sb, n = self.g["sb"], self.name
        self.x = sb(n + "_x", [128, NT, D], c=c)
        self.hits = [sb(f"{n}_hit{j}", [128, NT, E], c=c) for j in range(self.choices)]
        self.scores = [sb(f"{n}_score{j}", [128, NT], c=c) for j in range(self.choices)]
        self.to = [sb(f"{n}_to{j}", [128, NT], mybir.dt.uint32, c=c) for j in range(self.choices)]
        self.fro = [sb(f"{n}_fro{j}", [128, NT], mybir.dt.uint32, c=c) for j in range(self.choices)]
        self.expert = sb(n + "_expert", [128, self.blocks], mybir.dt.int32, c=c)

    def place(self, g):
        nc, a, sb, pb, sem = (g[k] for k in ("nc", "a", "sb", "pb", "sem"))
        n, NB, MJ, C = self.name + "_", self.blocks, self.most, self.choices
        with ExitStack() as c:
            valid = sb(n + "valid", [128, NT], c=c)
            trash = sb(n + "trash", [128, C, NT], c=c)
            numbers = sb(n + "numbers", [128, NB + 1], c=c)
            before = sb(n + "before", [128, TT], c=c)
            ones = sb(n + "ones", [128, TT], c=c)
            earlier = sb(n + "earlier", [128, E, E], c=c)
            both = sb(n + "both", [128, NT, E], c=c)
            rank = sb(n + "rank", [128, NT, E], c=c)
            picked = sb(n + "picked", [128, NT, E], c=c)
            slot = sb(n + "slot", [128, NT], c=c)
            count = sb(n + "count", [128, E], c=c)
            above = sb(n + "above", [128, E, MJ], c=c)
            nblocks = sb(n + "nblocks", [128, E], c=c)
            prior = sb(n + "prior", [128, E, E], c=c)
            first = sb(n + "first", [128, E], c=c)
            end = sb(n + "end", [128, E], c=c)
            passed = sb(n + "ended", [128, NB, E], c=c)
            owner = sb(n + "owner", [128, NB], c=c)
            psR = pb(n + "psRank", [128, 512], c=c)
            psN = pb(n + "psCount", [128, 512], c=c)
            consts_in = sem(n + "consts_in", c)
            both_done = sem(n + "both_done", c)
            rank_filled = sem(n + "rank_filled", c)
            chain = sem(n + "place_chain", c)
            block = c.enter_context(nc.Block())
            loads = [(valid[0:TT, :], a["valid"]), (trash[0:TT, :, :], a["trash" + self.suffix]),
                     (numbers[0:TT, :], a["numbers"][:, 0:NB + 1]), (before[0:TT, :], a["before"]),
                     (ones[0:TT, :], a["ones"]), (earlier[0:TT, :, :], a["earlier"])]

            @block.sync
            def _(sp):
                for dst, src in loads:
                    sp.dma_start(dst, src).then_inc(consts_in, 16)

            @block.tensor
            def _(pe):
                pe.wait_ge(both_done, 1)
                for j in range(NT - 1):
                    nc.tensor.matmul(psR[0:TT, (j + 1) * E:NT * E], ones[0:TT, :],
                                     both[0:TT, j, :].unsqueeze(1).broadcast_to([TT, NT - 1 - j, E]),
                                     start=j == 0, stop=False)
                nc.tensor.matmul(psR[0:TT, E:NT * E], before[0:TT, :], both[0:TT, 1:NT, :], start=False, stop=True)
                nc.tensor.matmul(psR[0:TT, 0:E], before[0:TT, :], both[0:TT, 0, :], start=True, stop=True)
                for j in range(NT):
                    mm = nc.tensor.matmul(psN[0:TT, 0:E], ones[0:TT, :], both[0:TT, j, :],
                                          start=j == 0, stop=j == NT - 1)
                mm.then_inc(rank_filled, 1)

            @block.vector
            def _(dve):
                link = linker(dve, chain)
                wide = [TT, NT, E]
                dve.wait_ge(consts_in, 16 * len(loads))
                for hit in self.hits:
                    link(nc.vector.tensor_tensor(hit[0:TT], hit[0:TT], valid[0:TT].unsqueeze(2).broadcast_to(wide),
                                                 ALU.mult))
                other = self.hits[1] if C == 2 else None
                if other is None:
                    link(nc.vector.tensor_scalar(both[0:TT], self.hits[0][0:TT], 0.0, None, ALU.add))
                else:
                    link(nc.vector.tensor_tensor(both[0:TT], self.hits[0][0:TT], other[0:TT], ALU.add))
                dve.sem_inc(both_done, 1)
                dve.wait_ge(rank_filled, 1)
                link(nc.vector.tensor_scalar(count[0:TT], psN[0:TT, 0:E], 0.0, None, ALU.add))
                link(nc.vector.tensor_scalar(prior[0:TT, 0, :], count[0:TT], 1.0 / BLOCK, None, ALU.mult))
                link(nc.vector.tensor_tensor(above[0:TT], prior[0:TT, 0, :].unsqueeze(2).broadcast_to([TT, E, MJ]),
                                             numbers[0:TT, 0:MJ].unsqueeze(1).broadcast_to([TT, E, MJ]), ALU.is_gt))
                link(nc.vector.tensor_reduce(nblocks[0:TT], above[0:TT], AX.X, ALU.add))
                link(nc.vector.tensor_tensor(prior[0:TT], earlier[0:TT],
                                             nblocks[0:TT].unsqueeze(1).broadcast_to([TT, E, E]), ALU.mult))
                link(nc.vector.tensor_reduce(first[0:TT], prior[0:TT], AX.X, ALU.add))
                link(nc.vector.tensor_tensor(end[0:TT], first[0:TT], nblocks[0:TT], ALU.add))
                link(nc.vector.tensor_tensor(passed[0:TT], end[0:TT].unsqueeze(1).broadcast_to([TT, NB, E]),
                                             numbers[0:TT, 0:NB].unsqueeze(2).broadcast_to([TT, NB, E]), ALU.is_le))
                link(nc.vector.tensor_reduce(owner[0:TT], passed[0:TT], AX.X, ALU.add))
                link(nc.vector.tensor_scalar(owner[0:TT], owner[0:TT], E - 1.0, None, ALU.min))
                link(nc.vector.tensor_copy(self.expert[0:TT], owner[0:TT]))
                link(nc.vector.tensor_scalar(first[0:TT], first[0:TT], float(BLOCK), None, ALU.mult))
                link(nc.vector.tensor_tensor(rank[0:TT], psR[0:TT, 0:NT * E].rearrange("p (i e) -> p i e", i=NT),
                                             first[0:TT].unsqueeze(1).broadcast_to(wide), ALU.add))
                for j in range(C):
                    link(nc.vector.tensor_tensor(picked[0:TT], self.hits[j][0:TT], rank[0:TT], ALU.mult))
                    link(nc.vector.tensor_reduce(slot[0:TT], picked[0:TT], AX.X, ALU.add))
                    link(nc.vector.tensor_copy(self.fro[j][0:TT], slot[0:TT]))
                    link(nc.vector.tensor_tensor(slot[0:TT], slot[0:TT], trash[0:TT, j, :], ALU.add))
                    link(nc.vector.tensor_copy(self.to[j][0:TT], slot[0:TT]))

    def experts(self, g):
        nc, a, sb, pb, sem, h, ident = (g[k] for k in ("nc", "a", "sb", "pb", "sem", "h", "ident"))
        n, NB, C = self.name + "_", self.blocks, self.choices
        W1, b1, W2, b2 = (a[k + self.suffix] for k in ("W1_", "b1_", "W2_", "b2_"))
        FB = 512 // BLOCK
        NU = KF // FB
        NG = 4
        with ExitStack() as c:
            w1 = sb(n + "w1", [128, 2, KD, F], c=c)
            w2 = sb(n + "w2", [128, 2, KF, D], c=c)
            bias1 = sb(n + "bias1", [128, 2, KF], c=c)
            bias2 = sb(n + "bias2", [128, 2, D], c=c)
            xb = sb(n + "xb", [128, 2, SUB, D], c=c)
            xbT = sb(n + "xbT", [128, 2, KD, BLOCK], c=c)
            hid = sb(n + "hid", [128, 2, KF, BLOCK], c=c)
            yb = sb(n + "yb", [128, 2, SUB, D], c=c)
            yg = sb(n + "yg", [128, NG, D], c=c)
            ps1 = pb(n + "ps1", [128, 4, 512], c=c)
            ps2 = pb(n + "ps2", [128, 2, 512], c=c)
            psX = pb(n + "psX", [128, 512], c=c)
            scattered = sem(n + "scattered", c)
            w1_in = [sem(f"{n}w1_in{j}", c) for j in range(2)]
            w2_in = [sem(f"{n}w2_in{j}", c) for j in range(2)]
            xb_in = [sem(f"{n}xb_in{j}", c) for j in range(2)]
            turned = sem(n + "x_turned", c)
            xT_kept = sem(n + "xT_kept", c)
            filled1 = sem(n + "filled1", c)
            kept1 = sem(n + "kept1", c)
            filled2 = sem(n + "filled2", c)
            kept2 = sem(n + "kept2", c)
            stored = [sem(f"{n}stored{j}", c) for j in range(2)]
            fetched = [sem(f"{n}fetched{j}", c) for j in range(NG)]
            added = sem(n + "added", c)
            block = c.enter_context(nc.Block())

            def since(b, k, one):
                return (b - k % 2) * (one // 2) + one

            @block.gpsimd
            def _(pool):
                pool.wait_ge(g["slots_zeroed"], 16 * self.zeroed)
                for i in range(NT):
                    for j in range(C):
                        pool.indirect_dma_start(self.x_slots, bass.IndirectOffsetOnAxis(ap=self.to[j][0:TT, i:i + 1], axis=0),
                                                self.x[0:TT, i, :], None).then_inc(scattered, 16)
                pool.wait_ge(scattered, 16 * NT * C)

                def load_x(b, k):
                    s = k % 2
                    reused(pool, turned, b, 2)
                    through(pool, b, g["passed"])
                    rows = self.x_slots[b * BLOCK:(b + 1) * BLOCK, :] if isinstance(b, int) \
                        else self.x_slots[bass.ds(b * BLOCK, BLOCK), :]
                    pool.dma_start(xb[:, s, :, :], rows.rearrange("(j p) d -> p j d", p=128)).then_inc(xb_in[s], 16)
                run(pool, NB, 2, [(0, load_x)])
                pool.wait_ge(stored[0], 16 * (NB - NB // 2))
                pool.wait_ge(stored[1], 16 * (NB // 2))
                for i in range(NT):
                    for j in range(C):
                        m = i * C + j
                        if m >= NG:
                            pool.wait_ge(added, m - NG + 1)
                        pool.indirect_dma_start(yg[0:TT, m % NG, :], None, self.y_slots,
                                                bass.IndirectOffsetOnAxis(ap=self.fro[j][0:TT, i:i + 1], axis=0))\
                            .then_inc(fetched[m % NG], 16)

            @block.sync
            def _(sp):
                def expert_of(b):
                    at = slice(b, b + 1) if isinstance(b, int) else bass.ds(b, 1)
                    return sp.value_load(self.expert[0:1, at], min_val=0, max_val=E - 1)

                def load1(b, k):
                    s = k % 2
                    e = expert_of(b)
                    reused(sp, kept1, b, 2, NU, 0)
                    sp.dma_start(w1[:, s, :, :], W1[e]).then_inc(w1_in[s], 16)
                    sp.dma_start(bias1[:, s, :], b1[e]).then_inc(w1_in[s], 16)

                def load2(b, k):
                    s = k % 2
                    e = expert_of(b)
                    reused(sp, kept2, b, 2, SUB, 0)
                    sp.dma_start(w2[:, s, :, :], W2[e]).then_inc(w2_in[s], 16)
                    sp.dma_start(bias2[:, s, :], b2[e].unsqueeze(0).broadcast_to([128, D])).then_inc(w2_in[s], 16)
                run(sp, NB, 2, [(0, load1), (1, load2)])

            @block.tensor
            def _(pe):
                def turn(b, k):
                    s = k % 2
                    pe.wait_ge(xb_in[s], since(b, k, 16))
                    reused(pe, xT_kept, b, 1)
                    for j in range(SUB):
                        for kc in range(KD):
                            at = kc * BLOCK + j * 128
                            mm = nc.tensor.transpose(psX[:, at:at + 128], xb[:, s, j, kc * 128:(kc + 1) * 128],
                                                     ident[:, :])
                    mm.then_inc(turned, 1)

                def up(b, k):
                    s = k % 2
                    pe.wait_ge(xT_kept, b + 1)
                    pe.wait_ge(w1_in[s], since(b, k, 32))
                    for u in range(NU):
                        reused(pe, kept1, b, 4 // NU, NU, u - NU + 1)
                        for q in range(FB):
                            f = u * FB + q
                            for kc in range(KD):
                                mm = nc.tensor.matmul(ps1[:, (s * NU + u) % 4, q * BLOCK:(q + 1) * BLOCK],
                                                      w1[:, s, kc, f * 128:(f + 1) * 128], xbT[:, s, kc, :],
                                                      start=kc == 0, stop=kc == KD - 1)
                        mm.then_inc(filled1, 1)

                def down(b, k):
                    s = k % 2
                    pe.wait_ge(kept1, b * NU + NU)
                    pe.wait_ge(w2_in[s], since(b, k, 32))
                    for j in range(SUB):
                        reused(pe, kept2, b, 2 // SUB, SUB, j - SUB + 1)
                        for f in range(KF):
                            mm = nc.tensor.matmul(ps2[:, (s * SUB + j) % 2, 0:D], hid[:, s, f, j * 128:(j + 1) * 128],
                                                  w2[:, s, f, :], start=f == 0, stop=f == KF - 1)
                        mm.then_inc(filled2, 1)
                run(pe, NB, 2, [(0, turn), (1, up), (2, down)])

            @block.scalar
            def _(act):
                def keep_xT(b, k):
                    act.wait_ge(turned, b + 1)
                    reused(act, filled1, b, 2, NU, 0)
                    nc.scalar.activation(xbT[:, k % 2, :, :],
                                         psX[:, 0:KD * BLOCK].rearrange("p (c t) -> p c t", c=KD), ACT.Copy)\
                        .then_inc(xT_kept, 1)

                def activate(b, k):
                    s = k % 2
                    act.wait_ge(w1_in[s], since(b, k, 32))
                    reused(act, filled2, b, 2, SUB, 0)
                    for u in range(NU):
                        act.wait_ge(filled1, b * NU + u + 1)
                        for q in range(FB):
                            f = u * FB + q
                            ins = nc.scalar.activation(hid[:, s, f, :],
                                                       ps1[:, (s * NU + u) % 4, q * BLOCK:(q + 1) * BLOCK],
                                                       ACT.Silu, bias=bias1[:, s, f:f + 1])
                        ins.then_inc(kept1, 1)

                def store_y(b, k):
                    s = k % 2
                    act.wait_ge(kept2, b * SUB + SUB)
                    rows = self.y_slots[b * BLOCK:(b + 1) * BLOCK, :] if isinstance(b, int) \
                        else self.y_slots[bass.ds(b * BLOCK, BLOCK), :]
                    act.dma_start(rows.rearrange("(j p) d -> p j d", p=128), yb[:, s, :, :]).then_inc(stored[s], 16)
                run(act, NB, 2, [(0, keep_xT), (1, activate), (3, store_y)])

            @block.vector
            def _(dve):
                def keep_y(b, k):
                    s = k % 2
                    dve.wait_ge(w2_in[s], since(b, k, 32))
                    if not (isinstance(b, int) and b < 2):
                        dve.wait_ge(stored[s], since(b, k, 16) - 16)
                    for j in range(SUB):
                        dve.wait_ge(filled2, b * SUB + j + 1)
                        nc.vector.tensor_tensor(yb[:, s, j, :], ps2[:, (s * SUB + j) % 2, 0:D], bias2[:, s, :], ALU.add)\
                            .then_inc(kept2, 1)
                run(dve, NB, 2, [(2, keep_y)])
                for i in range(NT):
                    for j in range(C):
                        m = i * C + j
                        dve.wait_ge(fetched[m % NG], 16 * (m // NG + 1))
                        if j:
                            dve.wait_ge(added, m)
                        nc.vector.scalar_tensor_tensor(out=h[0:TT, i, :], in0=yg[0:TT, m % NG, :],
                                                       scalar=self.scores[j][0:TT, i:i + 1], in1=h[0:TT, i, :],
                                                       op0=ALU.mult, op1=ALU.add).then_inc(added, 1)


def store(g, out):
    nc, h, sem = g["nc"], g["h"], g["sem"]
    with ExitStack() as c:
        stored = sem("stored", c)
        block = c.enter_context(nc.Block())
        flat = out.rearrange("b t d -> (b t) d")
        whole = IMAGES * TOK // TT
        rest = IMAGES * TOK - whole * TT

        @block.sync
        def _(sp):
            sp.dma_start(flat[0:whole * TT, :].rearrange("(n p) d -> p n d", p=TT), h[0:TT, 0:whole, :])\
                .then_inc(stored, 16)
            sp.dma_start(flat[whole * TT:, :], h[0:rest, whole, :]).then_inc(stored, 16)
            sp.wait_ge(stored, 32)


def host_arrays(v):
    x = np.asarray(v["x"])
    side = 6
    p = x.reshape(IMAGES, 3, side, 16, side, 16).transpose(1, 3, 5, 0, 2, 4).reshape(PATCH, IMAGES, side * side)
    pt = np.zeros((PATCH, NT * PER, TOK), x.dtype)
    pt[:, :IMAGES, 1:] = p
    pt = pt.reshape(KP, 128, NT, TT).transpose(1, 2, 0, 3)
    rows = np.asarray(v["L0_tok_b"])[None].repeat(TOK, 0)
    rows[0] = np.asarray(v["L0_tok_cls_token"])[0, 0]

    def bc(name):
        return np.asarray(v[name]).reshape(1, -1).repeat(TT, 0)

    tok = np.arange(TT)
    same = tok[:, None] // TOK == tok[None] // TOK
    mask = np.where(same & (tok[None] <= tok[:, None]), 0.0, MASKED).astype(np.float32)
    valid = ((np.arange(NT)[None] * TT + tok[:, None]) < IMAGES * TOK).astype(np.float32)

    def chunked(w):
        w = np.asarray(w)
        return w.reshape(E, w.shape[1] // 128, 128, w.shape[2]).transpose(0, 2, 1, 3)

    def trash(layer, choices):
        slots = ((choices * IMAGES * TOK - E) // BLOCK + E) * BLOCK
        row = slots + np.arange(choices)[None, :, None] * 128 + tok[:, None, None]
        return (row * (1 - valid[:, None, :])).astype(np.float32)

    a = {
        "patchesT": pt,
        "tok_WT": np.asarray(v["L0_tok_W"]).T,
        "cls_or_b": np.tile(rows, (PER, 1)),
        "pos": np.tile(np.asarray(v["L0_tok_pos_embedding"])[0], (PER, 1)),
        "ident": np.eye(128, dtype=np.float32),
        "mask4": np.tile(mask, (1, 4)),
        "bo": bc("L0_attn_bo"),
        "ffn_rms_w": bc("L0_ffn_rms_w"),
        "gate_wT": np.asarray(v["L0_ffn_gate_w"]).T,
        "number_less_e": np.tile(np.arange(E, dtype=np.float32) - E, (TT, 1)),
        "W1_0": chunked(v["L0_ffn_W1"]), "W2_0": chunked(v["L0_ffn_W2"]), "b2_0": np.asarray(v["L0_ffn_b2"]),
        "b1_0": np.asarray(v["L0_ffn_b1"]).reshape(E, KF, 128).transpose(0, 2, 1),
        "W1_1": chunked(v["L1_ffn_we1"]), "W2_1": chunked(v["L1_ffn_we2"]), "b2_1": np.asarray(v["L1_ffn_be2"]),
        "b1_1": np.asarray(v["L1_ffn_be1"]).reshape(E, KF, 128).transpose(0, 2, 1),
        "W_in": np.asarray(v["L1_attn_W_in"]), "W_out": np.asarray(v["L1_attn_W_out"]),
        "glu_w": np.asarray(v["L1_attn_glu_w"]), "glu_b": bc("L1_attn_glu_b"),
        "conv_w": np.asarray(v["L1_attn_conv_w"]).reshape(KC, 128, 4).transpose(1, 0, 2),
        "conv_b": np.asarray(v["L1_attn_conv_b"]).reshape(KC, 128).T,
        "m_rms_w": np.asarray(v["L1_attn_rms_w"]).reshape(DI // 128, 128).T,
        "D_skip": bc("L1_attn_D_skip"), "dt_bias": bc("L1_attn_dt_bias"), "A_log": bc("L1_attn_A_log"),
        "ln_w": bc("L1_attn_ln_w"), "ln_b": bc("L1_attn_ln_b"),
        "after": (tok[:, None] > tok[None]).astype(np.float32),
        "upto": (tok[:, None] <= tok[None]).astype(np.float32),
        "causal": (same & (tok[:, None] <= tok[None])).astype(np.float32),
        "valid": valid,
        "trash0": trash(0, 1), "trash1": trash(1, 2),
        "numbers": np.tile(np.arange(64, dtype=np.float32), (TT, 1)),
        "before": (tok[:, None] < tok[None]).astype(np.float32),
        "ones": np.ones((TT, TT), np.float32),
        "earlier": np.tile(np.tri(E, k=-1, dtype=np.float32), (TT, 1, 1)),
        "rw1": np.asarray(v["L1_ffn_rw1"]), "rw2": np.asarray(v["L1_ffn_rw2"]), "rb2": bc("L1_ffn_rb2"),
        "rb1": np.asarray(v["L1_ffn_rb1"]).reshape(KD, 128).T,
    }
    for w in ("Wq", "Wk", "Wv", "Wo"):
        a[w] = np.asarray(v["L0_attn_" + w])
    return a



def kernel(**inputs):
    import concourse.bacc as _bacc
    from concourse.bass_utils import run_bass_kernel_spmd as _run

    nc = _bacc.Bacc("TRN2", target_bir_lowering=False, num_devices=1)
    arrays, args = {}, {}
    for name, arr in host_arrays(inputs).items():
        arr = np.ascontiguousarray(arr)
        arrays[f"in_{name}"] = arr
        args[name] = nc.dram_tensor(f"in_{name}", arr.shape, mybir.dt.from_np(arr.dtype), kind="ExternalInput").ap()
    out = nc.dram_tensor("out_0", (IMAGES, TOK, D), F32, kind="ExternalOutput").ap()
    build(nc, args, out)
    r = _run(nc, [arrays], core_ids=[0])
    return r.results[0]["out_0"]
```

```python
from contextlib import ExitStack

import numpy as np
import concourse.bass as bass
from concourse import mybir

ALU = mybir.AluOpType
ACT = mybir.ActivationFunctionType
AX = mybir.AxisListType
F32 = mybir.dt.float32
BF16 = mybir.dt.bfloat16
F32R = mybir.dt.float32r

IMAGES, TOK, D = 64, 37, 256
PER = 3
TT = PER * TOK
NT = -(-IMAGES // PER)
NTOK = NT * TT
CUTS = ((0, 96), (96, TT))
KD = D // 128
PATCH = 3 * 16 * 16
KP = PATCH // 128
HEADS, HD = 16, 64
INNER = HEADS * HD
KI = INNER // 128
E = 8
F = 1024
KF = F // 128
DI, DS, MH = 512, 128, 8
CONV = DI + 2 * DS
KC = CONV // 128
BLOCK = 128
SUB = BLOCK // 128
MASKED = -8.0e9


def run(eng, n, unroll, stages, head=0):
    longest = max(lag for lag, _ in stages)
    head = max(longest + unroll, head)
    while head < n and (n - head) % unroll:
        head += 1

    def step(t, phase):
        for lag, fn in stages:
            if not isinstance(t, int) or 0 <= t - lag < n:
                fn(t - lag, (phase - lag) % unroll)

    for t in range(min(head, n)):
        step(t, t)
    if head < n:
        with eng.Fori(head, n - unroll + 1, unroll) as t0:
            for k in range(unroll):
                step(t0 + k, head + k)
    for t in range(n, n + longest):
        step(t, t)


def reused(eng, sem, i, depth, per=1, extra=0):
    if isinstance(i, int) and i < depth:
        return
    eng.wait_ge(sem, (i - depth + 1) * per + extra)


def through(eng, i, passed):
    if not isinstance(i, int):
        eng.sem_inc(passed, 1)


def build(nc, a, out):
    with ExitStack() as ctx:
        def sb(name, shape, dt=F32, c=ctx):
            return c.enter_context(nc.sbuf_tensor(name, shape, dt))

        def pb(name, shape, dt=F32, c=ctx):
            return c.enter_context(nc.psum_tensor(name, shape, dt))

        phases = {}

        def clear(sems):
            nc.clear_and_free_semaphores(sems)
            nc.all_engine_barrier()

        def sem(name, c=None):
            if c is None:
                return ctx.enter_context(nc.semaphore(name))
            if id(c) not in phases:
                phases[id(c)] = []
                c.callback(lambda: clear(phases.pop(id(c))))
            phases[id(c)].append(nc.alloc_semaphore(name))
            return phases[id(c)][-1]

        h = sb("h", [128, NT, D])
        xT = sb("xT", [128, KD, NTOK])
        ident = sb("ident", [128, 128])
        identb = sb("identb", [128, 128], BF16)
        mhalf = sb("mhalf", [128, 1])
        moments = sb("moments", [128, NT, 6])
        epsilon = sb("epsilon", [128, 2])
        loaded = sem("loaded")
        passed = sem("passed")
        g = dict(nc=nc, a=a, sb=sb, pb=pb, sem=sem, h=h, xT=xT, ident=ident, identb=identb, mhalf=mhalf, moments=moments, epsilon=epsilon,
                 passed=passed, loaded=loaded)
        sparse = [Sparse(g, "ffn0", 1, "0"), Sparse(g, "ffn1", 2, "1")]
        small = g["small"] = Loads(g, "small", ctx, [
            ("rms_w", [TT, D], a["ffn_rms_w"]),
            ("gate", [128, KD, E], a["gate_wT"].rearrange("(c p) e -> p c e", p=128)),
            ("less_e", [TT, E], a["number_less_e"]),
            ("rw1", [128, KD, D], a["rw1"].rearrange("(c p) e -> p c e", p=128)),
            ("rw2", [128, KD, E], a["rw2"].rearrange("(c p) e -> p c e", p=128)),
            ("rb1", [128, KD], a["rb1"]),
            ("rb2", [TT, E], a["rb2"]),
            ("wdt", [128, KD, MH], a["W_in"].rearrange("(c p) n -> p c n", p=128)[:, :, DI + CONV:]),
            ("dt_bias", [TT, MH], a["dt_bias"]),
            ("A_log", [TT, MH], a["A_log"]),
            ("valid", [TT, NT], a["valid"]),
            ("token_numbers", [TT, 2, 2, NT], a["token_numbers"]),
            ("numbers", [128, 129], a["numbers"]),
            ("before", [TT, TT], a["before"]),
            ("ones", [TT, TT], a["ones"]),
            ("earlier", [TT, E, E], a["earlier"]),
            ("spare0", [128, sparse[0].groups], a["spare0"]),
            ("spare1", [128, sparse[1].groups], a["spare1"])])
        with ExitStack() as c:
            weights = attention_weights(g, c)
            split = Split(g, c)
            embed(g, small, weights, split)
            attention(g, weights, split)
        with ExitStack() as outer:
            weights = mamba_weights(g, outer)
            with ExitStack() as c:
                ffn = sparse[0]
                ffn.allocate(c)
                route_top1(g, ffn, weights)
                ffn.place(g)
                ffn.experts(g)
            mamba(g, weights)
        with ExitStack() as c:
            ffn = sparse[1]
            ffn.allocate(c)
            route_top2(g, ffn)
            ffn.place(g)
            ffn.experts(g, out)


class Loads:

    def __init__(self, g, name, c, parts):
        self.g = g
        self.parts = [(g["sb"](n, [128] + shape[1:], c=c)[0:shape[0]], src) for n, shape, src in parts]
        self.buffers = {n: buffer for (n, _, _), (buffer, _) in zip(parts, self.parts)}
        self.landed = g["sem"](name + "_landed")

    def issue(self, eng, lo=0, hi=None):
        for dst, src in self.parts[lo:hi]:
            eng.dma_start(dst, src).then_inc(self.landed, 16)

    def wait(self, eng):
        eng.wait_ge(self.landed, 16 * len(self.parts))

    def __getitem__(self, name):
        return self.buffers[name]


class Moments:

    def __init__(self, g, c, name):
        self.g = g
        self.done = g["sem"](name + "_done", c)

    def of(self, dve, i, k, h_ready):
        dve.wait_ge(h_ready, i + 1)
        self.take(dve, i)

    def take(self, dve, i):
        through(dve, i, self.g["passed"])
        self.g["nc"].vector.bn_stats(self.g["moments"][0:TT, i, :], self.g["h"][0:TT, i, :]).then_inc(self.done, 1)


class LayerNorm:

    SLOTS = 4

    def __init__(self, g, c, name, slots=False, known=False):
        self.g = g
        self.known = known
        sb, pb, sem = g["sb"], g["pb"], g["sem"]
        if known:
            self.mv = sb(name + "_mv", [128, NT, 2], c=c)
            self.rstd = sb(name + "_rstd", [128, 2, NT], c=c)
        else:
            self.stats = sb(name + "_stats", [128, 2, 6], c=c)
            self.mv = sb(name + "_mv", [128, 2, 2], c=c)
            self.rstd = sb(name + "_rstd", [128, 2, 2], c=c)
        self.xn = sb(name + "_xn", [128, self.SLOTS, D], c=c)
        self.psT = pb(name + "_psT", [128, 2, 512], c=c)
        self.stats_done = sem(name + "_stats_done", c)
        self.mv_done = sem(name + "_mv_done", c)
        self.rstd_done = sem(name + "_rstd_done", c)
        self.xn_done = sem(name + "_xn_done", c)
        self.turned = sem(name + "_turned", c)
        self.kept = sem(name + "_kept", c)
        if slots:
            self.xs = sb(name + "_xs", [128, 2, KD, TT], c=c)
            self.xs_kept = sem(name + "_xs_kept", c)

    def statistics(self, dve, i, k, h_ready=None):
        nc, h = self.g["nc"], self.g["h"]
        if h_ready is not None:
            dve.wait_ge(h_ready, i + 1)
        through(dve, i, self.g["passed"])
        nc.vector.bn_stats(self.stats[0:TT, k % 2, :], h[0:TT, i, :]).then_inc(self.stats_done, 1)
        dve.wait_ge(self.stats_done, i + 1)
        reused(dve, self.xn_done, i, 2)
        through(dve, i, self.g["passed"])
        nc.vector.bn_aggr(self.mv[0:TT, k % 2, :], self.stats[0:TT, k % 2, :]).then_inc(self.mv_done, 1)

    def inverse(self, pool, i, k):
        nc = self.g["nc"]
        pool.wait_ge(self.mv_done, i + 1)
        reused(pool, self.xn_done, i, 2)
        nc.gpsimd.tensor_tensor(self.rstd[0:TT, k % 2, 0:1], self.mv[0:TT, k % 2, 1:2],
                                self.g["epsilon"][0:TT, 0:1], ALU.add).then_inc(self.rstd_done, 1)
        pool.wait_ge(self.rstd_done, i * 2 + 1)
        nc.gpsimd.tensor_tensor(self.rstd[0:TT, k % 2, 1:2], self.rstd[0:TT, k % 2, 0:1],
                                self.g["mhalf"][0:TT, :], ALU.pow).then_inc(self.rstd_done, 1)

    def aggregate_all(self, dve):
        for i in range(NT):
            self.g["nc"].vector.bn_aggr(self.mv[0:TT, i, :], self.g["moments"][0:TT, i, :]).then_inc(self.mv_done, 1)

    def inverse_all(self, pool):
        nc = self.g["nc"]
        for n, (lo, hi) in enumerate(((0, self.SLOTS), (self.SLOTS, NT))):
            wide = [TT, hi - lo]
            pool.wait_ge(self.mv_done, hi)
            nc.gpsimd.tensor_tensor(self.rstd[0:TT, 0, lo:hi], self.mv[0:TT, lo:hi, 1],
                                    self.g["epsilon"][0:TT, 0:1].broadcast_to(wide), ALU.add)\
                .then_inc(self.rstd_done, 1)
            pool.wait_ge(self.rstd_done, 2 * n + 1)
            nc.gpsimd.tensor_tensor(self.rstd[0:TT, 1, lo:hi], self.rstd[0:TT, 0, lo:hi],
                                    self.g["mhalf"][0:TT, :].broadcast_to(wide), ALU.pow).then_inc(self.rstd_done, 1)

    def normalise(self, dve, i, k):
        nc, h = self.g["nc"], self.g["h"]
        if self.known:
            at = slice(i, i + 1) if isinstance(i, int) else bass.ds(i, 1)
            mean, rstd = self.mv[0:TT, i, 0:1], self.rstd[0:TT, 1, at]
            dve.wait_ge(self.rstd_done, 2 if isinstance(i, int) and i < self.SLOTS else 4)
        else:
            mean, rstd = self.mv[0:TT, k % 2, 0:1], self.rstd[0:TT, k % 2, 1:2]
            dve.wait_ge(self.rstd_done, i * 2 + 2)
            dve.wait_ge(self.mv_done, i + 1)
        reused(dve, self.turned, i, self.SLOTS)
        nc.vector.tensor_scalar(self.xn[0:TT, k, :], h[0:TT, i, :], mean, rstd,
                                ALU.subtract, ALU.mult).then_inc(self.xn_done, 1)

    def turn(self, pe, i, k, ready=None, src=None):
        nc = self.g["nc"]
        pe.wait_ge(ready or self.xn_done, i + 1)
        reused(pe, self.kept, i, 2)
        src = self.xn[0:TT, k, :] if src is None else src
        for c in range(KD):
            mm = nc.tensor.transpose(self.psT[:, k % 2, c * TT:(c + 1) * TT], src[:, c * 128:(c + 1) * 128],
                                     self.g["ident"][0:TT, 0:TT])
        mm.then_inc(self.turned, 1)

    def keep(self, act, i, k):
        nc, xT = self.g["nc"], self.g["xT"]
        act.wait_ge(self.turned, i + 1)
        through(act, i, self.g["passed"])
        nc.scalar.activation(xT[:, :, cols(i)], self.psT[:, k % 2, 0:KD * TT].rearrange("p (c t) -> p c t", c=KD),
                             ACT.Copy).then_inc(self.kept, 1)


    def keep_stationary(self, act, i, k, used, last=False):
        act.wait_ge(self.turned, i + 1)
        reused(act, used, i, 2)
        self.g["nc"].scalar.activation(self.xs[:, k % 2, :, :],
                                       self.psT[:, k % 2, 0:KD * TT].rearrange("p (c t) -> p c t", c=KD),
                                       ACT.Copy).then_inc(self.kept if last else self.xs_kept, 1)


def cols(i, n=1):
    return slice(i * TT, i * TT + n * TT) if isinstance(i, int) else bass.ds(i * TT, n * TT)


class Split:

    NAMES = ("Wq", "Wk", "Wv", "Wo")

    def __init__(self, g, c):
        self.g = g
        self.high, self.low = ({w: g["sb"](f"{w}_{part}", self.shape(w), F32R, c=c) for w in self.NAMES}
                               for part in ("high", "low"))
        self.high_done = g["sem"]("high_done")
        self.low_done = g["sem"]("low_done")

    @staticmethod
    def shape(w):
        return [128, KI, D] if w == "Wo" else [128, KD, INNER]

    def highs(self, raw, at):
        def fn(i, k):
            if isinstance(i, int) and i in range(at, at + len(self.NAMES)):
                w = self.NAMES[i - at]
                self.g["nc"].scalar.activation(self.high[w][:], raw[w], ACT.Copy).then_inc(self.high_done, 1)
        return fn

    def lows(self, dve, raw, at):
        def fn(i, k):
            if isinstance(i, int) and i in range(at, at + len(self.NAMES)):
                w = self.NAMES[i - at]
                dve.wait_ge(self.high_done, i - at + 1)
                self.g["nc"].vector.tensor_tensor(self.low[w][:], raw[w], self.high[w][:].bitcast(F32),
                                                  ALU.subtract).then_inc(self.low_done, 1)
        return fn


def embed(g, small, weights, split):
    nc, a, sb, pb, sem, h, ident = (g[k] for k in ("nc", "a", "sb", "pb", "sem", "h", "ident"))
    loaded = g["loaded"]
    with ExitStack() as c:
        NP = 4
        raw = Loads(g, "qkv", c, [(n + "_raw", Split.shape(n), a[n].rearrange("(c p) n -> p c n", p=128))
                                  for n in Split.NAMES])
        SPLIT_AT = 13
        HEAD = SPLIT_AT + len(Split.NAMES) + 1
        raw_of = {w: raw[w + "_raw"] for w in Split.NAMES}
        wT = sb("tok_wT", [128, KP, D], c=c)
        patches = sb("patches", [128, NP, KP, TT], c=c)
        base = sb("base", [128, D], c=c)
        pos = sb("pos", [128, D], c=c)
        psE = pb("psE", [128, 2, 512], c=c)
        patches_in = [sem(f"patches_in{s}", c) for s in range(NP)]
        mhalf_set = sem("mhalf_set", c)
        base_done = sem("base_done", c)
        embedded = sem("embedded", c)
        h_done = sem("h_done", c)
        ln = LayerNorm(g, c, "ln0")
        block = c.enter_context(nc.Block())

        @block.sync
        def _(sp):
            sp.dma_start(wT[:, :, :], a["tok_WT"].rearrange("(c p) d -> p c d", p=128)).then_inc(loaded, 16)
            sp.dma_start(base[0:TT, :], a["cls_or_b"]).then_inc(loaded, 16)
            sp.dma_start(pos[0:TT, :], a["pos"]).then_inc(loaded, 16)
            sp.dma_start(ident[:, :], a["ident"]).then_inc(loaded, 16)

            def load(i, k):
                reused(sp, embedded, i, NP)
                sp.dma_start(patches[:, k, :, :], a["patchesT"][:, i, :, :]).then_inc(patches_in[k], 16)
            run(sp, NT, NP, [(0, load)])

        @block.tensor
        def _(pe):
            pe.wait_ge(loaded, 64)

            def project(i, k):
                pe.wait_ge(patches_in[k], (i - k) * (16 // NP) + 16)
                reused(pe, h_done, i, 2)
                for kc in range(KP):
                    mm = nc.tensor.matmul(psE[0:TT, k % 2, 0:D], patches[:, k, kc, :], wT[:, kc, :],
                                          start=kc == 0, stop=kc == KP - 1)
                mm.then_inc(embedded, 1)
            run(pe, NT, NP, [(0, project), (3, lambda i, k: ln.turn(pe, i, k))])

        @block.vector
        def _(dve):
            nc.vector.memset(g["mhalf"][:, :], -0.5).then_inc(mhalf_set, 1)
            nc.vector.memset(g["epsilon"][:, 0:1], 1e-5).then_inc(mhalf_set, 1)
            nc.vector.memset(g["epsilon"][:, 1:2], 1e-6).then_inc(mhalf_set, 1)
            dve.wait_ge(loaded, 64)
            nc.vector.tensor_tensor(base[0:TT, :], base[0:TT, :], pos[0:TT, :], ALU.add).then_inc(base_done, 1)
            dve.wait_ge(base_done, 1)
            nc.vector.tensor_copy(g["identb"][:, :], ident[:, :]).then_inc(base_done, 1)

            def add(i, k):
                dve.wait_ge(embedded, i + 1)
                nc.vector.tensor_tensor(h[0:TT, i, :], psE[0:TT, k % 2, 0:D], base[0:TT, :],
                                        ALU.add).then_inc(h_done, 1)
            run(dve, NT, NP, [(0, add), (0, lambda i, k: ln.statistics(dve, i, k, h_done)),
                              (1, lambda i, k: ln.normalise(dve, i, k)), (0, split.lows(dve, raw_of, SPLIT_AT))],
                HEAD)

        @block.gpsimd
        def _(pool):
            pool.wait_ge(mhalf_set, 3)
            run(pool, NT, NP, [(0, lambda i, k: ln.inverse(pool, i, k))])

        @block.scalar
        def _(act):
            def load_ahead(i, k):
                if isinstance(i, int) and i < 2 * len(Split.NAMES) and i % 2 == 0:
                    act.wait_ge(embedded, i + 1)
                    raw.issue(act, i // 2, i // 2 + 1)
                if isinstance(i, int) and i == 2 * len(Split.NAMES):
                    weights.issue(act)
                    small.issue(act)

            def matrices(i, k):
                if isinstance(i, int) and i == SPLIT_AT:
                    raw.wait(act)
            run(act, NT, NP, [(3, lambda i, k: ln.keep(act, i, k)), (0, load_ahead), (0, matrices),
                              (0, split.highs(raw_of, SPLIT_AT))], HEAD)


def attention_weights(g, c):
    a = g["a"]
    return Loads(g, "attn", c, [("bo", [TT, D], a["bo"]), ("mask_f32", [TT, 4 * TT], a["mask4"])])


def attention(g, weights, split):
    nc, a, sb, pb, sem, h, xT, ident = (g[k] for k in ("nc", "a", "sb", "pb", "sem", "h", "xT", "ident"))
    identb = g["identb"]
    U = 4
    with ExitStack() as c:
        bo, mask_f32 = (weights[n] for n in ("bo", "mask_f32"))
        mask = sb("mask", [128, 4 * TT], BF16, c=c)
        xh, xl = (sb(n, [128, 2, KD, 2 * TT], F32R, c=c) for n in ("xh", "xl"))
        qk = sb("qk", [128, 2, 2 * KI, 2 * TT], c=c)
        v = sb("v", [128, 2, INNER], c=c)
        s = sb("s", [128, 2, HEADS, TT], c=c)
        pT = sb("pT", [128, HEADS, TT], c=c)
        oTh, oTl = (sb(n, [128, 2, KI, TT], F32R, c=c) for n in ("oTh", "oTl"))
        top = sb("top", [128, 2, HEADS], c=c)
        total = sb("total", [128, 2, HEADS], c=c)
        inv = sb("inv", [128, 2, HEADS], c=c)
        psS = pb("psS", [128, 2, 2, 512], c=c)
        psP = pb("psP", [128, 2, 512], c=c)
        psT = pb("psT", [128, 512], c=c)
        psO = pb("psO", [128, 512], c=c)
        xh_done = sem("xh_done", c)
        xl_done = sem("xl_done", c)
        mask_done = sem("mask_done", c)
        proj_filled = sem("proj_filled", c)
        proj_freed = sem("proj_freed", c)
        scores_done = sem("scores_done", c)
        top_done = sem("top_done", c)
        shifted = sem("shifted", c)
        exp_done = sem("exp_done", c)
        total_done = sem("total_done", c)
        inv_done = sem("inv_done", c)
        prob_done = sem("prob_done", c)
        pT_filled = sem("pT_filled", c)
        pT_kept = sem("pT_kept", c)
        oT_filled = sem("oT_filled", c)
        oT_kept = sem("oT_kept", c)
        oT_rest = sem("oT_rest", c)
        wo_done = sem("wo_done", c)
        h_done = sem("attn_h_done", c)
        moments = Moments(g, c, "attn_moments")
        h_bias = sem("attn_h_bias", c)
        block = c.enter_context(nc.Block())

        def v_unit(i, k, n):
            if k % 2 == 0:
                return i * 6 + 8 + n
            return i * 6 + 12 + n - (8 if isinstance(i, int) and i == NT - 1 else 0)

        def qk_unit(t, n):
            return n if isinstance(t, int) and t == 0 else t * 6 - 2 + n

        @block.gpsimd
        def _(pool):
            def split_pair(t, k):
                if k % 2:
                    return
                s = (k // 2) % 2
                if not (isinstance(t, int) and t < 4):
                    pool.wait_ge(proj_filled, t * 6 - 4)
                through(pool, t, g["passed"])
                nc.gpsimd.tensor_copy(xh[:, s, :, :], xT[:, :, cols(t, 2)]).then_inc(xh_done, 2)
                pool.wait_ge(xh_done, t + 2)
                through(pool, t, g["passed"])
                nc.gpsimd.tensor_tensor(xl[:, s, :, :], xT[:, :, cols(t, 2)], xh[:, s, :, :].bitcast(F32),
                                        ALU.subtract).then_inc(xl_done, 2)
            run(pool, NT, U, [(0, split_pair)])

        @block.tensor
        def _(pe):
            weights.wait(pe)
            pe.wait_ge(mask_done, 1)

            pe.wait_ge(split.low_done, len(Split.NAMES))

            def free_unit(u):
                if not (isinstance(u, int) and u < 2):
                    pe.wait_ge(proj_freed, u - 1)

            def product(out, lhs, rhs, chunks=KD):
                for kc in range(chunks):
                    (lh, ll), (rh, rl) = lhs(kc), rhs(kc)
                    for n, (p, q) in enumerate(((lh, rh), (lh, rl), (ll, rh))):
                        mm = nc.tensor.matmul(out, p, q, start=kc + n == 0, stop=kc == chunks - 1 and n == 2)
                return mm

            def values(n):
                def fn(i, k):
                    free_unit(v_unit(i, k, n))
                    at = slice((k % 2) * TT, (k % 2 + 1) * TT)
                    product(psP[0:TT, n % 2, :],
                            lambda kc: [x[:, (k // 2) % 2, kc, at] for x in (xh, xl)],
                            lambda kc: [w["Wv"][:, kc, n * 512:(n + 1) * 512] for w in (split.high, split.low)])\
                        .then_inc(proj_filled, 1)
                return fn

            def queries_keys(t, k):
                if k % 2:
                    return
                pe.wait_ge(xh_done, t + 2)
                pe.wait_ge(xl_done, t + 2)
                for n in range(8):
                    free_unit(qk_unit(t, n))
                    for half in range(2):
                        ch = 2 * n + half
                        w = Split.NAMES[ch // KI]
                        at = slice((ch % KI) * 128, (ch % KI + 1) * 128)
                        mm = product(psP[:, n % 2, half * 2 * TT:(half + 1) * 2 * TT],
                                     lambda kc: [m[w][:, kc, at] for m in (split.high, split.low)],
                                     lambda kc: [x[:, (k // 2) % 2, kc, :] for x in (xh, xl)])
                    mm.then_inc(proj_filled, 1)

            def scores(hf):
                def fn(i, k):
                    pe.wait_ge(proj_freed, qk_unit(i if k % 2 == 0 else i - 1, 7) + 1)
                    reused(pe, shifted, i, 1, 2, hf - 1)
                    for p in range(2):
                        nc.tensor.matmul(psS[0:TT, hf, p, 0:4 * TT], identb[0:TT, 0:TT], mask[0:TT, :],
                                         start=True, stop=False)
                        for j in range(4):
                            ch = hf * 4 + j
                            q = qk[64 * p:64 * p + 64, (k // 2) % 2, ch, (k % 2) * TT:(k % 2 + 1) * TT]
                            kk = qk[64 * p:64 * p + 64, (k // 2) % 2, KI + ch, (k % 2) * TT:(k % 2 + 1) * TT]
                            mm = nc.tensor.matmul(psS[0:TT, hf, p, j * TT:(j + 1) * TT], q, kk,
                                                  start=False, stop=j == 3)
                    mm.then_inc(scores_done, 1)
                return fn

            def turn(q):
                def fn(i, k):
                    pe.wait_ge(prob_done, i * 2 + q // 2 + 1)
                    if q or not isinstance(i, int) or i:
                        pe.wait_ge(pT_kept, i * 4 + q)
                    for j in range(4):
                        mm = nc.tensor.transpose(psT[0:TT, j * TT:(j + 1) * TT], s[0:TT, k % 2, 4 * q + j, :],
                                                 ident[0:TT, 0:TT])
                    mm.then_inc(pT_filled, 1)
                return fn

            def mix(hf):
                def fn(i, k):
                    pe.wait_ge(pT_kept, i * 4 + 2 * hf + 2)
                    if hf == 0:
                        pe.wait_ge(proj_freed, v_unit(i, k, 1) + 1)
                        reused(pe, h_done, i, 1)
                    else:
                        pe.wait_ge(oT_rest, i * 2 + 1)
                    for j in range(4):
                        for p in range(2):
                            head = 2 * (4 * hf + j) + p
                            mm = nc.tensor.matmul(psO[64 * p:64 * p + 64, j * TT:(j + 1) * TT],
                                                  v[0:TT, k % 2, head * HD:(head + 1) * HD],
                                                  pT[0:TT, 8 * hf + 4 * p + j, :], start=True, stop=True)
                    mm.then_inc(oT_filled, 1)
                return fn

            def output(i, k):
                pe.wait_ge(oT_rest, i * 2 + 2)
                product(psO[0:TT, 0:D], lambda ch: [o[:, k % 2, ch, :] for o in (oTh, oTl)],
                        lambda ch: [w["Wo"][:, ch, :] for w in (split.high, split.low)], KI).then_inc(wo_done, 1)

            run(pe, NT, U, [(2, values(0)), (4, output), (3, turn(0)), (2, values(1)), (3, turn(1)), (2, scores(0)),
                            (3, turn(2)), (3, mix(0)), (3, turn(3)), (2, scores(1)), (3, mix(1)),
                            (0, queries_keys)])

        @block.scalar
        def _(act):
            def values(n):
                def fn(t, k):
                    act.wait_ge(proj_filled, v_unit(t, k, n) + 1)
                    reused(act, oT_filled, t, 2, 2)
                    nc.scalar.activation(v[0:TT, k % 2, n * 512:(n + 1) * 512], psP[0:TT, n % 2, :],
                                         ACT.Copy).then_inc(proj_freed, 1)
                return fn

            def queries_keys(lo, hi):
                def fn(t, k):
                    if k % 2:
                        return
                    for n in range(lo, hi):
                        act.wait_ge(proj_filled, qk_unit(t, n) + 1)
                        if n == 0 and not (isinstance(t, int) and t < 4):
                            act.wait_ge(scores_done, (t - 2) * 2)
                        nc.scalar.activation(
                            qk[:, (k // 2) % 2, 2 * n:2 * n + 2, :],
                            psP[:, n % 2, 0:4 * TT].rearrange("p (c t) -> p c t", c=2),
                            ACT.Copy).then_inc(proj_freed, 1)
                return fn

            def keep_pT(q):
                def fn(i, k):
                    act.wait_ge(pT_filled, i * 4 + q + 1)
                    if not (isinstance(i, int) and i < 1):
                        act.wait_ge(oT_filled, (i - 1) * 2 + q // 2 + 1)
                    nc.scalar.activation(pT[0:TT, 4 * q:4 * q + 4, :],
                                         psT[0:TT, 0:4 * TT].rearrange("p (j t) -> p j t", j=4),
                                         ACT.Copy).then_inc(pT_kept, 1)
                return fn

            def keep_oT(hf):
                def fn(i, k):
                    act.wait_ge(oT_filled, i * 2 + hf + 1)
                    reused(act, wo_done, i, 2)
                    nc.scalar.activation(oTh[:, k % 2, 4 * hf:4 * hf + 4, :],
                                         psO[:, 0:4 * TT].rearrange("p (j t) -> p j t", j=4),
                                         ACT.Copy).then_inc(oT_kept, 1)
                return fn

            def exps(hf):
                def fn(i, k):
                    act.wait_ge(shifted, i * 2 + hf + 1)
                    sv = s[0:TT, k % 2, 8 * hf:8 * hf + 8, :]
                    nc.scalar.activation(sv, sv, ACT.Exp, scale=HD ** -0.5).then_inc(exp_done, 1)
                return fn

            run(act, NT, U, [(2, values(0)), (3, keep_pT(0)), (2, values(1)), (3, keep_pT(1)),
                             (3, keep_pT(2)), (3, keep_oT(0)), (3, keep_pT(3)), (3, keep_oT(1)),
                             (2, exps(0)), (0, queries_keys(0, 4)), (2, exps(1)), (0, queries_keys(4, 8))])

        @block.vector
        def _(dve):
            weights.wait(dve)
            nc.vector.tensor_copy(mask[0:TT, :], mask_f32[0:TT, :]).then_inc(mask_done, 1)

            def shift(hf):
                def fn(i, k):
                    dve.wait_ge(scores_done, i * 2 + hf + 1)
                    reused(dve, shifted, i, 1, 2, hf - 1)
                    src = psS[0:TT, hf, :, 0:4 * TT].rearrange("q p (j t) -> q p j t", j=4)
                    tv = top[0:TT, hf, 0:8]
                    nc.vector.tensor_reduce(tv.rearrange("q (p j) -> q p j", p=2), src, AX.X, ALU.max)\
                        .then_inc(top_done, 1)
                    dve.wait_ge(top_done, i * 2 + hf + 1)
                    reused(dve, pT_filled, i, 2, 4, 0)
                    nc.vector.tensor_tensor(
                        s[0:TT, k % 2, 8 * hf:8 * hf + 8, :].rearrange("q (p j) t -> q p j t", p=2), src,
                        tv.rearrange("q (p j) -> q p j", p=2).unsqueeze(3).broadcast_to([TT, 2, 4, TT]),
                        ALU.subtract).then_inc(shifted, 1)
                return fn

            def scale(hf):
                def fn(i, k):
                    dve.wait_ge(exp_done, i * 2 + hf + 1)
                    sv = s[0:TT, k % 2, 8 * hf:8 * hf + 8, :]
                    nc.vector.tensor_reduce(total[0:TT, hf, 0:8], sv, AX.X, ALU.add).then_inc(total_done, 1)
                    dve.wait_ge(total_done, i * 2 + hf + 1)
                    nc.vector.reciprocal(inv[0:TT, hf, 0:8], total[0:TT, hf, 0:8]).then_inc(inv_done, 1)
                    dve.wait_ge(inv_done, i * 2 + hf + 1)
                    nc.vector.tensor_tensor(sv, sv, inv[0:TT, hf, 0:8].unsqueeze(2).broadcast_to([TT, 8, TT]),
                                            ALU.mult).then_inc(prob_done, 1)
                return fn

            def rest(hf):
                def fn(i, k):
                    dve.wait_ge(oT_kept, i * 2 + hf + 1)
                    reused(dve, wo_done, i, 2)
                    at = slice(4 * hf, 4 * hf + 4)
                    nc.vector.tensor_tensor(oTl[:, k % 2, at, :], psO[:, 0:4 * TT].rearrange("p (j t) -> p j t", j=4),
                                            oTh[:, k % 2, at, :].bitcast(F32), ALU.subtract).then_inc(oT_rest, 1)
                return fn

            def add(i, k):
                nc.vector.tensor_tensor(h[0:TT, i, :], h[0:TT, i, :], bo[0:TT, :], ALU.add).then_inc(h_bias, 1)
                dve.wait_ge(h_bias, i + 1)
                dve.wait_ge(wo_done, i + 1)
                nc.vector.tensor_tensor(h[0:TT, i, :], h[0:TT, i, :], psO[0:TT, 0:D], ALU.add)\
                    .then_inc(h_done, 1)

            run(dve, NT, U, [(4, add), (2, shift(0)), (3, rest(0)), (2, shift(1)), (3, rest(1)), (2, scale(0)), (2, scale(1)),
                             (5, lambda i, k: moments.of(dve, i, k, h_done))])


def linker(eng, sem):
    count = [0]

    def link(ins):
        count[0] += 1
        ins.then_inc(sem, 1)
        eng.wait_ge(sem, count[0])
    return link


def one_hot_of_max(nc, link, x, top, hit, number, number_less_e, first):
    wide = [TT, NT, E]
    link(nc.vector.tensor_reduce(top, x, AX.X, ALU.max))
    link(nc.vector.tensor_tensor(hit, x, top.unsqueeze(2).broadcast_to(wide), ALU.is_equal))
    link(nc.vector.tensor_tensor(number, hit, number_less_e.unsqueeze(1).broadcast_to(wide), ALU.mult))
    link(nc.vector.tensor_reduce(first, number, AX.X, ALU.min))
    link(nc.vector.tensor_tensor(hit, number_less_e.unsqueeze(1).broadcast_to(wide),
                                 first.unsqueeze(2).broadcast_to(wide), ALU.is_equal))


def route_top1(g, ffn, later):
    nc, a, sb, pb, sem, h, xT = (g[k] for k in ("nc", "a", "sb", "pb", "sem", "h", "xT"))
    U = 4
    with ExitStack() as c:
        ln = LayerNorm(g, c, "ln1", slots=True, known=True)
        small = g["small"]
        rms_w, gate, less_e = (small[n] for n in ("rms_w", "gate", "less_e"))
        square = sb("square", [128, D], c=c)
        ms = sb("ms", [128, 2, 3], c=c)
        NR = 4
        xr = sb("xr", [128, NR, D], c=c)
        logits = sb("logits", [128, NT, E], c=c)
        p = sb("p", [128, NT, E], c=c)
        top, first, total, best = (sb(n, [128, NT], c=c) for n in ("r_top", "r_first", "r_total", "r_best"))
        psG = pb("psG", [128, 2, 512], c=c)
        ms_done = sem("ms_done", c)
        ms_eps = sem("ms_eps", c)
        rms_done = sem("rms_done", c)
        xr_done = sem("xr_done", c)
        x_stored = [sem(f"route_x_stored{j}", c) for j in range(NR)]
        gated = sem("gated", c)
        logits_done = sem("logits_done", c)
        chain = sem("route_chain", c)
        shift_done = sem("route_shift_done", c)
        exp_done = sem("route_exp_done", c)
        block = c.enter_context(nc.Block())

        @block.sync
        def _(sp):
            later.issue(sp)

            def store_x(i, k):
                sp.wait_ge(xr_done, i + 1)
                sp.dma_start(ffn.rows_of(i), xr[0:TT, k, :]).then_inc(x_stored[k], 16)
            run(sp, NT, NR, [(0, store_x)])
            for k in range(NR):
                sp.wait_ge(x_stored[k], 16 * len(range(k, NT, NR)))

        @block.vector
        def _(dve):
            small.wait(dve)

            def mean_square(i, k):
                dve.wait_ge(ln.xn_done, i + 1)
                reused(dve, xr_done, i, 2)
                nc.vector.scalar_tensor_tensor(out=square[0:TT, :], in0=ln.xn[0:TT, k, :], scalar=1.0 / D,
                                               in1=ln.xn[0:TT, k, :], op0=ALU.mult, op1=ALU.mult,
                                               accum_out=ms[0:TT, k % 2, 0:1]).then_inc(ms_done, 1)

            def rms(i, k):
                dve.wait_ge(rms_done, i + 1)
                reused(dve, ln.turned, i, NR)
                if not (isinstance(i, int) and i < NR):
                    dve.wait_ge(x_stored[k], (i - k) * (16 // NR))
                nc.vector.scalar_tensor_tensor(out=xr[0:TT, k, :], in0=ln.xn[0:TT, k, :],
                                               scalar=ms[0:TT, k % 2, 2:3], in1=rms_w[0:TT, :],
                                               op0=ALU.mult, op1=ALU.mult).then_inc(xr_done, 1)

            def normalise(i, k):
                reused(dve, xr_done, i, U)
                ln.normalise(dve, i, k)

            def keep_logits(i, k):
                dve.wait_ge(gated, i + 1)
                nc.vector.tensor_scalar(logits[0:TT, i, :], psG[0:TT, k % 2, 0:E], 0.0, None, ALU.add)\
                    .then_inc(logits_done, 1)
            ln.aggregate_all(dve)
            run(dve, NT, U, [(0, normalise), (0, mean_square), (1, rms), (4, keep_logits)])
            link = linker(dve, chain)
            dve.wait_ge(logits_done, NT)
            hit, number = ffn.hits[0], p
            one_hot_of_max(nc, link, logits[0:TT], top[0:TT], hit[0:TT], number[0:TT], less_e[0:TT], first[0:TT])
            nc.vector.tensor_tensor(logits[0:TT], logits[0:TT], top[0:TT].unsqueeze(2).broadcast_to([TT, NT, E]),
                                    ALU.subtract).then_inc(shift_done, 1)
            dve.wait_ge(exp_done, 1)
            link(nc.vector.tensor_reduce(total[0:TT], logits[0:TT], AX.X, ALU.add))
            link(nc.vector.tensor_reduce(best[0:TT], logits[0:TT], AX.X, ALU.max))
            link(nc.vector.reciprocal(total[0:TT], total[0:TT]))
            link(nc.vector.tensor_tensor(ffn.scores[0][0:TT], best[0:TT], total[0:TT], ALU.mult))

        @block.gpsimd
        def _(pool):
            def inverse_rms(i, k):
                pool.wait_ge(ms_done, i + 1)
                nc.gpsimd.tensor_tensor(ms[0:TT, k % 2, 1:2], ms[0:TT, k % 2, 0:1], g["epsilon"][0:TT, 1:2],
                                        ALU.add).then_inc(ms_eps, 1)
                pool.wait_ge(ms_eps, i + 1)
                nc.gpsimd.tensor_tensor(ms[0:TT, k % 2, 2:3], ms[0:TT, k % 2, 1:2], g["mhalf"][0:TT, :],
                                        ALU.pow).then_inc(rms_done, 1)

            ln.inverse_all(pool)
            run(pool, NT, U, [(1, inverse_rms)])

        @block.tensor
        def _(pe):
            small.wait(pe)

            def logit(i, k):
                pe.wait_ge(ln.kept, i + 1)
                reused(pe, logits_done, i, 2)
                for kc in range(KD):
                    mm = nc.tensor.matmul(psG[0:TT, k % 2, 0:E], ln.xs[:, k % 2, kc, :], gate[:, kc, :],
                                          start=kc == 0, stop=kc == KD - 1)
                mm.then_inc(gated, 1)
            run(pe, NT, U, [(2, lambda i, k: ln.turn(pe, i, k, xr_done, xr[0:TT, k, :])), (3, logit)])

        @block.scalar
        def _(act):
            run(act, NT, U, [(2, lambda i, k: ln.keep_stationary(act, i, k, gated, last=True))])
            act.wait_ge(shift_done, 1)
            nc.scalar.activation(logits[0:TT], logits[0:TT], ACT.Exp).then_inc(exp_done, 1)


def route_top2(g, ffn):
    nc, a, sb, pb, sem, h, xT = (g[k] for k in ("nc", "a", "sb", "pb", "sem", "h", "xT"))
    U = LayerNorm.SLOTS
    with ExitStack() as c:
        ln = LayerNorm(g, c, "ln3", slots=True, known=True)
        small = g["small"]
        rw1, rb1, rw2, rb2, less_e = (small[n] for n in ("rw1", "rb1", "rw2", "rb2", "less_e"))
        hidden = sb("hidden", [128, U, KD, TT], c=c)
        logits = sb("logits2", [128, NT, E], c=c)
        rest, number = (sb(n, [128, NT, E], c=c) for n in ("r_rest", "r_number"))
        hit1, hit2 = ffn.hits
        top1, top2, first, total = (sb(n, [128, NT], c=c) for n in ("r_top1", "r_top2", "r2_first", "r2_total"))
        psH = pb("psRH", [128, 2, 512], c=c)
        psG = pb("psRG", [128, 2, 512], c=c)
        hidden_filled = sem("hidden_filled", c)
        hidden_kept = sem("hidden_kept", c)
        gated = sem("gated2", c)
        logits_done = sem("logits2_done", c)
        h_done = sem("router_h_done", c)
        x_stored = [sem(f"route2_x_stored{j}", c) for j in range(LayerNorm.SLOTS)]
        chain = sem("route2_chain", c)
        shift_done = sem("route2_shift_done", c)
        exp_done = sem("route2_exp_done", c)
        block = c.enter_context(nc.Block())

        @block.sync
        def _(sp):
            def store_x(i, k):
                sp.wait_ge(ln.xn_done, i + 1)
                sp.dma_start(ffn.rows_of(i), ln.xn[0:TT, k, :]).then_inc(x_stored[k], 16)
            run(sp, NT, U, [(0, store_x)])
            for k in range(U):
                sp.wait_ge(x_stored[k], 16 * len(range(k, NT, U)))

        @block.vector
        def _(dve):
            small.wait(dve)

            def residual(i, k):
                dve.wait_ge(ln.xn_done, i + 1)
                nc.vector.tensor_tensor(h[0:TT, i, :], h[0:TT, i, :], ln.xn[0:TT, k, :], ALU.add)\
                    .then_inc(h_done, 1)

            def normalise(i, k):
                reused(dve, h_done, i, U)
                if not (isinstance(i, int) and i < U):
                    dve.wait_ge(x_stored[k], (i - k) * (16 // U))
                ln.normalise(dve, i, k)

            def keep_logits(i, k):
                dve.wait_ge(gated, i + 1)
                nc.vector.tensor_tensor(logits[0:TT, i, :], psG[0:TT, k % 2, 0:E], rb2[0:TT, :], ALU.add)\
                    .then_inc(logits_done, 1)
            ln.aggregate_all(dve)
            run(dve, NT, U, [(1, normalise), (1, residual),
                             (6, keep_logits)])
            link = linker(dve, chain)
            dve.wait_ge(logits_done, NT)
            one_hot_of_max(nc, link, logits[0:TT], top1[0:TT], hit1[0:TT], number[0:TT], less_e[0:TT], first[0:TT])
            link(nc.vector.scalar_tensor_tensor(out=rest[0:TT], in0=hit1[0:TT], scalar=-1.0e30, in1=logits[0:TT],
                                                op0=ALU.mult, op1=ALU.add))
            one_hot_of_max(nc, link, rest[0:TT], top2[0:TT], hit2[0:TT], number[0:TT], less_e[0:TT], first[0:TT])
            nc.vector.tensor_tensor(top2[0:TT], top2[0:TT], top1[0:TT], ALU.subtract).then_inc(shift_done, 1)
            dve.wait_ge(exp_done, 1)
            link(nc.vector.tensor_scalar(total[0:TT], top2[0:TT], 1.0, None, ALU.add))
            link(nc.vector.reciprocal(ffn.scores[0][0:TT], total[0:TT]))
            link(nc.vector.tensor_tensor(ffn.scores[1][0:TT], top2[0:TT], ffn.scores[0][0:TT], ALU.mult))

        @block.gpsimd
        def _(pool):
            ln.inverse_all(pool)

        @block.tensor
        def _(pe):
            small.wait(pe)

            def hide(i, k):
                pe.wait_ge(ln.kept, i + 1)
                reused(pe, hidden_kept, i, 2)
                for m in range(KD):
                    for kc in range(KD):
                        mm = nc.tensor.matmul(psH[:, k % 2, m * TT:(m + 1) * TT], rw1[:, kc, m * 128:(m + 1) * 128],
                                              ln.xs[:, k % 2, kc, :], start=kc == 0, stop=kc == KD - 1)
                mm.then_inc(hidden_filled, 1)

            def logit(i, k):
                pe.wait_ge(hidden_kept, i + 1)
                reused(pe, logits_done, i, 2)
                for kc in range(KD):
                    mm = nc.tensor.matmul(psG[0:TT, k % 2, 0:E], hidden[:, k, kc, :], rw2[:, kc, :],
                                          start=kc == 0, stop=kc == KD - 1)
                mm.then_inc(gated, 1)
            run(pe, NT, U, [(5, logit), (1, lambda i, k: ln.turn(pe, i, k)), (2, hide)])

        @block.scalar
        def _(act):
            small.wait(act)

            def keep_hidden(i, k):
                act.wait_ge(hidden_filled, i + 1)
                reused(act, gated, i, U)
                for m in range(KD):
                    ins = nc.scalar.activation(hidden[:, k, m, :], psH[:, k % 2, m * TT:(m + 1) * TT], ACT.Silu,
                                               bias=rb1[:, m:m + 1])
                ins.then_inc(hidden_kept, 1)
            run(act, NT, U, [(1, lambda i, k: ln.keep_stationary(act, i, k, hidden_filled, last=True)),
                             (2, keep_hidden)])
            act.wait_ge(shift_done, 1)
            nc.scalar.activation(top2[0:TT], top2[0:TT], ACT.Exp).then_inc(exp_done, 1)


def step_sizes(g, ln_out, dt, dA, dA_parts):
    nc, a, sb, pb, sem, h, xT = (g[k] for k in ("nc", "a", "sb", "pb", "sem", "h", "xT"))
    U = LayerNorm.SLOTS
    with ExitStack() as c:
        ln = LayerNorm(g, c, "ln2", slots=True, known=True)
        small = g["small"]
        wdt, dt_bias, A_log = (small[n] for n in ("wdt", "dt_bias", "A_log"))
        A_exp = sb("A_exp", [128, MH], c=c)
        raw, u, w, lnw, t0 = (sb("sp_" + n, [128, NT, MH], c=c) for n in ("raw", "u", "w", "lnw", "t0"))
        psD = pb("psD", [128, 2, 512], c=c)
        dt_filled = sem("dt_filled", c)
        raw_done = sem("dt_raw_done", c)
        xn_kept = sem("xn_kept", c)
        chain = sem("dt_chain", c)
        abs_done = sem("dt_abs_done", c)
        exp_done = sem("dt_exp_done", c)
        w_done = sem("dt_w_done", c)
        ln_done = sem("dt_ln_done", c)
        block = c.enter_context(nc.Block())

        @block.vector
        def _(dve):
            small.wait(dve)

            def normalise(i, k):
                reused(dve, xn_kept, i, U)
                ln.normalise(dve, i, k)

            def keep_raw(i, k):
                dve.wait_ge(dt_filled, i + 1)
                nc.vector.tensor_tensor(raw[0:TT, i, :], psD[0:TT, k % 2, 0:MH], dt_bias[0:TT, :], ALU.add)\
                    .then_inc(raw_done, 1)
            ln.aggregate_all(dve)
            run(dve, NT, U, [(1, normalise), (4, keep_raw)])
            link = linker(dve, chain)
            dve.wait_ge(raw_done, NT)
            nc.vector.scalar_tensor_tensor(out=u[0:TT], in0=raw[0:TT], scalar=-1.0, in1=raw[0:TT],
                                           op0=ALU.mult, op1=ALU.max).then_inc(abs_done, 1)
            dve.wait_ge(exp_done, 1)
            nc.vector.tensor_scalar(w[0:TT], u[0:TT], 1.0, None, ALU.add).then_inc(w_done, 1)
            dve.wait_ge(ln_done, 1)
            link(nc.vector.tensor_scalar(w[0:TT], w[0:TT], -1.0, None, ALU.add))
            link(nc.vector.tensor_scalar(t0[0:TT], w[0:TT], 0.0, None, ALU.is_equal))
            link(nc.vector.tensor_tensor(w[0:TT], w[0:TT], t0[0:TT], ALU.add))
            link(nc.vector.reciprocal(w[0:TT], w[0:TT]))
            link(nc.vector.tensor_tensor(lnw[0:TT], lnw[0:TT], w[0:TT], ALU.mult))
            link(nc.vector.tensor_tensor(lnw[0:TT], lnw[0:TT], t0[0:TT], ALU.add))
            link(nc.vector.tensor_tensor(u[0:TT], u[0:TT], lnw[0:TT], ALU.mult))
            link(nc.vector.scalar_tensor_tensor(out=dt[0:TT], in0=raw[0:TT], scalar=0.0, in1=u[0:TT],
                                                op0=ALU.max, op1=ALU.add))
            link(nc.vector.scalar_tensor_tensor(out=dA[0:TT], in0=dt[0:TT], scalar=-1.0,
                                                in1=A_exp[0:TT].unsqueeze(1).broadcast_to([TT, NT, MH]),
                                                op0=ALU.mult, op1=ALU.mult))
            high, low = dA_parts
            link(nc.vector.tensor_copy(high[0:TT], dA[0:TT]))
            link(nc.vector.tensor_tensor(low[0:TT], dA[0:TT], high[0:TT].bitcast(F32), ALU.subtract))

        @block.gpsimd
        def _(pool):
            ln.inverse_all(pool)

        @block.tensor
        def _(pe):
            small.wait(pe)

            def product(i, k):
                pe.wait_ge(ln.xs_kept, i + 1)
                reused(pe, raw_done, i, 2)
                for kc in range(KD):
                    mm = nc.tensor.matmul(psD[0:TT, k % 2, 0:MH], ln.xs[:, k % 2, kc, :], wdt[:, kc, :],
                                          start=kc == 0, stop=kc == KD - 1)
                mm.then_inc(dt_filled, 1)
            run(pe, NT, U, [(1, lambda i, k: ln.turn(pe, i, k)), (2, product)])

        @block.scalar
        def _(act):
            small.wait(act)

            def keep_xn(i, k):
                act.wait_ge(ln.xn_done, i + 1)
                through(act, i, g["passed"])
                nc.scalar.activation(ln_out[0:TT, i, :], ln.xn[0:TT, k, :], ACT.Copy).then_inc(xn_kept, 1)
            run(act, NT, U, [(0, keep_xn), (1, lambda i, k: ln.keep_stationary(act, i, k, dt_filled)),
                             (1, lambda i, k: ln.keep(act, i, k))])
            nc.scalar.activation(A_exp[0:TT], A_log[0:TT], ACT.Exp)
            act.wait_ge(abs_done, 1)
            nc.scalar.activation(u[0:TT], u[0:TT], ACT.Exp, scale=-1.0).then_inc(exp_done, 1)
            act.wait_ge(w_done, 1)
            nc.scalar.activation(lnw[0:TT], w[0:TT], ACT.Ln).then_inc(ln_done, 1)


def mamba_weights(g, c):
    a = g["a"]
    W_in = a["W_in"].rearrange("(c p) n -> p c n", p=128)
    return Loads(g, "mamba", c, [
        ("wz", [128, KD, DI], W_in[:, :, 0:DI]), ("wx", [128, KD, CONV], W_in[:, :, DI:DI + CONV]),
        ("wout", [128, DI // 128, D], a["W_out"].rearrange("(c p) n -> p c n", p=128)),
        ("wglu", [128, KD, 2 * D], a["glu_w"].rearrange("(c p) n -> p c n", p=128)),
        ("glu_b", [TT, 2 * D], a["glu_b"]), ("conv_w", [128, KC, 4], a["conv_w"]), ("conv_b", [128, KC], a["conv_b"]),
        ("out_w", [128, DI // 128], a["m_rms_w"]),
        ("skip", [128, DI // 128], a["D_skip"]), ("ln_w", [TT, D], a["ln_w"]), ("ln_b", [TT, D], a["ln_b"]),
        ("after", [TT, TT], a["after"]),
        ("upto", [TT, TT], a["upto"]),
        ("causal", [TT, TT], a["causal"])])


def mamba(g, weights):
    nc, a, sb, pb, sem, h, xT, ident = (g[k] for k in ("nc", "a", "sb", "pb", "sem", "h", "xT", "ident"))
    U = 4
    PAD = 3
    UN = 2 * TT
    NU = KC // 2
    KY = DI // 128
    HH = MH // 2
    with ExitStack() as c:
        xn = sb("xn", [128, NT, D], c=c)
        dt = sb("dt", [128, NT, MH], c=c)
        dA = sb("dA", [128, NT, MH], c=c)
        dA_parts = [sb("dA_" + part, [128, NT, MH], F32R, c=c) for part in ("high", "low")]
        step_sizes(g, xn, dt, dA, dA_parts)

        wz, wx, wout, wglu, glu_b, conv_w, conv_b, out_w, skip, ln_w, ln_b, after, upto, causal = (
            weights[n] for n in ("wz wx wout wglu glu_b conv_w conv_b out_w skip ln_w ln_b after upto causal").split())
        xs = sb("m_xs", [128, U, KD, TT], c=c)
        raw = sb("m_raw", [128, 2, KC, PER, PAD + TOK], c=c)
        acc = sb("m_acc", [128, 2, KC, TT], c=c)
        xbc = sb("m_xbc", [128, 2, KC, TT], c=c)
        zs = sb("m_zs", [128, U, DI], c=c)
        R = [sb("m_R_" + part, [128, 2, MH, TT], F32R, c=c) for part in ("high", "low")]
        after_r = sb("after_r", [128, TT], F32R, c=c)
        W = sb("m_W", [128, 2, MH, TT], c=c)
        G = sb("m_G", [128, 2, TT], c=c)
        xdt = sb("m_xdt", [128, 2, DI], c=c)
        skips = sb("m_skips", [128, KY, 128], c=c)
        y = sb("m_y", [128, 2, DI], c=c)
        junk = sb("m_junk", [128, DI], c=c)
        ms = sb("m_ms", [128, 2, 3], c=c)
        yT = sb("m_yT", [128, 2, KY, TT], c=c)
        y1 = sb("m_y1", [128, 2, D], c=c)
        y1T = sb("m_y1T", [128, 2, KD, TT], c=c)
        glu = sb("m_glu", [128, 2, 2 * D], c=c)
        th = sb("m_th", [128, 2, D], c=c)
        y2 = sb("m_y2", [128, 2, D], c=c)
        st = sb("m_st", [128, 2, 6], c=c)
        mv = sb("m_mv", [128, 2, 2], c=c)
        rs = sb("m_rs", [128, 2, 2], c=c)
        nrm = sb("m_nrm", [128, 2, D], c=c)
        psC = pb("psC", [128, 2, 512], c=c)
        psG = pb("psCB", [128, 512], c=c)
        psR = pb("psR", [128, 512], c=c)
        psX = pb("psX", [128, 512], c=c)
        psS = pb("psSeg", [128, 512], c=c)
        psY = pb("psY", [128, 512], c=c)
        psU = pb("psU", [128, 512], c=c)
        names = ("raw_zeroed wout_done xs_done xbc_filled raw_kept tap0_done conv_tap xbc_done skipped z_filled zs_done "
                 "R_done x_filled G_filled xdt_done skips_done G_done seg_filled seg_exp W_done y_filled "
                 "y_gated y_squared ms_eps ms_done yT_filled yT_kept out_filled y1_done y1T_filled y1T_kept "
                 "glu_filled glu_biased tanh_done gated y2_done st_done mv_done rs_eps rs_done nrm_done scaled "
                 "biased h_done").split()
        m = {n: sem("m_" + n, c) for n in names}
        (raw_zeroed, wout_done, xs_done, xbc_filled, raw_kept, tap0_done, conv_tap, xbc_done, skipped, z_filled, zs_done,
         R_done, x_filled, G_filled, xdt_done, skips_done, G_done, seg_filled, seg_exp, W_done, y_filled,
         y_gated, y_squared, ms_eps, ms_done, yT_filled, yT_kept, out_filled, y1_done, y1T_filled, y1T_kept,
         glu_filled, glu_biased, tanh_done, gated, y2_done, st_done, mv_done, rs_eps, rs_done, nrm_done, scaled,
         biased, h_done) = (m[n] for n in names)
        moments = Moments(g, c, "mamba_moments")
        block = c.enter_context(nc.Block())

        @block.gpsimd
        def _(pool):
            passed = g["passed"]
            weights.wait(pool)

            def stationary(i, k):
                reused(pool, z_filled, i, U)
                through(pool, i, passed)
                nc.gpsimd.tensor_copy(xs[:, k, :, :], xT[:, :, cols(i)]).then_inc(xs_done, 1)

            def spread(i, k):
                reused(pool, seg_filled, i, 2, 2, 0)
                through(pool, i, passed)
                for r, part in zip(R, dA_parts):
                    nc.gpsimd.tensor_tensor(
                        r[0:TT, k % 2, :, :], upto[0:TT, :].unsqueeze(1).broadcast_to([TT, MH, TT]),
                        part[0:TT, i, :].bitcast(F32).unsqueeze(2).broadcast_to([TT, MH, TT]), ALU.mult)\
                        .then_inc(R_done, 1)

            def inverse_rms(i, k):
                pool.wait_ge(y_squared, i + 1)
                nc.gpsimd.tensor_tensor(ms[0:TT, k % 2, 1:2], ms[0:TT, k % 2, 0:1], g["epsilon"][0:TT, 0:1],
                                        ALU.add).then_inc(ms_eps, 1)
                pool.wait_ge(ms_eps, i + 1)
                nc.gpsimd.tensor_tensor(ms[0:TT, k % 2, 2:3], ms[0:TT, k % 2, 1:2], g["mhalf"][0:TT, :],
                                        ALU.pow).then_inc(ms_done, 1)

            def inverse_deviation(i, k):
                pool.wait_ge(mv_done, i + 1)
                reused(pool, nrm_done, i, 2)
                nc.gpsimd.tensor_tensor(rs[0:TT, k % 2, 0:1], mv[0:TT, k % 2, 1:2], g["epsilon"][0:TT, 0:1],
                                        ALU.add).then_inc(rs_eps, 1)
                pool.wait_ge(rs_eps, i + 1)
                nc.gpsimd.tensor_tensor(rs[0:TT, k % 2, 1:2], rs[0:TT, k % 2, 0:1], g["mhalf"][0:TT, :],
                                        ALU.pow).then_inc(rs_done, 1)

            def affine(i, k):
                pool.wait_ge(nrm_done, i + 1)
                nc.gpsimd.tensor_tensor(nrm[0:TT, k % 2, :], nrm[0:TT, k % 2, :], ln_w[0:TT, :], ALU.mult)\
                    .then_inc(scaled, 1)
                pool.wait_ge(scaled, i + 1)
                nc.gpsimd.tensor_tensor(nrm[0:TT, k % 2, :], nrm[0:TT, k % 2, :], ln_b[0:TT, :], ALU.add)\
                    .then_inc(biased, 1)
                pool.wait_ge(biased, i + 1)
                through(pool, i, passed)
                nc.gpsimd.tensor_tensor(h[0:TT, i, :], h[0:TT, i, :], nrm[0:TT, k % 2, :], ALU.add)\
                    .then_inc(h_done, 1)
            run(pool, NT, U, [(0, stationary), (2, spread), (5, inverse_rms), (7, inverse_deviation), (8, affine)])

        @block.tensor
        def _(pe):
            weights.wait(pe)
            pe.wait_ge(wout_done, 1)
            pe.wait_ge(skips_done, 2)

            def heads(i, k):
                pe.wait_ge(W_done, i * 2 + 2)
                pe.wait_ge(xdt_done, i + 1)
                for hd in range(MH):
                    mm = nc.tensor.matmul(psY[0:TT, hd * 64:(hd + 1) * 64], W[0:TT, k % 2, hd, :],
                                          xdt[0:TT, k % 2, hd * 64:(hd + 1) * 64], start=False, stop=hd == MH - 1)
                mm.then_inc(y_filled, 1)

            def project(i, k):
                pe.wait_ge(xs_done, i + 1)
                for u in range(NU):
                    if u == 0:
                        reused(pe, raw_kept, i, 1, NU, 0)
                    elif u == 1:
                        reused(pe, zs_done, i, 2)
                    else:
                        pe.wait_ge(raw_kept, i * NU + 1)
                    for half in range(2):
                        ch = 2 * u + half
                        for kc in range(KD):
                            mm = nc.tensor.matmul(psC[:, u % 2, half * TT:(half + 1) * TT],
                                                  wx[:, kc, ch * 128:(ch + 1) * 128], xs[:, k, kc, :],
                                                  start=kc == 0, stop=kc == KD - 1)
                    mm.then_inc(xbc_filled, 1)

            def turn_y1(i, k):
                pe.wait_ge(y1_done, i + 1)
                for ch in range(KD):
                    mm = nc.tensor.transpose(psR[:, ch * TT:(ch + 1) * TT],
                                             y1[0:TT, k % 2, ch * 128:(ch + 1) * 128], ident[0:TT, 0:TT])
                mm.then_inc(y1T_filled, 1)

            def gates(i, k):
                pe.wait_ge(raw_kept, NT * NU if isinstance(i, int) and i == NT - 1 else (i + 1) * NU + 2)
                for kc in range(KD):
                    mm = nc.tensor.matmul(psC[0:TT, 1, :], xs[:, k, kc, :], wz[:, kc, :],
                                          start=kc == 0, stop=kc == KD - 1)
                mm.then_inc(z_filled, 1)

            def turn_x(i, k):
                pe.wait_ge(xbc_done, i + 1)
                reused(pe, xdt_done, i, 1)
                for ch in range(KY):
                    mm = nc.tensor.transpose(psX[0:TT, ch * 128:(ch + 1) * 128], xbc[:, k % 2, ch, :], ident[:, :])
                mm.then_inc(x_filled, 1)
                reused(pe, G_done, i, 1)
                nc.tensor.matmul(psG[0:TT, 0:TT], xbc[:, k % 2, KY, :], xbc[:, k % 2, KY + 1, :],
                                 start=True, stop=True).then_inc(G_filled, 1)

            def skip_term(i, k):
                reused(pe, y_gated, i, 1)
                for ch in range(KY):
                    mm = nc.tensor.matmul(psY[0:TT, ch * 128:(ch + 1) * 128], xbc[:, k % 2, ch, :], skips[:, ch, :],
                                          start=ch == 0, stop=False)
                mm.then_inc(skipped, 1)

            def turn_y(i, k):
                pe.wait_ge(y_gated, i + 1)
                reused(pe, y1T_kept, i, 1)
                for ch in range(KY):
                    mm = nc.tensor.transpose(psR[:, ch * TT:(ch + 1) * TT],
                                             y[0:TT, k % 2, ch * 128:(ch + 1) * 128], ident[0:TT, 0:TT])
                mm.then_inc(yT_filled, 1)

            def sums(hf):
                def fn(i, k):
                    if hf == 0:
                        pe.wait_ge(R_done, i * 2 + 2)
                    if not (isinstance(i, int) and i * 2 + hf < 1):
                        pe.wait_ge(seg_exp, i * 2 + hf)
                    for n, r in enumerate(R):
                        mm = nc.tensor.matmul(psS[0:TT, 0:HH * TT], after_r[0:TT, :],
                                              r[0:TT, k % 2, hf * HH:(hf + 1) * HH, :], start=n == 0, stop=n == 1)
                    mm.then_inc(seg_filled, 1)
                return fn

            def linear_unit(i, k):
                pe.wait_ge(y1T_kept, i + 1)
                reused(pe, glu_biased, i, 1)
                for kc in range(KD):
                    mm = nc.tensor.matmul(psU[0:TT, :], y1T[:, k % 2, kc, :], wglu[:, kc, :],
                                          start=kc == 0, stop=kc == KD - 1)
                mm.then_inc(glu_filled, 1)

            def output(i, k):
                pe.wait_ge(yT_kept, i + 1)
                for ch in range(KY):
                    mm = nc.tensor.matmul(psR[0:TT, 0:D], yT[:, k % 2, ch, :], wout[:, ch, :],
                                          start=ch == 0, stop=ch == KY - 1)
                mm.then_inc(out_filled, 1)
            run(pe, NT, U, [(4, heads), (0, project), (6, turn_y1), (3, sums(0)), (1, gates), (3, turn_x),
                            (5, turn_y), (3, sums(1)), (3, skip_term), (6, linear_unit), (5, output)])

        @block.scalar
        def _(act):
            act.wait_ge(raw_zeroed, 1)
            weights.wait(act)

            def keep_raw(i, k):
                reused(act, conv_tap, i, 2, 3, 0)
                for u in range(NU):
                    act.wait_ge(xbc_filled, i * NU + u + 1)
                    for half in range(2):
                        ins = nc.scalar.activation(
                            raw[:, k % 2, 2 * u + half, :, PAD:],
                            psC[:, u % 2, half * TT:(half + 1) * TT].rearrange("p (b t) -> p b t", b=PER), ACT.Copy)
                    ins.then_inc(raw_kept, 1)

            def keep_y1T(i, k):
                act.wait_ge(y1T_filled, i + 1)
                reused(act, glu_filled, i, 2)
                nc.scalar.activation(y1T[:, k % 2, :, :], psR[:, 0:UN].rearrange("p (c t) -> p c t", c=KD),
                                     ACT.Copy).then_inc(y1T_kept, 1)

            def first_tap(i, k):
                act.wait_ge(raw_kept, i * NU + NU)
                reused(act, xbc_done, i, 2)
                for ch in range(KC):
                    ins = nc.scalar.activation(acc[:, k % 2, ch, :].rearrange("p (b t) -> p b t", b=PER),
                                               raw[:, k % 2, ch, :, 0:TOK], ACT.Identity, scale=conv_w[:, ch, 0:1],
                                               bias=conv_b[:, ch:ch + 1])
                ins.then_inc(tap0_done, 1)

            def square(i, k):
                act.wait_ge(y_gated, i + 1)
                reused(act, y1_done, i, 2)
                nc.scalar.activation(junk[0:TT, :], y[0:TT, k % 2, :], ACT.Square, scale=DI ** -0.5,
                                     accum_out=ms[0:TT, k % 2, 0:1]).then_inc(y_squared, 1)

            def activate(i, k):
                act.wait_ge(conv_tap, i * 3 + 3)
                reused(act, skipped, i, 2)
                nc.scalar.activation(xbc[:, k % 2, :, :], acc[:, k % 2, :, :], ACT.Silu).then_inc(xbc_done, 1)

            def gate(i, k):
                reused(act, y_gated, i, U)
                act.wait_ge(z_filled, i + 1)
                nc.scalar.activation(zs[0:TT, k, :], psC[0:TT, 1, :], ACT.Silu).then_inc(zs_done, 1)

            def keep_yT(i, k):
                act.wait_ge(yT_filled, i + 1)
                reused(act, out_filled, i, 2)
                nc.scalar.activation(yT[:, k % 2, :, :], psR[:, 0:KY * TT].rearrange("p (c t) -> p c t", c=KY),
                                     ACT.Copy).then_inc(yT_kept, 1)

            def decay(hf):
                def fn(i, k):
                    if hf == 0:
                        reused(act, y_filled, i, 2)
                    act.wait_ge(seg_filled, i * 2 + hf + 1)
                    nc.scalar.activation(W[0:TT, k % 2, hf * HH:(hf + 1) * HH, :],
                                         psS[0:TT, 0:HH * TT].rearrange("p (j t) -> p j t", j=HH), ACT.Exp)\
                        .then_inc(seg_exp, 1)
                return fn

            def half_gate(i, k):
                act.wait_ge(glu_biased, i + 1)
                reused(act, gated, i, 2)
                nc.scalar.activation(th[0:TT, k % 2, :], glu[0:TT, k % 2, D:], ACT.Tanh, scale=0.5)\
                    .then_inc(tanh_done, 1)
            run(act, NT, U, [(0, keep_raw), (6, keep_y1T), (3, decay(0)), (2, activate), (1, gate), (5, keep_yT),
                             (3, decay(1)), (4, square), (6, half_gate), (0, first_tap)])

        @block.vector
        def _(dve):
            nc.vector.memset(raw[:, :, :, :, :], 0.0).then_inc(raw_zeroed, 1)
            weights.wait(dve)
            nc.vector.tensor_tensor(wout[:, :, :], wout[:, :, :], out_w[:, :].unsqueeze(2).broadcast_to([128, KY, D]),
                                    ALU.mult).then_inc(wout_done, 1)
            nc.vector.tensor_tensor(skips[:, :, :], ident[:, :].unsqueeze(1).broadcast_to([128, KY, 128]),
                                    skip.unsqueeze(2).broadcast_to([128, KY, 128]), ALU.mult).then_inc(skips_done, 1)
            nc.vector.tensor_copy(after_r[0:TT, :], after).then_inc(skips_done, 1)

            def heads(i, k):
                dve.wait_ge(y_filled, i + 1)
                dve.wait_ge(zs_done, i + 1)
                reused(dve, yT_filled, i, 2)
                reused(dve, y_squared, i, 2)
                nc.vector.tensor_tensor(y[0:TT, k % 2, :], psY[0:TT, :], zs[0:TT, k, :], ALU.mult)\
                    .then_inc(y_gated, 1)

            def convolve(i, k):
                dve.wait_ge(tap0_done, i + 1)
                for tap in range(1, 4):
                    if tap > 1:
                        dve.wait_ge(conv_tap, i * 3 + tap - 1)
                    for ch in range(KC):
                        src = raw[:, k % 2, ch, :, tap:tap + TOK]
                        dst = acc[:, k % 2, ch, :].rearrange("p (b t) -> p b t", b=PER)
                        ins = nc.vector.scalar_tensor_tensor(out=dst, in0=src, scalar=conv_w[:, ch, tap:tap + 1],
                                                             in1=dst, op0=ALU.mult, op1=ALU.add)
                    ins.then_inc(conv_tap, 1)

            def inputs(i, k):
                xv = psX[0:TT, :].rearrange("s (j d) -> s j d", j=MH)
                wide = [TT, MH, 64]
                dve.wait_ge(x_filled, i + 1)
                reused(dve, y_filled, i, 2)
                nc.vector.tensor_tensor(xdt[0:TT, k % 2, :].rearrange("s (j d) -> s j d", j=MH), xv,
                                        dt[0:TT, i, :].unsqueeze(2).broadcast_to(wide), ALU.mult).then_inc(xdt_done, 1)
                dve.wait_ge(G_filled, i + 1)
                nc.vector.tensor_tensor(G[0:TT, k % 2, :], psG[0:TT, 0:TT], causal[0:TT, :], ALU.mult)\
                    .then_inc(G_done, 1)

            def decayed(i, k):
                dve.wait_ge(G_done, i + 1)
                for hf in range(2):
                    dve.wait_ge(seg_exp, i * 2 + hf + 1)
                    w = W[0:TT, k % 2, hf * HH:(hf + 1) * HH, :]
                    nc.vector.tensor_tensor(w, w, G[0:TT, k % 2, :].unsqueeze(1).broadcast_to([TT, HH, TT]), ALU.mult)\
                        .then_inc(W_done, 1)

            def residual(i, k):
                dve.wait_ge(out_filled, i + 1)
                dve.wait_ge(ms_done, i + 1)
                reused(dve, y2_done, i, 2)
                nc.vector.scalar_tensor_tensor(out=y1[0:TT, k % 2, :], in0=psR[0:TT, 0:D],
                                               scalar=ms[0:TT, k % 2, 2:3], in1=xn[0:TT, i, :],
                                               op0=ALU.mult, op1=ALU.add).then_inc(y1_done, 1)

            def linear_unit(i, k):
                dve.wait_ge(glu_filled, i + 1)
                reused(dve, gated, i, 2)
                nc.vector.tensor_tensor(glu[0:TT, k % 2, :], psU[0:TT, :], glu_b[0:TT, :], ALU.add)\
                    .then_inc(glu_biased, 1)
                dve.wait_ge(tanh_done, i + 1)
                nc.vector.scalar_tensor_tensor(out=th[0:TT, k % 2, :], in0=th[0:TT, k % 2, :], scalar=1.0,
                                               in1=glu[0:TT, k % 2, 0:D], op0=ALU.add, op1=ALU.mult).then_inc(gated, 1)
                dve.wait_ge(gated, i + 1)
                dve.wait_ge(y1_done, i + 1)
                reused(dve, nrm_done, i, 2)
                nc.vector.scalar_tensor_tensor(out=y2[0:TT, k % 2, :], in0=th[0:TT, k % 2, :], scalar=0.5,
                                               in1=y1[0:TT, k % 2, :], op0=ALU.mult, op1=ALU.add).then_inc(y2_done, 1)
                dve.wait_ge(y2_done, i + 1)
                nc.vector.bn_stats(st[0:TT, k % 2, :], y2[0:TT, k % 2, :]).then_inc(st_done, 1)
                dve.wait_ge(st_done, i + 1)
                through(dve, i, g["passed"])
                nc.vector.bn_aggr(mv[0:TT, k % 2, :], st[0:TT, k % 2, :]).then_inc(mv_done, 1)

            def normalise(i, k):
                dve.wait_ge(rs_done, i + 1)
                reused(dve, h_done, i, 2)
                nc.vector.tensor_scalar(nrm[0:TT, k % 2, :], y2[0:TT, k % 2, :], mv[0:TT, k % 2, 0:1],
                                        rs[0:TT, k % 2, 1:2], ALU.subtract, ALU.mult).then_inc(nrm_done, 1)
            run(dve, NT, U, [(4, heads), (1, convolve), (3, inputs), (3, decayed), (7, normalise), (6, linear_unit),
                             (5, residual), (9, lambda i, k: moments.of(dve, i, k, h_done))])


class Sparse:

    def __init__(self, g, name, choices, suffix):
        nc = g["nc"]
        self.name, self.choices, self.suffix = name, choices, suffix
        self.most = -(-IMAGES * TOK // BLOCK)
        self.blocks = (choices * IMAGES * TOK - E) // BLOCK + E
        self.groups = self.blocks * SUB
        self.x_rows = nc.dram_tensor(name + "_x_rows", (NTOK, D), F32, kind="Internal").ap()
        self.y_rows = nc.dram_tensor(name + "_y_rows", (choices * NTOK + self.groups * 128, D), F32,
                                     kind="Internal").ap()
        self.g = g

    def rows_of(self, i):
        return self.x_rows[i * TT:(i + 1) * TT, :] if isinstance(i, int) else self.x_rows[bass.ds(i * TT, TT), :]

    def allocate(self, c):
        sb, n = self.g["sb"], self.name
        self.hits = [sb(f"{n}_hit{j}", [128, NT, E], c=c) for j in range(self.choices)]
        self.scores = [sb(f"{n}_score{j}", [128, NT], c=c) for j in range(self.choices)]
        self.source = sb(n + "_source", [128, self.groups], mybir.dt.uint32, c=c)
        self.target = sb(n + "_target", [128, self.groups], mybir.dt.uint32, c=c)
        self.expert = sb(n + "_expert", [128, self.blocks], mybir.dt.int32, c=c)

    def place(self, g):
        nc, a, sb, pb, sem = (g[k] for k in ("nc", "a", "sb", "pb", "sem"))
        n, NB, MJ, C = self.name + "_", self.blocks, self.most, self.choices
        with ExitStack() as c:
            small = g["small"]
            valid, numbers, before, ones, earlier, token_numbers = (
                small[k] for k in ("valid", "numbers", "before", "ones", "earlier", "token_numbers"))
            spare = small["spare" + self.suffix]
            G = self.groups
            both = sb(n + "both", [128, NT, E], BF16, c=c)
            beforeb = sb(n + "before", [128, TT], BF16, c=c)
            onesb = sb(n + "ones", [128, TT], BF16, c=c)
            rank = sb(n + "rank", [128, NT, E], c=c)
            picked = sb(n + "picked", [128, NT, E], c=c)
            slot = sb(n + "slot", [128, NT], c=c)
            count = sb(n + "count", [128, E], c=c)
            above = sb(n + "above", [128, E, MJ], c=c)
            nblocks = sb(n + "nblocks", [128, E], c=c)
            prior = sb(n + "prior", [128, E, E], c=c)
            first = sb(n + "first", [128, E], c=c)
            end = sb(n + "end", [128, E], c=c)
            passed = sb(n + "ended", [128, NB, E], c=c)
            owner = sb(n + "owner", [128, NB], c=c)
            psR = pb(n + "psRank", [128, 512], c=c)
            reached = sb(n + "reached", [128, NT, G - 1], c=c)
            group = sb(n + "group", [128, NT], c=c)
            at_group = sb(n + "at_group", [128, NT, G], c=c)
            of_group = sb(n + "of_group", [128, C, NT, 2, G], BF16, c=c)
            of_place = sb(n + "of_place", [128, C, NT, 128], BF16, c=c)
            token = sb(n + "token", [128, G], c=c)
            empty = sb(n + "empty", [128, G], c=c)
            second = sb(n + "second", [128, G], c=c)
            psI = pb(n + "psInverse", [128, 512], c=c)
            placed = sem(n + "placed", c)
            inverted = sem(n + "inverted", c)
            both_done = sem(n + "both_done", c)
            rank_filled = sem(n + "rank_filled", c)
            chain = sem(n + "place_chain", c)
            block = c.enter_context(nc.Block())

            @block.tensor
            def _(pe):
                pe.wait_ge(both_done, 1)
                for j in range(NT):
                    if j == NT - 1:
                        nc.tensor.matmul(psR[0:TT, E:NT * E], beforeb[0:TT, :], both[0:TT, 1:NT, :],
                                         start=False, stop=False)
                    nc.tensor.matmul(psR[0:TT, (j + 1) * E:(NT + 1) * E], onesb[0:TT, :],
                                     both[0:TT, j, :].unsqueeze(1).broadcast_to([TT, NT - j, E]),
                                     start=j == 0, stop=j == NT - 1)
                mm = nc.tensor.matmul(psR[0:TT, 0:E], beforeb[0:TT, :], both[0:TT, 0, :], start=True, stop=True)
                mm.then_inc(rank_filled, 1)
                for j in range(C):
                    pe.wait_ge(placed, j + 1)
                    for i in range(NT):
                        mm = nc.tensor.matmul(psI[:, 0:2 * G], of_place[0:TT, j, i, :], of_group[0:TT, j, i, :],
                                              start=i + j == 0, stop=i == NT - 1 and j == C - 1)
                mm.then_inc(inverted, 1)

            @block.vector
            def _(dve):
                link = linker(dve, chain)
                wide = [TT, NT, E]
                link(nc.vector.tensor_copy(onesb[0:TT], ones))
                link(nc.vector.tensor_copy(beforeb[0:TT], before))
                for hit in self.hits:
                    link(nc.vector.tensor_tensor(hit[0:TT], hit[0:TT], valid[0:TT].unsqueeze(2).broadcast_to(wide),
                                                 ALU.mult))
                other = self.hits[1] if C == 2 else None
                if other is None:
                    link(nc.vector.tensor_scalar(both[0:TT], self.hits[0][0:TT], 0.0, None, ALU.add))
                else:
                    link(nc.vector.tensor_tensor(both[0:TT], self.hits[0][0:TT], other[0:TT], ALU.add))
                dve.sem_inc(both_done, 1)
                dve.wait_ge(rank_filled, 1)
                link(nc.vector.tensor_scalar(count[0:TT], psR[0:TT, NT * E:(NT + 1) * E], 0.0, None, ALU.add))
                link(nc.vector.tensor_scalar(prior[0:TT, 0, :], count[0:TT], 1.0 / BLOCK, None, ALU.mult))
                link(nc.vector.tensor_tensor(above[0:TT], prior[0:TT, 0, :].unsqueeze(2).broadcast_to([TT, E, MJ]),
                                             numbers[0:TT, 0:MJ].unsqueeze(1).broadcast_to([TT, E, MJ]), ALU.is_gt))
                link(nc.vector.tensor_reduce(nblocks[0:TT], above[0:TT], AX.X, ALU.add))
                link(nc.vector.tensor_tensor(prior[0:TT], earlier[0:TT],
                                             nblocks[0:TT].unsqueeze(1).broadcast_to([TT, E, E]), ALU.mult))
                link(nc.vector.tensor_reduce(first[0:TT], prior[0:TT], AX.X, ALU.add))
                link(nc.vector.tensor_tensor(end[0:TT], first[0:TT], nblocks[0:TT], ALU.add))
                link(nc.vector.tensor_tensor(passed[0:TT], end[0:TT].unsqueeze(1).broadcast_to([TT, NB, E]),
                                             numbers[0:TT, 0:NB].unsqueeze(2).broadcast_to([TT, NB, E]), ALU.is_le))
                link(nc.vector.tensor_reduce(owner[0:TT], passed[0:TT], AX.X, ALU.add))
                link(nc.vector.tensor_scalar(owner[0:TT], owner[0:TT], E - 1.0, None, ALU.min))
                link(nc.vector.tensor_copy(self.expert[0:TT], owner[0:TT]))
                link(nc.vector.tensor_scalar(first[0:TT], first[0:TT], float(BLOCK), None, ALU.mult))
                link(nc.vector.tensor_tensor(rank[0:TT], psR[0:TT, 0:NT * E].rearrange("p (i e) -> p i e", i=NT),
                                             first[0:TT].unsqueeze(1).broadcast_to(wide), ALU.add))
                for j in range(C):
                    link(nc.vector.tensor_tensor(picked[0:TT], self.hits[j][0:TT], rank[0:TT], ALU.mult))
                    link(nc.vector.tensor_reduce(slot[0:TT], picked[0:TT], AX.X, ALU.add))
                    link(nc.vector.tensor_scalar(group[0:TT], slot[0:TT], 1.0 / 128, None, ALU.mult))
                    link(nc.vector.tensor_tensor(reached[0:TT], group[0:TT].unsqueeze(2).broadcast_to([TT, NT, G - 1]),
                                                 numbers[0:TT, 1:G].unsqueeze(1).broadcast_to([TT, NT, G - 1]),
                                                 ALU.is_ge))
                    link(nc.vector.tensor_reduce(group[0:TT], reached[0:TT], AX.X, ALU.add))
                    link(nc.vector.scalar_tensor_tensor(out=slot[0:TT], in0=group[0:TT], scalar=-128.0,
                                                        in1=slot[0:TT], op0=ALU.mult, op1=ALU.add))
                    link(nc.vector.tensor_tensor(at_group[0:TT], group[0:TT].unsqueeze(2).broadcast_to([TT, NT, G]),
                                                 numbers[0:TT, 0:G].unsqueeze(1).broadcast_to([TT, NT, G]),
                                                 ALU.is_equal))
                    for part in range(2):
                        link(nc.vector.tensor_tensor(
                            of_group[0:TT, j, :, part, :], at_group[0:TT],
                            token_numbers[0:TT, j, part].unsqueeze(2).broadcast_to([TT, NT, G]), ALU.mult))
                    link(nc.vector.tensor_tensor(of_place[0:TT, j], slot[0:TT].unsqueeze(2).broadcast_to([TT, NT, 128]),
                                                 numbers[0:TT, 0:128].unsqueeze(1).broadcast_to([TT, NT, 128]),
                                                 ALU.is_equal))
                    dve.sem_inc(placed, 1)
                dve.wait_ge(inverted, 1)
                link(nc.vector.tensor_scalar(token[:], psI[:, 0:G], 64.0, -1.0, ALU.mult, ALU.add))
                link(nc.vector.tensor_tensor(token[:], token[:], psI[:, G:2 * G], ALU.add))
                link(nc.vector.tensor_scalar(empty[:], token[:], 0.0, None, ALU.is_lt))
                link(nc.vector.tensor_tensor(empty[:], empty[:], spare, ALU.mult))
                link(nc.vector.tensor_tensor(empty[:], empty[:], token[:], ALU.add))
                link(nc.vector.tensor_copy(self.target[:], empty[:]))
                if C == 2:
                    link(nc.vector.tensor_scalar(second[:], token[:], float(NTOK), None, ALU.is_ge))
                    link(nc.vector.scalar_tensor_tensor(out=token[:], in0=second[:], scalar=-float(NTOK),
                                                        in1=token[:], op0=ALU.mult, op1=ALU.add))
                link(nc.vector.tensor_scalar(token[:], token[:], 0.0, None, ALU.max))
                link(nc.vector.tensor_copy(self.source[:], token[:]))

    def experts(self, g, out=None):
        nc, a, sb, pb, sem, h, ident = (g[k] for k in ("nc", "a", "sb", "pb", "sem", "h", "ident"))
        n, NB, C = self.name + "_", self.blocks, self.choices
        W1, b1, W2, b2 = (a[k + self.suffix] for k in ("W1_", "b1_", "W2_", "b2_"))
        FB = 512 // BLOCK
        NU = KF // FB
        PART = 3
        whole = IMAGES * TOK // TT
        rest = IMAGES * TOK - whole * TT
        parts = [(i, min(i + PART, whole)) for i in range(0, whole, PART)]
        with ExitStack() as c:
            w1 = sb(n + "w1", [128, 2, KD, F], c=c)
            w2 = sb(n + "w2", [128, 2, KF, D], c=c)
            bias1 = sb(n + "bias1", [128, 2, KF], c=c)
            bias2 = sb(n + "bias2", [128, 2, D], c=c)
            xb = sb(n + "xb", [128, 2, SUB, D], c=c)
            xbT = sb(n + "xbT", [128, 2, KD, BLOCK], c=c)
            hid = sb(n + "hid", [128, KF, BLOCK], c=c)
            w2h, w2l = (sb(n + "w2_" + part, [128, 2, KF, D], F32R, c=c) for part in ("high", "low"))
            hidh, hidl = (sb(n + "hid_" + part, [128, 2, KF, BLOCK], F32R, c=c) for part in ("high", "low"))
            yb = sb(n + "yb", [128, 2, SUB, D], c=c)
            yg = sb(n + "yg", [128, C, NT, D], c=c)
            ps1 = pb(n + "ps1", [128, 4, 512], c=c)
            ps2 = pb(n + "ps2", [128, 2, 512], c=c)
            psX = pb(n + "psX", [128, 512], c=c)
            w1_in = [sem(f"{n}w1_in{j}", c) for j in range(2)]
            w2_in = [sem(f"{n}w2_in{j}", c) for j in range(2)]
            xb_in = [sem(f"{n}xb_in{j}", c) for j in range(2)]
            turned = sem(n + "x_turned", c)
            xT_kept = sem(n + "xT_kept", c)
            filled1 = sem(n + "filled1", c)
            kept1 = sem(n + "kept1", c)
            hid_high, hid_low, w2_high, w2_low = (sem(n + k, c) for k in ("hid_high", "hid_low", "w2_high", "w2_low"))
            bias2_in = [sem(f"{n}bias2_in{j}", c) for j in range(2)]
            filled2 = sem(n + "filled2", c)
            kept2 = sem(n + "kept2", c)
            stored = [sem(f"{n}stored{j}", c) for j in range(2)]
            fetched = [sem(f"{n}fetched{j}", c) for j in range(len(parts) + 1)]
            added = sem(n + "added", c)
            added_pool = sem(n + "added_pool", c)
            scored = sem(n + "scored", c)
            h_stored = sem(n + "h_stored", c)
            moments = Moments(g, c, n + "moments")
            block = c.enter_context(nc.Block())

            shares = [[i for i in range(NT) if i % 4 < 3], [i for i in range(NT) if i % 4 == 3]]

            def sum_tiles(eng, share, add):
                for n, (lo, hi) in enumerate(parts + [(whole, NT)]):
                    p = TT if hi <= whole else rest
                    eng.wait_ge(fetched[n], 16 * C * (2 if p == TT else 1))
                    for i in share:
                        if lo <= i < hi:
                            for j in range(C):
                                add(i, j, p, share.index(i) * C + j)
                            yield i

            def wait_summed(eng, tiles):
                for share, done in zip(shares, (added, added_pool)):
                    eng.wait_ge(done, C * sum(i < tiles for i in share))

            def since(b, k, one):
                return (b - k % 2) * (one // 2) + one

            @block.gpsimd
            def _(pool):
                for b in range(NB + 4):
                    if b < NB:
                        reused(pool, turned, b, 2)
                        for j in range(SUB):
                            at = b * SUB + j
                            pool.indirect_dma_start(
                                xb[:, b % 2, j, :], None, self.x_rows,
                                bass.IndirectOffsetOnAxis(ap=self.source[:, at:at + 1], axis=0))\
                                .then_inc(xb_in[b % 2], 16)
                    if b >= 4:
                        d = b - 4
                        pool.wait_ge(kept2, d * SUB + SUB)
                        for j in range(SUB):
                            at = d * SUB + j
                            pool.indirect_dma_start(
                                self.y_rows, bass.IndirectOffsetOnAxis(ap=self.target[:, at:at + 1], axis=0),
                                yb[:, d % 2, j, :], None).then_inc(stored[d % 2], 16)

                def add(i, j, p, count):
                    y = yg[0:p, j, i, :]
                    nc.gpsimd.tensor_tensor(y, y, self.scores[j][0:p, i:i + 1].broadcast_to([p, D]), ALU.mult)\
                        .then_inc(scored, 1)
                    pool.wait_ge(scored, count + 1)
                    if j:
                        pool.wait_ge(added_pool, count)
                    nc.gpsimd.tensor_tensor(h[0:p, i, :], h[0:p, i, :], y, ALU.add).then_inc(added_pool, 1)
                for _ in sum_tiles(pool, shares[1], add):
                    pass

            @block.sync
            def _(sp):
                def expert_of(b):
                    def load(b):
                        at = slice(b, b + 1) if isinstance(b, int) else bass.ds(b, 1)
                        return sp.value_load(self.expert[0:1, at], min_val=0, max_val=E - 1)
                    e = load(b)
                    return e, None if isinstance(b, int) and b < 2 else e != load(b - 2)

                def load1(b, k):
                    s = k % 2
                    e, lacking = expert_of(b)
                    reused(sp, kept1, b, 2, NU, 0)
                    through(sp, b, g["passed"])
                    sp.dma_start(w1[:, s, :, :], W1[e], cond=lacking).then_inc(w1_in[s], 16)
                    sp.dma_start(bias1[:, s, :], b1[e]).then_inc(w1_in[s], 16)

                def load2(b, k):
                    s = k % 2
                    e, lacking = expert_of(b)
                    reused(sp, w2_low, b, 2)
                    through(sp, b, g["passed"])
                    sp.dma_start(w2[:, s, :, :], W2[e], cond=lacking).then_inc(w2_in[s], 16)

                def load_bias2(b, k):
                    s = k % 2
                    e, _ = expert_of(b)
                    reused(sp, kept2, b, 2, SUB, 0)
                    through(sp, b, g["passed"])
                    sp.dma_start(bias2[:, s, :], b2[e].unsqueeze(0).broadcast_to([128, D])).then_inc(bias2_in[s], 16)
                run(sp, NB, 2, [(1, load2), (0, load1), (1, load_bias2)])
                sp.wait_ge(stored[0], 16 * SUB * (NB - NB // 2))
                sp.wait_ge(stored[1], 16 * SUB * (NB // 2))
                for n, (lo, hi) in enumerate(parts):
                    for j in range(C):
                        rows = self.y_rows[j * NTOK + lo * TT:j * NTOK + hi * TT, :].rearrange("(n p) d -> p n d", p=TT)
                        for p, q in CUTS:
                            sp.dma_start(yg[p:q, j, lo:hi, :], rows[p:q]).then_inc(fetched[n], 16)
                for j in range(C):
                    at = j * NTOK + whole * TT
                    sp.dma_start(yg[0:rest, j, whole, :], self.y_rows[at:at + rest, :]).then_inc(fetched[-1], 16)
                if out is not None:
                    flat = out.rearrange("b t d -> (b t) d")
                    for lo, hi in parts:
                        wait_summed(sp, hi)
                        rows = flat[lo * TT:hi * TT, :].rearrange("(n p) d -> p n d", p=TT)
                        for p, q in CUTS:
                            sp.dma_start(rows[p:q], h[p:q, lo:hi, :]).then_inc(h_stored, 16)
                    wait_summed(sp, NT)
                    sp.dma_start(flat[whole * TT:, :], h[0:rest, whole, :]).then_inc(h_stored, 16)
                    sp.wait_ge(h_stored, 16 * (2 * len(parts) + 1))

            @block.tensor
            def _(pe):
                def turn(b, k):
                    s = k % 2
                    pe.wait_ge(xb_in[s], since(b, k, 16 * SUB))
                    reused(pe, xT_kept, b, 1)
                    for j in range(SUB):
                        for kc in range(KD):
                            at = kc * BLOCK + j * 128
                            mm = nc.tensor.transpose(psX[:, at:at + 128], xb[:, s, j, kc * 128:(kc + 1) * 128],
                                                     ident[:, :])
                    mm.then_inc(turned, 1)

                def up(b, k):
                    s = k % 2
                    pe.wait_ge(xT_kept, b + 1)
                    pe.wait_ge(w1_in[s], since(b, k, 32))
                    for u in range(NU):
                        reused(pe, kept1, b, 4 // NU, NU, u - NU + 1)
                        for q in range(FB):
                            f = u * FB + q
                            for kc in range(KD):
                                mm = nc.tensor.matmul(ps1[:, (s * NU + u) % 4, q * BLOCK:(q + 1) * BLOCK],
                                                      w1[:, s, kc, f * 128:(f + 1) * 128], xbT[:, s, kc, :],
                                                      start=kc == 0, stop=kc == KD - 1)
                        mm.then_inc(filled1, 1)

                def down(b, k):
                    s = k % 2
                    pe.wait_ge(hid_low, b + 1)
                    pe.wait_ge(w2_low, b + 1)
                    for j in range(SUB):
                        reused(pe, kept2, b, 2 // SUB, SUB, j - SUB + 1)
                        for f in range(KF):
                            for m, (x, w) in enumerate(((hidh, w2h), (hidh, w2l), (hidl, w2h))):
                                mm = nc.tensor.matmul(ps2[:, (s * SUB + j) % 2, 0:D],
                                                      x[:, s, f, j * 128:(j + 1) * 128], w[:, s, f, :],
                                                      start=f + m == 0, stop=f == KF - 1 and m == 2)
                        mm.then_inc(filled2, 1)
                run(pe, NB, 2, [(0, turn), (1, up), (2, down)])

            @block.scalar
            def _(act):
                def keep_xT(b, k):
                    act.wait_ge(turned, b + 1)
                    reused(act, filled1, b, 2, NU, 0)
                    nc.scalar.activation(xbT[:, k % 2, :, :],
                                         psX[:, 0:KD * BLOCK].rearrange("p (c t) -> p c t", c=KD), ACT.Copy)\
                        .then_inc(xT_kept, 1)

                def activate(b, k):
                    s = k % 2
                    act.wait_ge(w1_in[s], since(b, k, 32))
                    reused(act, hid_low, b, 1)
                    for u in range(NU):
                        act.wait_ge(filled1, b * NU + u + 1)
                        for q in range(FB):
                            f = u * FB + q
                            ins = nc.scalar.activation(hid[:, f, :],
                                                       ps1[:, (s * NU + u) % 4, q * BLOCK:(q + 1) * BLOCK],
                                                       ACT.Silu, bias=bias1[:, s, f:f + 1])
                        ins.then_inc(kept1, 1)
                    act.wait_ge(kept1, b * NU + NU)
                    reused(act, filled2, b, 2, SUB, 0)
                    nc.scalar.activation(hidh[:, s, :, :], hid[:, :, :], ACT.Copy).then_inc(hid_high, 1)

                def split_w2(b, k):
                    s = k % 2
                    act.wait_ge(w2_in[s], since(b, k, 16))
                    reused(act, filled2, b, 2, SUB, 0)
                    nc.scalar.activation(w2h[:, s, :, :], w2[:, s, :, :], ACT.Copy).then_inc(w2_high, 1)
                run(act, NB, 2, [(0, keep_xT), (1, activate), (1, split_w2)])

            @block.vector
            def _(dve):
                def keep_y(b, k):
                    s = k % 2
                    dve.wait_ge(bias2_in[s], since(b, k, 16))
                    if not (isinstance(b, int) and b < 2):
                        dve.wait_ge(stored[s], since(b, k, 16 * SUB) - 16 * SUB)
                    for j in range(SUB):
                        dve.wait_ge(filled2, b * SUB + j + 1)
                        nc.vector.tensor_tensor(yb[:, s, j, :], ps2[:, (s * SUB + j) % 2, 0:D], bias2[:, s, :], ALU.add)\
                            .then_inc(kept2, 1)

                def rest_of_hid(b, k):
                    dve.wait_ge(hid_high, b + 1)
                    reused(dve, filled2, b, 2, SUB, 0)
                    nc.vector.tensor_tensor(hidl[:, k % 2, :, :], hid[:, :, :], hidh[:, k % 2, :, :].bitcast(F32),
                                            ALU.subtract).then_inc(hid_low, 1)

                def rest_of_w2(b, k):
                    dve.wait_ge(w2_high, b + 1)
                    nc.vector.tensor_tensor(w2l[:, k % 2, :, :], w2[:, k % 2, :, :],
                                            w2h[:, k % 2, :, :].bitcast(F32), ALU.subtract).then_inc(w2_low, 1)
                run(dve, NB, 2, [(1, rest_of_hid), (1, rest_of_w2), (2, keep_y)])
                taken = 0

                def statistics(upto):
                    for t in range(taken, upto):
                        wait_summed(dve, t + 1)
                        moments.take(dve, t)

                def add(i, j, p, count):
                    if j:
                        dve.wait_ge(added, count)
                    nc.vector.scalar_tensor_tensor(out=h[0:p, i, :], in0=yg[0:p, j, i, :],
                                                   scalar=self.scores[j][0:p, i:i + 1], in1=h[0:p, i, :],
                                                   op0=ALU.mult, op1=ALU.add).then_inc(added, 1)
                for i in sum_tiles(dve, shares[0], add):
                    if out is None:
                        statistics(i)
                        taken = i
                if out is None:
                    statistics(NT)


def host_arrays(v):
    x = np.asarray(v["x"])
    side = 6
    p = x.reshape(IMAGES, 3, side, 16, side, 16).transpose(1, 3, 5, 0, 2, 4).reshape(PATCH, IMAGES, side * side)
    pt = np.zeros((PATCH, NT * PER, TOK), x.dtype)
    pt[:, :IMAGES, 1:] = p
    pt = pt.reshape(KP, 128, NT, TT).transpose(1, 2, 0, 3)
    rows = np.asarray(v["L0_tok_b"])[None].repeat(TOK, 0)
    rows[0] = np.asarray(v["L0_tok_cls_token"])[0, 0]

    def bc(name):
        return np.asarray(v[name]).reshape(1, -1).repeat(TT, 0)

    tok = np.arange(TT)
    same = tok[:, None] // TOK == tok[None] // TOK
    mask = np.where(same & (tok[None] <= tok[:, None]), 0.0, MASKED).astype(np.float32)
    valid = ((np.arange(NT)[None] * TT + tok[:, None]) < IMAGES * TOK).astype(np.float32)

    def chunked(w):
        w = np.asarray(w)
        return w.reshape(E, w.shape[1] // 128, 128, w.shape[2]).transpose(0, 2, 1, 3)

    numbered = (np.arange(NT)[None, None] * TT + tok[:, None, None] + np.arange(2)[None, :, None] * NTOK + 1)

    def spare(choices):
        groups = ((choices * IMAGES * TOK - E) // BLOCK + E) * SUB
        return (np.arange(groups)[None] * 128 + np.arange(128)[:, None] + choices * NTOK + 1).astype(np.float32)

    a = {
        "patchesT": pt,
        "tok_WT": np.asarray(v["L0_tok_W"]).T,
        "cls_or_b": np.tile(rows, (PER, 1)),
        "pos": np.tile(np.asarray(v["L0_tok_pos_embedding"])[0], (PER, 1)),
        "ident": np.eye(128, dtype=np.float32),
        "mask4": np.tile(mask, (1, 4)),
        "bo": bc("L0_attn_bo"),
        "ffn_rms_w": bc("L0_ffn_rms_w"),
        "gate_wT": np.asarray(v["L0_ffn_gate_w"]).T,
        "number_less_e": np.tile(np.arange(E, dtype=np.float32) - E, (TT, 1)),
        "W1_0": chunked(v["L0_ffn_W1"]), "W2_0": chunked(v["L0_ffn_W2"]), "b2_0": np.asarray(v["L0_ffn_b2"]),
        "b1_0": np.asarray(v["L0_ffn_b1"]).reshape(E, KF, 128).transpose(0, 2, 1),
        "W1_1": chunked(v["L1_ffn_we1"]), "W2_1": chunked(v["L1_ffn_we2"]), "b2_1": np.asarray(v["L1_ffn_be2"]),
        "b1_1": np.asarray(v["L1_ffn_be1"]).reshape(E, KF, 128).transpose(0, 2, 1),
        "W_in": np.asarray(v["L1_attn_W_in"]), "W_out": np.asarray(v["L1_attn_W_out"]),
        "glu_w": np.asarray(v["L1_attn_glu_w"]), "glu_b": bc("L1_attn_glu_b"),
        "conv_w": np.asarray(v["L1_attn_conv_w"]).reshape(KC, 128, 4).transpose(1, 0, 2),
        "conv_b": np.asarray(v["L1_attn_conv_b"]).reshape(KC, 128).T,
        "m_rms_w": np.asarray(v["L1_attn_rms_w"]).reshape(DI // 128, 128).T,
        "D_skip": np.asarray(v["L1_attn_D_skip"]).repeat(DI // MH).reshape(DI // 128, 128).T, "dt_bias": bc("L1_attn_dt_bias"), "A_log": bc("L1_attn_A_log"),
        "ln_w": bc("L1_attn_ln_w"), "ln_b": bc("L1_attn_ln_b"),
        "after": (tok[:, None] > tok[None]).astype(np.float32),
        "upto": (tok[:, None] <= tok[None]).astype(np.float32),
        "causal": (same & (tok[:, None] <= tok[None])).astype(np.float32),
        "valid": valid,
        "token_numbers": np.stack([numbered // 64 * valid[:, None, :], numbered % 64 * valid[:, None, :]], 2)
        .astype(np.float32),
        "spare0": spare(1), "spare1": spare(2),
        "numbers": np.tile(np.arange(129, dtype=np.float32), (128, 1)),
        "before": (tok[:, None] < tok[None]).astype(np.float32),
        "ones": np.ones((TT, TT), np.float32),
        "earlier": np.tile(np.tri(E, k=-1, dtype=np.float32), (TT, 1, 1)),
        "rw1": np.asarray(v["L1_ffn_rw1"]), "rw2": np.asarray(v["L1_ffn_rw2"]), "rb2": bc("L1_ffn_rb2"),
        "rb1": np.asarray(v["L1_ffn_rb1"]).reshape(KD, 128).T,
    }
    for w in ("Wq", "Wk", "Wv", "Wo"):
        a[w] = np.asarray(v["L0_attn_" + w])
    return a



def kernel(**inputs):
    import concourse.bacc as _bacc
    from concourse.bass_utils import run_bass_kernel_spmd as _run

    nc = _bacc.Bacc("TRN2", target_bir_lowering=False, num_devices=1)
    arrays, args = {}, {}
    for name, arr in host_arrays(inputs).items():
        arr = np.ascontiguousarray(arr)
        arrays[f"in_{name}"] = arr
        args[name] = nc.dram_tensor(f"in_{name}", arr.shape, mybir.dt.from_np(arr.dtype), kind="ExternalInput").ap()
    out = nc.dram_tensor("out_0", (IMAGES, TOK, D), F32, kind="ExternalOutput").ap()
    build(nc, args, out)
    r = _run(nc, [arrays], core_ids=[0])
    return r.results[0]["out_0"]
```
